# Optimizing a Trainium2 kernel written in Bass

```python
import numpy as np
import jax
import jax.numpy as jnp

def _softmax(x, axis=-1):
    return jax.nn.softmax(x, axis=axis)

def _gelu(x):
    return jax.nn.gelu(x, approximate=True)

def _silu(x):
    return jax.nn.silu(x)

def _sigmoid(x):
    return jax.nn.sigmoid(x)

def _layernorm(x, axis=-1, eps=1e-05):
    m = jnp.mean(x, axis=axis, keepdims=True)
    v = jnp.var(x, axis=axis, keepdims=True)
    return (x - m) / jnp.sqrt(v + eps)

def _scatter_add(tgt, idx, src, axis=0):
    return tgt.at[idx].add(src)

def _segment_sum(src, seg, n):
    return jax.ops.segment_sum(src, seg, n)
kernel_name = 'mk_cond_seq_d4_seqx_r4_1508e6'

def setup_inputs(seed: int=0):
    np.random.seed(seed)
    _w = jnp.asarray

    def _rec_inputs():
        import jax
        import jax.numpy as jnp
        _rk = jax.random.key(seed)
        x = -0.0003929 + 0.9999 * jax.random.normal(jax.random.fold_in(_rk, 1), (32, 256, 256), jnp.float32)
        _lenS = 256 - jax.random.randint(jax.random.fold_in(_rk, 7), (32,), 0, max(1, 256 // 4) + 1, jnp.int32)
        _lenS2 = 256 - jax.random.randint(jax.random.fold_in(_rk, 8), (32,), 0, max(1, 256 // 4) + 1, jnp.int32)
        cond_2048 = 0.00782532 + 1.00527 * jax.random.normal(jax.random.fold_in(_rk, 11), (32, 512), jnp.float32)
        cond_1024 = 0.00786388 + 1.0143 * jax.random.normal(jax.random.fold_in(_rk, 14), (32, 256), jnp.float32)
        _validS = jnp.arange(256)[None, :] < _lenS[:, None]
        _validS2 = jnp.arange(256)[None, :] < _lenS2[:, None]
        _causal = jnp.tril(jnp.ones((256, 256), dtype=bool))
        mask_BxS_ik0 = jnp.where(jnp.broadcast_to(_validS[:, :], (32, 256)), 0, 1).astype(jnp.int32)
        mask_BxS_ff1 = jnp.where(jnp.ones((32, 256), dtype=bool), 1.0, 0.0).astype(jnp.float32)
        mask_BxSx1_fk1 = jnp.where(jnp.ones((32, 256, 1), dtype=bool), 1.0, 0.0).astype(jnp.float32)
        return (x, cond_2048, cond_1024, mask_BxS_ik0, mask_BxS_ff1, mask_BxSx1_fk1)
    x, cond_2048, cond_1024, mask_BxS_ik0, mask_BxS_ff1, mask_BxSx1_fk1 = _rec_inputs()

    def _L0_cond_setup():
        import jax, jax.numpy as jnp
        import numpy as np
        H = 16
        LN_EPS = 1e-05

        def _layernorm(x, scale, bias):
            mu = jnp.mean(x, axis=-1, keepdims=True)
            var = jnp.var(x, axis=-1, keepdims=True)
            return (x - mu) * jax.lax.rsqrt(var + LN_EPS) * scale + bias
        key = jax.random.key(seed)
        ks = jax.random.split(key, 8)
        B, T, D, E = (4, 1024, 256, 512)
        s = 0.02
        return {'x': jax.random.normal(ks[0], (B, T, D), jnp.float32), 'emb': jax.random.normal(ks[1], (B, E), jnp.float32), 'src_mask': jax.random.randint(ks[2], (B, T), 0, 2).astype(jnp.int32), 'norm_scale': jnp.ones((D,), jnp.float32), 'norm_bias': jnp.zeros((D,), jnp.float32), 'Wq': jax.random.normal(ks[3], (D, D), jnp.float32) * s, 'bq': jnp.zeros((D,), jnp.float32), 'Wk': jax.random.normal(ks[4], (D, D), jnp.float32) * s, 'bk': jnp.zeros((D,), jnp.float32), 'Wv': jax.random.normal(ks[5], (D, D), jnp.float32) * s, 'bv': jnp.zeros((D,), jnp.float32), 'film_emb_W': jax.random.normal(ks[6], (E, 2 * D), jnp.float32) * s, 'film_emb_b': jnp.zeros((2 * D,), jnp.float32), 'film_norm_scale': jnp.ones((D,), jnp.float32), 'film_norm_bias': jnp.zeros((D,), jnp.float32), 'film_out_W': jax.random.normal(ks[7], (D, D), jnp.float32) * s, 'film_out_b': jnp.zeros((D,), jnp.float32)}
    _L0_cond_all = _L0_cond_setup()
    _L0_cond_in = {k: v for k, v in _L0_cond_all.items() if k in ('norm_scale', 'norm_bias', 'Wq', 'bq', 'Wk', 'bk', 'Wv', 'bv', 'film_emb_W', 'film_emb_b', 'film_norm_scale', 'film_norm_bias', 'film_out_W', 'film_out_b')}
    del _L0_cond_all

    def _L1_cond_setup():
        import jax, jax.numpy as jnp
        import numpy as np
        B, T, D, H, TE = (8, 256, 256, 16, 512)
        LN_EPS = 1e-05

        def layer_norm(x, w, b):
            m = jnp.mean(x, axis=-1, keepdims=True)
            v = jnp.var(x, axis=-1, keepdims=True)
            return (x - m) / jnp.sqrt(v + LN_EPS) * w + b
        key = jax.random.key(seed)
        ks = jax.random.split(key, 8)
        s = lambda k, sh: jax.random.normal(k, sh, jnp.float32) * 0.02
        return dict(x=jax.random.normal(ks[0], (B, T, D), jnp.float32), emb=jax.random.normal(ks[1], (B, TE), jnp.float32), src_mask=jnp.ones((B, T), jnp.float32), norm_w=jnp.ones((D,), jnp.float32), norm_b=jnp.zeros((D,), jnp.float32), q_w=s(ks[2], (D, D)), q_b=jnp.zeros((D,), jnp.float32), k_w=s(ks[3], (D, D)), k_b=jnp.zeros((D,), jnp.float32), v_w=s(ks[4], (D, D)), v_b=jnp.zeros((D,), jnp.float32), emb_w=s(ks[5], (TE, 2 * D)), emb_b=jnp.zeros((2 * D,), jnp.float32), sb_norm_w=jnp.ones((D,), jnp.float32), sb_norm_b=jnp.zeros((D,), jnp.float32), out_w=s(ks[6], (D, D)), out_b=jnp.zeros((D,), jnp.float32))
    _L1_cond_all = _L1_cond_setup()
    _L1_cond_in = {k: v for k, v in _L1_cond_all.items() if k in ('norm_w', 'norm_b', 'q_w', 'q_b', 'k_w', 'k_b', 'v_w', 'v_b', 'emb_w', 'emb_b', 'sb_norm_w', 'sb_norm_b', 'out_w', 'out_b')}
    del _L1_cond_all

    def _L2_cond_setup():
        import jax, jax.numpy as jnp
        import numpy as np
        B, S, D, E, N, R = (2, 256, 256, 512, 16, 64)
        EPS = 1e-05

        def _ln(x, g, b):
            m = jnp.mean(x, -1, keepdims=True)
            v = jnp.mean((x - m) ** 2, -1, keepdims=True)
            return (x - m) * jax.lax.rsqrt(v + EPS) * g + b

        def _ssm(u, Wdbc, Wdt, bdt, Alog, Dp):
            dbc = jnp.einsum('bse,re->bsr', u, Wdbc)
            dlt, Bm, Cm = jnp.split(dbc, [R, R + N], axis=-1)
            delta = jax.nn.softplus(jnp.einsum('bsr,er->bse', dlt, Wdt) + bdt)
            A = -jnp.exp(Alog)
            dA = jnp.exp(delta[..., None] * A)
            dBu = delta[..., None] * Bm[:, :, None, :] * u[..., None]

            def step(h, xs):
                dA_t, dBu_t, C_t = xs
                h = dA_t * h + dBu_t
                y = jnp.einsum('ben,bn->be', h, C_t)
                return (h, y)
            h0 = jnp.zeros((u.shape[0], u.shape[2], N), u.dtype)
            _, ys = jax.lax.scan(step, h0, (dA.swapaxes(0, 1), dBu.swapaxes(0, 1), Cm.swapaxes(0, 1)))
            return ys.swapaxes(0, 1) + u * Dp
        key = jax.random.key(seed)
        ks = jax.random.split(key, 16)
        f = lambda k, sh, s=0.02: jax.random.normal(k, sh, jnp.float32) * s
        Alog = jnp.log(jnp.tile(jnp.arange(1, N + 1, dtype=jnp.float32), (E, 1)))
        return dict(x=f(ks[0], (B, S, D), 1.0), c=f(ks[1], (B, 2 * D), 1.0), w=f(ks[2], (B, D), 1.0), norm1_g=jnp.ones((D,)), norm1_b=jnp.zeros((D,)), norm2_g=jnp.ones((D,)), norm2_b=jnp.zeros((D,)), Wx=f(ks[3], (E, D)), bx=jnp.zeros((E,)), Wz=f(ks[4], (E, D)), bz=jnp.zeros((E,)), Wf=f(ks[5], (D, E)), bf=jnp.zeros((D,)), Wada=f(ks[6], (3 * D, 2 * D)), bada=jnp.zeros((3 * D,)), Wc1=f(ks[7], (E, E)), bc1=jnp.zeros((E,)), Wc2=f(ks[8], (E, E)), bc2=jnp.zeros((E,)), Wdbc1=f(ks[9], (R + 2 * N, E)), Wdt1=f(ks[10], (E, R)), bdt1=jnp.zeros((E,)), Alog1=Alog, Dp1=jnp.ones((E,)), Wdbc2=f(ks[11], (R + 2 * N, E)), Wdt2=f(ks[12], (E, R)), bdt2=jnp.zeros((E,)), Alog2=Alog, Dp2=jnp.ones((E,)))
    _L2_cond_all = _L2_cond_setup()
    _L2_cond_in = {k: v for k, v in _L2_cond_all.items() if k in ('norm1_g', 'norm1_b', 'norm2_g', 'norm2_b', 'Wx', 'bx', 'Wz', 'bz', 'Wf', 'bf', 'Wada', 'bada', 'Wc1', 'bc1', 'Wc2', 'bc2', 'Wdbc1', 'Wdt1', 'bdt1', 'Alog1', 'Dp1', 'Wdbc2', 'Wdt2', 'bdt2', 'Alog2', 'Dp2')}
    del _L2_cond_all

    def _L3_cond_setup():
        import jax, jax.numpy as jnp
        import numpy as np
        B, T, D, H, TE = (4, 512, 256, 8, 512)
        EPS = 1e-05

        def _ln(x, w, b):
            m = jnp.mean(x, axis=-1, keepdims=True)
            v = jnp.mean((x - m) ** 2, axis=-1, keepdims=True)
            return (x - m) * jax.lax.rsqrt(v + EPS) * w + b
        key = jax.random.key(seed)
        ks = jax.random.split(key, 16)
        s = 0.02
        inp = {'x': jax.random.normal(ks[0], (B, T, D), jnp.float32), 'emb': jax.random.normal(ks[1], (B, TE), jnp.float32), 'src_mask': (jax.random.uniform(ks[2], (B, T, 1)) > 0.2).astype(jnp.float32), 'num_head': H, 'ln_w': jnp.ones((D,), jnp.float32), 'ln_b': jnp.zeros((D,), jnp.float32), 'Wq': jax.random.normal(ks[3], (D, D), jnp.float32) * s, 'bq': jnp.zeros((D,), jnp.float32), 'Wk': jax.random.normal(ks[4], (D, D), jnp.float32) * s, 'bk': jnp.zeros((D,), jnp.float32), 'Wv': jax.random.normal(ks[5], (D, D), jnp.float32) * s, 'bv': jnp.zeros((D,), jnp.float32), 'W_emb': jax.random.normal(ks[6], (TE, 2 * D), jnp.float32) * s, 'b_emb': jnp.zeros((2 * D,), jnp.float32), 'ln2_w': jnp.ones((D,), jnp.float32), 'ln2_b': jnp.zeros((D,), jnp.float32), 'W_out': jax.random.normal(ks[7], (D, D), jnp.float32) * s, 'b_out': jnp.zeros((D,), jnp.float32)}
        return inp
    _L3_cond_all = _L3_cond_setup()
    _L3_cond_in = {k: v for k, v in _L3_cond_all.items() if k in ('ln_w', 'ln_b', 'Wq', 'bq', 'Wk', 'bk', 'Wv', 'bv', 'W_emb', 'b_emb', 'ln2_w', 'ln2_b', 'W_out', 'b_out')}
    del _L3_cond_all
    return {'x': x, 'cond_2048': cond_2048, 'cond_1024': cond_1024, 'mask_BxS_ik0': mask_BxS_ik0, 'mask_BxS_ff1': mask_BxS_ff1, 'mask_BxSx1_fk1': mask_BxSx1_fk1, 'L0_cond_norm_scale': _L0_cond_in['norm_scale'], 'L0_cond_norm_bias': _L0_cond_in['norm_bias'], 'L0_cond_Wq': _L0_cond_in['Wq'], 'L0_cond_bq': _L0_cond_in['bq'], 'L0_cond_Wk': _L0_cond_in['Wk'], 'L0_cond_bk': _L0_cond_in['bk'], 'L0_cond_Wv': _L0_cond_in['Wv'], 'L0_cond_bv': _L0_cond_in['bv'], 'L0_cond_film_emb_W': _L0_cond_in['film_emb_W'], 'L0_cond_film_emb_b': _L0_cond_in['film_emb_b'], 'L0_cond_film_norm_scale': _L0_cond_in['film_norm_scale'], 'L0_cond_film_norm_bias': _L0_cond_in['film_norm_bias'], 'L0_cond_film_out_W': _L0_cond_in['film_out_W'], 'L0_cond_film_out_b': _L0_cond_in['film_out_b'], 'L1_cond_norm_w': _L1_cond_in['norm_w'], 'L1_cond_norm_b': _L1_cond_in['norm_b'], 'L1_cond_q_w': _L1_cond_in['q_w'], 'L1_cond_q_b': _L1_cond_in['q_b'], 'L1_cond_k_w': _L1_cond_in['k_w'], 'L1_cond_k_b': _L1_cond_in['k_b'], 'L1_cond_v_w': _L1_cond_in['v_w'], 'L1_cond_v_b': _L1_cond_in['v_b'], 'L1_cond_emb_w': _L1_cond_in['emb_w'], 'L1_cond_emb_b': _L1_cond_in['emb_b'], 'L1_cond_sb_norm_w': _L1_cond_in['sb_norm_w'], 'L1_cond_sb_norm_b': _L1_cond_in['sb_norm_b'], 'L1_cond_out_w': _L1_cond_in['out_w'], 'L1_cond_out_b': _L1_cond_in['out_b'], 'L2_cond_norm1_g': _L2_cond_in['norm1_g'], 'L2_cond_norm1_b': _L2_cond_in['norm1_b'], 'L2_cond_norm2_g': _L2_cond_in['norm2_g'], 'L2_cond_norm2_b': _L2_cond_in['norm2_b'], 'L2_cond_Wx': _L2_cond_in['Wx'], 'L2_cond_bx': _L2_cond_in['bx'], 'L2_cond_Wz': _L2_cond_in['Wz'], 'L2_cond_bz': _L2_cond_in['bz'], 'L2_cond_Wf': _L2_cond_in['Wf'], 'L2_cond_bf': _L2_cond_in['bf'], 'L2_cond_Wada': _L2_cond_in['Wada'], 'L2_cond_bada': _L2_cond_in['bada'], 'L2_cond_Wc1': _L2_cond_in['Wc1'], 'L2_cond_bc1': _L2_cond_in['bc1'], 'L2_cond_Wc2': _L2_cond_in['Wc2'], 'L2_cond_bc2': _L2_cond_in['bc2'], 'L2_cond_Wdbc1': _L2_cond_in['Wdbc1'], 'L2_cond_Wdt1': _L2_cond_in['Wdt1'], 'L2_cond_bdt1': _L2_cond_in['bdt1'], 'L2_cond_Alog1': _L2_cond_in['Alog1'], 'L2_cond_Dp1': _L2_cond_in['Dp1'], 'L2_cond_Wdbc2': _L2_cond_in['Wdbc2'], 'L2_cond_Wdt2': _L2_cond_in['Wdt2'], 'L2_cond_bdt2': _L2_cond_in['bdt2'], 'L2_cond_Alog2': _L2_cond_in['Alog2'], 'L2_cond_Dp2': _L2_cond_in['Dp2'], 'L3_cond_ln_w': _L3_cond_in['ln_w'], 'L3_cond_ln_b': _L3_cond_in['ln_b'], 'L3_cond_Wq': _L3_cond_in['Wq'], 'L3_cond_bq': _L3_cond_in['bq'], 'L3_cond_Wk': _L3_cond_in['Wk'], 'L3_cond_bk': _L3_cond_in['bk'], 'L3_cond_Wv': _L3_cond_in['Wv'], 'L3_cond_bv': _L3_cond_in['bv'], 'L3_cond_W_emb': _L3_cond_in['W_emb'], 'L3_cond_b_emb': _L3_cond_in['b_emb'], 'L3_cond_ln2_w': _L3_cond_in['ln2_w'], 'L3_cond_ln2_b': _L3_cond_in['ln2_b'], 'L3_cond_W_out': _L3_cond_in['W_out'], 'L3_cond_b_out': _L3_cond_in['b_out']}

def reference(x, cond_2048, cond_1024, mask_BxS_ik0, mask_BxS_ff1, mask_BxSx1_fk1, L0_cond_norm_scale, L0_cond_norm_bias, L0_cond_Wq, L0_cond_bq, L0_cond_Wk, L0_cond_bk, L0_cond_Wv, L0_cond_bv, L0_cond_film_emb_W, L0_cond_film_emb_b, L0_cond_film_norm_scale, L0_cond_film_norm_bias, L0_cond_film_out_W, L0_cond_film_out_b, L1_cond_norm_w, L1_cond_norm_b, L1_cond_q_w, L1_cond_q_b, L1_cond_k_w, L1_cond_k_b, L1_cond_v_w, L1_cond_v_b, L1_cond_emb_w, L1_cond_emb_b, L1_cond_sb_norm_w, L1_cond_sb_norm_b, L1_cond_out_w, L1_cond_out_b, L2_cond_norm1_g, L2_cond_norm1_b, L2_cond_norm2_g, L2_cond_norm2_b, L2_cond_Wx, L2_cond_bx, L2_cond_Wz, L2_cond_bz, L2_cond_Wf, L2_cond_bf, L2_cond_Wada, L2_cond_bada, L2_cond_Wc1, L2_cond_bc1, L2_cond_Wc2, L2_cond_bc2, L2_cond_Wdbc1, L2_cond_Wdt1, L2_cond_bdt1, L2_cond_Alog1, L2_cond_Dp1, L2_cond_Wdbc2, L2_cond_Wdt2, L2_cond_bdt2, L2_cond_Alog2, L2_cond_Dp2, L3_cond_ln_w, L3_cond_ln_b, L3_cond_Wq, L3_cond_bq, L3_cond_Wk, L3_cond_bk, L3_cond_Wv, L3_cond_bv, L3_cond_W_emb, L3_cond_b_emb, L3_cond_ln2_w, L3_cond_ln2_b, L3_cond_W_out, L3_cond_b_out):
    import jax
    import jax.numpy as jnp

    def _L0_cond_ref(x, emb, src_mask, norm_scale, norm_bias, Wq, bq, Wk, bk, Wv, bv, film_emb_W, film_emb_b, film_norm_scale, film_norm_bias, film_out_W, film_out_b):
        import jax, jax.numpy as jnp
        import numpy as np
        H = 16
        LN_EPS = 1e-05

        def _layernorm(x, scale, bias):
            mu = jnp.mean(x, axis=-1, keepdims=True)
            var = jnp.var(x, axis=-1, keepdims=True)
            return (x - mu) * jax.lax.rsqrt(var + LN_EPS) * scale + bias
        B, T, D = x.shape
        dh = D // H
        xn = _layernorm(x, norm_scale, norm_bias)
        q = xn @ Wq + bq
        k = xn @ Wk + bk
        v = xn @ Wv + bv
        mask = (src_mask == 1)[:, :, None]
        k = jnp.where(mask, -jnp.inf, k)
        v = jnp.where(mask, 0.0, v)
        q = q.reshape(B, T, H, dh).transpose(0, 2, 1, 3)
        k = k.reshape(B, T, H, dh).transpose(0, 2, 1, 3)
        v = v.reshape(B, T, H, dh).transpose(0, 2, 1, 3)
        q = jax.nn.softmax(q, axis=-1)
        k = jax.nn.softmax(k, axis=2)
        attn = jnp.einsum('bhse,bhsd->bhed', k, v)
        y = jnp.einsum('bhtd,bhed->bhte', q, attn)
        y = y.transpose(0, 2, 1, 3).reshape(B, T, D)
        emb_out = jax.nn.silu(emb) @ film_emb_W + film_emb_b
        scale, shift = jnp.split(emb_out, 2, axis=-1)
        h = _layernorm(y, film_norm_scale, film_norm_bias) * (1.0 + scale[:, None, :]) + shift[:, None, :]
        h = jax.nn.silu(h) @ film_out_W + film_out_b
        return x + h

    def _L1_cond_ref(x, emb, src_mask, norm_w, norm_b, q_w, q_b, k_w, k_b, v_w, v_b, emb_w, emb_b, sb_norm_w, sb_norm_b, out_w, out_b):
        import jax, jax.numpy as jnp
        import numpy as np
        B, T, D, H, TE = (8, 256, 256, 16, 512)
        LN_EPS = 1e-05

        def layer_norm(x, w, b):
            m = jnp.mean(x, axis=-1, keepdims=True)
            v = jnp.var(x, axis=-1, keepdims=True)
            return (x - m) / jnp.sqrt(v + LN_EPS) * w + b
        Bx, Tx, Dx = x.shape
        xn = layer_norm(x, norm_w, norm_b)
        q = (xn @ q_w + q_b).reshape(Bx, Tx, H, -1)
        k = (xn @ k_w + k_b).reshape(Bx, Tx, H, -1)
        att = jnp.einsum('bnhl,bmhl->bnmh', q, k)
        mask = src_mask.reshape(Bx, 1, Tx, 1)
        att = att + (1.0 - mask) * -1000000.0
        att = jax.nn.softmax(att, axis=2)
        v = ((xn @ v_w + v_b) * src_mask[:, :, None]).reshape(Bx, Tx, H, -1)
        y = jnp.einsum('bnmh,bmhl->bnhl', att, v).reshape(Bx, Tx, Dx)
        e = jax.nn.silu(emb) @ emb_w + emb_b
        scale, shift = jnp.split(e[:, None, :], 2, axis=2)
        h = layer_norm(y, sb_norm_w, sb_norm_b) * (1.0 + scale) + shift
        h = jax.nn.silu(h) @ out_w + out_b
        return x + h

    def _L2_cond_ref(x, c, w, norm1_g, norm1_b, norm2_g, norm2_b, Wx, bx, Wz, bz, Wf, bf, Wada, bada, Wc1, bc1, Wc2, bc2, Wdbc1, Wdt1, bdt1, Alog1, Dp1, Wdbc2, Wdt2, bdt2, Alog2, Dp2):
        import jax, jax.numpy as jnp
        import numpy as np
        B, S, D, E, N, R = (2, 256, 256, 512, 16, 64)
        EPS = 1e-05

        def _ln(x, g, b):
            m = jnp.mean(x, -1, keepdims=True)
            v = jnp.mean((x - m) ** 2, -1, keepdims=True)
            return (x - m) * jax.lax.rsqrt(v + EPS) * g + b

        def _ssm(u, Wdbc, Wdt, bdt, Alog, Dp):
            dbc = jnp.einsum('bse,re->bsr', u, Wdbc)
            dlt, Bm, Cm = jnp.split(dbc, [R, R + N], axis=-1)
            delta = jax.nn.softplus(jnp.einsum('bsr,er->bse', dlt, Wdt) + bdt)
            A = -jnp.exp(Alog)
            dA = jnp.exp(delta[..., None] * A)
            dBu = delta[..., None] * Bm[:, :, None, :] * u[..., None]

            def step(h, xs):
                dA_t, dBu_t, C_t = xs
                h = dA_t * h + dBu_t
                y = jnp.einsum('ben,bn->be', h, C_t)
                return (h, y)
            h0 = jnp.zeros((u.shape[0], u.shape[2], N), u.dtype)
            _, ys = jax.lax.scan(step, h0, (dA.swapaxes(0, 1), dBu.swapaxes(0, 1), Cm.swapaxes(0, 1)))
            return ys.swapaxes(0, 1) + u * Dp
        ada = jax.nn.silu(c) @ Wada.T + bada
        shift, scale, gate = jnp.split(ada, 3, axis=1)
        x_ssm = _ln(x, norm1_g, norm1_b)
        x_ssm = x_ssm * (1.0 + scale[:, None, :]) + shift[:, None, :]
        skip = x_ssm
        x_ssm = _ln(x_ssm, norm2_g, norm2_b)
        mz = jnp.einsum('bsd,ed->bse', x_ssm, Wz) + bz
        mx = jnp.einsum('bsd,ed->bse', x_ssm, Wx) + bx
        act_mx = jax.nn.silu(mx)
        z1 = jnp.einsum('bse,fe->bsf', mz, Wc1) + bc1
        z1 = _ssm(z1, Wdbc1, Wdt1, bdt1, Alog1, Dp1)
        y1 = act_mx * z1
        z2 = jnp.einsum('bse,fe->bsf', mz, Wc2) + bc2
        z2 = jnp.flip(z2, axis=1)
        z2 = _ssm(z2, Wdbc2, Wdt2, bdt2, Alog2, Dp2)
        z2 = jnp.flip(z2, axis=1)
        y2 = act_mx * z2
        out = jnp.einsum('bse,de->bsd', y1 + y2, Wf) + bf + skip
        return x + gate[:, None, :] * out

    def _L3_cond_ref(x, emb, src_mask, num_head, ln_w, ln_b, Wq, bq, Wk, bk, Wv, bv, W_emb, b_emb, ln2_w, ln2_b, W_out, b_out):
        import jax, jax.numpy as jnp
        import numpy as np
        B, T, D, H, TE = (4, 512, 256, 8, 512)
        EPS = 1e-05

        def _ln(x, w, b):
            m = jnp.mean(x, axis=-1, keepdims=True)
            v = jnp.mean((x - m) ** 2, axis=-1, keepdims=True)
            return (x - m) * jax.lax.rsqrt(v + EPS) * w + b
        b, t, d = x.shape
        h = num_head
        dh = d // h
        xn = _ln(x, ln_w, ln_b)
        q = xn @ Wq + bq
        k = xn @ Wk + bk + (1.0 - src_mask) * -1000000.0
        q = jax.nn.softmax(q.reshape(b, t, h, dh), axis=-1)
        k = jax.nn.softmax(k.reshape(b, t, h, dh), axis=1)
        v = ((xn @ Wv + bv) * src_mask).reshape(b, t, h, dh)
        att = jnp.einsum('bnhd,bnhl->bhdl', k, v)
        y = jnp.einsum('bnhd,bhdl->bnhl', q, att).reshape(b, t, d)
        emb_out = (jax.nn.silu(emb) @ W_emb + b_emb)[:, None, :]
        scale, shift = jnp.split(emb_out, 2, axis=2)
        hh = _ln(y, ln2_w, ln2_b) * (1.0 + scale) + shift
        hh = jax.nn.silu(hh) @ W_out + b_out
        return x + hh
    x = _L0_cond_ref(x, cond_2048, mask_BxS_ik0, L0_cond_norm_scale, L0_cond_norm_bias, L0_cond_Wq, L0_cond_bq, L0_cond_Wk, L0_cond_bk, L0_cond_Wv, L0_cond_bv, L0_cond_film_emb_W, L0_cond_film_emb_b, L0_cond_film_norm_scale, L0_cond_film_norm_bias, L0_cond_film_out_W, L0_cond_film_out_b)
    x = _L1_cond_ref(x, cond_2048, mask_BxS_ff1, L1_cond_norm_w, L1_cond_norm_b, L1_cond_q_w, L1_cond_q_b, L1_cond_k_w, L1_cond_k_b, L1_cond_v_w, L1_cond_v_b, L1_cond_emb_w, L1_cond_emb_b, L1_cond_sb_norm_w, L1_cond_sb_norm_b, L1_cond_out_w, L1_cond_out_b)
    x = _L2_cond_ref(x, cond_2048, cond_1024, L2_cond_norm1_g, L2_cond_norm1_b, L2_cond_norm2_g, L2_cond_norm2_b, L2_cond_Wx, L2_cond_bx, L2_cond_Wz, L2_cond_bz, L2_cond_Wf, L2_cond_bf, L2_cond_Wada, L2_cond_bada, L2_cond_Wc1, L2_cond_bc1, L2_cond_Wc2, L2_cond_bc2, L2_cond_Wdbc1, L2_cond_Wdt1, L2_cond_bdt1, L2_cond_Alog1, L2_cond_Dp1, L2_cond_Wdbc2, L2_cond_Wdt2, L2_cond_bdt2, L2_cond_Alog2, L2_cond_Dp2)
    x = _L3_cond_ref(x, cond_2048, mask_BxSx1_fk1, 8, L3_cond_ln_w, L3_cond_ln_b, L3_cond_Wq, L3_cond_bq, L3_cond_Wk, L3_cond_bk, L3_cond_Wv, L3_cond_bv, L3_cond_W_emb, L3_cond_b_emb, L3_cond_ln2_w, L3_cond_ln2_b, L3_cond_W_out, L3_cond_b_out)
    return x

_drawn_inputs = setup_inputs


def setup_inputs(seed=0):
    import zlib

    import numpy as np

    out = dict(_drawn_inputs(seed))
    spreads = {'L0_cond_norm_scale': (1.0, 0.2),
     'L0_cond_norm_bias': (0.0, 0.1),
     'L0_cond_bq': (0.0, 0.1),
     'L0_cond_bk': (0.0, 0.1),
     'L0_cond_bv': (0.0, 0.1),
     'L0_cond_film_emb_b': (0.0, 0.1),
     'L0_cond_film_norm_scale': (1.0, 0.2),
     'L0_cond_film_norm_bias': (0.0, 0.1),
     'L0_cond_film_out_b': (0.0, 0.1),
     'L1_cond_norm_w': (1.0, 0.2),
     'L1_cond_norm_b': (0.0, 0.1),
     'L1_cond_q_b': (0.0, 0.1),
     'L1_cond_k_b': (0.0, 0.1),
     'L1_cond_v_b': (0.0, 0.1),
     'L1_cond_emb_b': (0.0, 0.1),
     'L1_cond_sb_norm_w': (1.0, 0.2),
     'L1_cond_sb_norm_b': (0.0, 0.1),
     'L1_cond_out_b': (0.0, 0.1),
     'L2_cond_norm1_g': (1.0, 0.2),
     'L2_cond_norm1_b': (0.0, 0.1),
     'L2_cond_norm2_g': (1.0, 0.2),
     'L2_cond_norm2_b': (0.0, 0.1),
     'L2_cond_bx': (0.0, 0.1),
     'L2_cond_bz': (0.0, 0.1),
     'L2_cond_bf': (0.0, 0.1),
     'L2_cond_bada': (0.0, 0.1),
     'L2_cond_bc1': (0.0, 0.1),
     'L2_cond_bc2': (0.0, 0.1),
     'L2_cond_bdt1': (0.0, 0.1),
     'L2_cond_Dp1': (1.0, 0.2),
     'L2_cond_bdt2': (0.0, 0.1),
     'L2_cond_Dp2': (1.0, 0.2),
     'L3_cond_ln_w': (1.0, 0.2),
     'L3_cond_ln_b': (0.0, 0.1),
     'L3_cond_bq': (0.0, 0.1),
     'L3_cond_bk': (0.0, 0.1),
     'L3_cond_bv': (0.0, 0.1),
     'L3_cond_b_emb': (0.0, 0.1),
     'L3_cond_ln2_w': (1.0, 0.2),
     'L3_cond_ln2_b': (0.0, 0.1),
     'L3_cond_b_out': (0.0, 0.1)}
    factors = {}
    for name, (base, spread) in spreads.items():
        noise = np.random.default_rng([zlib.crc32(name.encode()), seed]).standard_normal(out[name].shape)
        drawn = base * np.exp(spread * noise) if base else spread * noise
        out[name] = jnp.asarray(drawn.astype(out[name].dtype))
    for name, factor in factors.items():
        out[name] = (out[name] * factor).astype(out[name].dtype)
    return out
```

```python
from contextlib import ExitStack

import concourse.bass as bass
from concourse import mybir

F32 = mybir.dt.float32
I32 = mybir.dt.int32
ALU = mybir.AluOpType
ACT = mybir.ActivationFunctionType
AX = mybir.AxisListType.X

P = 128
NB, T, D = 32, 256, 256
E, N, R, CE = 512, 16, 64, 512
TT, KD, KE = T // P, D // P, E // P
H1, DH1, PADH = 16, 16, 32
NQ, N4, E32 = N // 4, 4, 32
EPS = 1e-5
NEG0, NEG1 = -1e30, -1e6
PCOLS = 18
OFFSET = {"A": 2, "C": 1, "S": 0, "T": -1}
ACT_SET = "natural_log_exp_and_others"


class Step:

    def __init__(self, chain, eng, n, emit, after, pos, group=None, inc=1):
        self.chain, self.eng, self.n, self.emit, self.after, self.pos = chain, eng, n, emit, after, pos
        self.group, self.inc, self.plain = group, inc, False


class Ago:

    def __init__(self, chain, name, turns=1):
        self.chain, self.name, self.turns = chain, name, turns


class Chain:

    def __init__(self, name):
        self.name, self.steps, self.count, self.names, self.pos = name, [], {}, {}, 0.0

    def add(self, eng, emit, after, name=None, group=None, cost=1.0):
        key = group or eng
        n = self.count.get(key, 0)
        self.count[key] = n + 1
        step = Step(self, eng, n, emit, after, self.pos, group, 16 if group else 1)
        self.pos += cost
        self.steps.append(step)
        if name:
            assert name not in self.names, name
            self.names[name] = step
        return step

    def key(self, step):
        return (self.name, step.group or step.eng)


def rep(ap, dim, n):
    return ap.unsqueeze(dim).broadcast_to(list(ap.shape[:dim]) + [n] + list(ap.shape[dim:]))


def setup_weights(nc, W, keep, scr, sem):
    with ExitStack() as ctx:
        todo = []

        def sb(name, shape, dt=F32):
            return ctx.enter_context(nc.sbuf_tensor("set_" + name, shape, dt))

        ps = ctx.enter_context(nc.psum_tensor("set_ps", [P, 4, 512], F32))
        loads = []

        def load(dst, src):
            loads.append((dst, src))

        def step(eng, emit):
            todo.append((eng, emit))

        mm_bank = [0]

        def product(out, terms, shape, view=None, scale=None, plus=None):
            b = mm_bank[0] = (mm_bank[0] + 1) % 4
            region = ps[0:shape[0], b, 0:shape[1]]
            for n, (lhsT, rhs) in enumerate(terms):
                step("PE", lambda e, l=lhsT, r=rhs, n=n: e.matmul(region, l, r, start=n == 0, stop=n == len(terms) - 1))
            src = region if view is None else view(region)
            if plus is not None:
                step("DVE", lambda e: e.tensor_tensor(out, src, plus, ALU.add))
            elif scale is not None:
                step("DVE", lambda e: e.tensor_scalar(out, src, scale, None, ALU.mult))
            else:
                step("DVE", lambda e: e.tensor_copy(out, src))

        def transposed(out, blocks, rows, cols, view=None):
            b = mm_bank[0] = (mm_bank[0] + 1) % 4
            for n, blk in enumerate(blocks):
                step("PE", lambda e, n=n, blk=blk: e.transpose(ps[0:cols, b, n * rows:(n + 1) * rows], blk, keep["ident"][0:rows, 0:rows]))
            src = ps[0:cols, b, 0:len(blocks) * rows]
            step("DVE", lambda e: e.tensor_copy(out, src if view is None else view(src)))

        ident = keep["ident"]
        step("Pool", lambda e: e.memset(ident[:], 0.0))
        step("Pool", lambda e: e.affine_select(out=ident[:], in_=ident[:], compare_op=ALU.not_equal, fill=1.0, base=0,
                                               pattern=[[-1, P]], channel_multiplier=1))
        s4 = keep["sum4"]
        step("DVE", lambda e: e.tensor_tensor(s4[:], ident[:, 0:32], ident[:, 32:64], ALU.add))
        step("DVE", lambda e: e.tensor_tensor(s4[:], s4[:], ident[:, 64:96], ALU.add))
        step("DVE", lambda e: e.tensor_tensor(s4[:], s4[:], ident[:, 96:128], ALU.add))
        for name, dh in (("same16", 16), ("same32", 32)):
            m = keep[name]
            g = P // dh
            mv = m[:].rearrange("p (g d) -> p g d", g=g)
            step("Pool", lambda e, m=m: e.memset(m[:], 1.0))
            step("Pool", lambda e, mv=mv, g=g, dh=dh: e.affine_select(
                out=mv, in_=mv, compare_op=ALU.is_ge, fill=0.0, base=0, pattern=[[-dh, g], [0, dh]], channel_multiplier=1))
            step("Pool", lambda e, mv=mv, g=g, dh=dh: e.affine_select(
                out=mv, in_=mv, compare_op=ALU.is_ge, fill=0.0, base=dh - 1, pattern=[[dh, g], [0, dh]], channel_multiplier=-1))
        step("DVE", lambda e: e.memset(keep["ones"][:], 1.0))
        step("DVE", lambda e: e.memset(keep["eps"][:], EPS))
        ones32 = sb("ones32", [1, 32])
        step("DVE", lambda e: e.memset(ones32[:], 1.0))

        def col(name, src, k):
            t = sb(name, [P, k])
            load(t[:], src.rearrange("(k p) -> p k", p=P))
            return t

        def row(name, src):
            t = sb(name, [1, src.shape[0]])
            load(t[:], src.rearrange("(a n) -> a n", a=1))
            return t

        names = {
            "L0": ("norm_scale", "norm_bias", "Wq", "bq", "Wk", "bk", "Wv", "bv", "film_out_W", "film_out_b"),
            "L1": ("norm_w", "norm_b", "q_w", "q_b", "k_w", "k_b", "v_w", "v_b", "out_w", "out_b"),
            "L3": ("ln_w", "ln_b", "Wq", "bq", "Wk", "bk", "Wv", "bv", "W_out", "b_out"),
        }
        for L, ns in names.items():
            a = [W[f"{L}_cond_{n}"] for n in ns]
            g, b = col(L + "g", a[0], KD), col(L + "b", a[1], KD)
            load(keep[L + "wo"][:], a[8].rearrange("(k p) n -> p k n", p=P))
            load(keep[L + "bo"][:], a[9].rearrange("(a n) -> a n", a=1))
            for m, (w, bias) in {"q": a[2:4], "k": a[4:6], "v": a[6:8]}.items():
                raw = sb(L + m + "raw", [P, KD, D])
                load(raw[:], w.rearrange("(k p) n -> p k n", p=P))
                brow = row(L + m + "b", bias)
                wt, bt = keep[L + "w" + m], keep[L + "b" + m]
                padded = L == "L1" and m != "v"
                if padded:
                    step("DVE", lambda e, wt=wt: e.memset(wt[:], 0.0))
                    step("DVE", lambda e, bt=bt: e.memset(bt[0:1, :], 0.0))
                for k in range(KD):
                    dst, src = wt[:, k, :], raw[:, k, :]
                    if padded:
                        dst = dst.rearrange("p (h d) -> p h d", d=PADH)[:, :, 0:DH1]
                        src = src.rearrange("p (h d) -> p h d", d=DH1)
                    step("DVE", lambda e, dst=dst, src=src, g=g, k=k: e.tensor_scalar(dst, src, g[:, k:k + 1], None, ALU.mult))
                dst, view, plus = bt[0:1, :], None, brow[:]
                if padded:
                    dst = dst.rearrange("p (h d) -> p h d", d=PADH)[:, :, 0:DH1]
                    view = lambda r: r.rearrange("p (h d) -> p h d", d=DH1)
                    plus = view(plus)
                product(dst, [(b[:, k:k + 1], raw[:, k, :]) for k in range(KD)], (1, D), view=view, plus=plus)
                if padded and m == "q":
                    spare = bt[0:1, :].rearrange("p (h d) -> p h d", d=PADH)[:, :, DH1:DH1 + 1]
                    step("DVE", lambda e, spare=spare: e.memset(spare, 1.0))
        for L in ("L0", "L1", "L3"):
            n = D if L != "L1" else H1 * PADH
            where = sb(L + "where", [1, n])
            step("DVE", lambda e, w=where, L=L: e.memset(w[:], 0.0 if L == "L1" else 1.0))
            if L == "L1":
                v = where[:].rearrange("p (h d) -> p h d", d=PADH)[:, :, DH1:DH1 + 1]
                step("DVE", lambda e, v=v: e.memset(v, 1.0))
            step("SP", lambda e, w=where, L=L: e.dma_start(keep[L + "bk"][1:2, :], w[:]))

        cond = sb("cond", [NB, CE])
        sig = sb("sig", [NB, CE])
        condT = sb("condT", [P, KE, NB])
        load(cond[:], W["cond_2048"])
        step("ACT", lambda e: e.activation(sig[:], cond[:], ACT.Exp, scale=-1.0))
        step("ACT", lambda e: e.activation(sig[:], sig[:], ACT.Ln, bias=1.0))
        step("ACT", lambda e: e.activation(sig[:], sig[:], ACT.Exp, scale=-1.0))
        step("DVE", lambda e: e.tensor_tensor(cond[:], cond[:], sig[:], ALU.mult))
        transposed(condT[:], [cond[:, k * P:(k + 1) * P] for k in range(KE)], NB, P, lambda r: r.rearrange("p (k b) -> p k b", k=KE))

        pc = sb("pcol", [P, NB, PCOLS])
        film = {"L0": ("film_emb_W", "film_emb_b", "film_norm_scale", "film_norm_bias", 4),
                "L1": ("emb_w", "emb_b", "sb_norm_w", "sb_norm_b", 8), "L3": ("W_emb", "b_emb", "ln2_w", "ln2_b", 14)}
        fw = sb("fw", [P, KE, 2 * D])
        so = sb("so", [P, 4, NB])
        serial = []
        for L, (w, b, s, t, at) in film.items():
            bc, sc, tc = col(L + "fb", W[f"{L}_cond_{b}"], 4), col(L + "fs", W[f"{L}_cond_{s}"], KD), col(L + "ft", W[f"{L}_cond_{t}"], KD)
            step("SP", lambda e, w=w, L=L: e.dma_start(fw[:], W[f"{L}_cond_{w}"].rearrange("(k p) n -> p k n", p=P)))
            for m in range(4):
                product(so[:, m, :], [(fw[:, k, m * P:(m + 1) * P], condT[:, k, :]) for k in range(KE)], (P, NB))
                step("DVE", lambda e, m=m, bc=bc: e.tensor_scalar(so[:, m, :], so[:, m, :], bc[:, m:m + 1], 1.0 if m < 2 else 0.0, ALU.add, ALU.add))
            for k in range(KD):
                a_, b_ = pc[:, :, at + k], pc[:, :, at + 2 + k]
                step("DVE", lambda e, a_=a_, k=k, sc=sc: e.tensor_scalar(a_, so[:, k, :], sc[:, k:k + 1], None, ALU.mult))
                step("DVE", lambda e, b_=b_, k=k, tc=tc: e.scalar_tensor_tensor(b_, so[:, k, :], tc[:, k:k + 1], so[:, 2 + k, :], ALU.mult, ALU.add))

        mi = sb("mi", [NB, T], I32)
        mf = sb("mf", [NB, 3, T])
        mr = sb("mr", [NB, 3, T])
        load(mi[:], W["mask_BxS_ik0"])
        load(mf[:, 1, :], W["mask_BxS_ff1"])
        load(mf[:, 2, :], W["mask_BxSx1_fk1"].rearrange("b t a -> b (t a)"))
        step("DVE", lambda e: e.tensor_copy(mf[:, 0, :], mi[:]))
        step("DVE", lambda e: e.tensor_scalar(mr[:, 0, :], mf[:, 0, :], 1.0, NEG0, ALU.is_equal, ALU.mult))
        step("DVE", lambda e: e.tensor_scalar(mf[:, 0, :], mf[:, 0, :], 1.0, None, ALU.not_equal))
        step("DVE", lambda e: e.tensor_scalar(mr[:, 1:3, :], mf[:, 1:3, :], -1.0, 1.0, ALU.mult, ALU.add))
        step("DVE", lambda e: e.tensor_scalar(mr[:, 1:3, :], mr[:, 1:3, :], NEG1, None, ALU.mult))
        step("SP", lambda e: e.dma_start(scr["mask"], mr[:]))
        for m, at in ((0, 0), (1, 2), (2, 12)):
            transposed(pc[:, :, at:at + 2].rearrange("p b t -> p t b"), [mf[:, m, tt * P:(tt + 1) * P] for tt in range(TT)], NB, P,
                       lambda r: r.rearrange("p (t b) -> p t b", t=TT))

        step("SP", lambda e: e.dma_start(scr["pcol"].rearrange("b p n -> p b n"), pc[:]))

        wada = sb("wada", [P, 6, CE])
        wadaT = sb("wadaT", [P, KE, 3 * D])
        load(wada[:], W["L2_cond_Wada"].rearrange("(m p) k -> p m k", p=P))
        bada = row("bada", W["L2_cond_bada"])
        for k in range(KE):
            for h in range(2):
                transposed(wadaT[:, k, h * 384:(h + 1) * 384], [wada[:, 3 * h + m, k * P:(k + 1) * P] for m in range(3)], P, P)
        ada = sb("ada", [NB, 3, D])
        mod = sb("mod", [NB, 4, D])
        rows = sb("rows", [NB, 3, D])
        for n, src in enumerate(("norm1_g", "norm1_b", "bf")):
            load(rows[:, n, :], W["L2_cond_" + src].partition_broadcast(NB))
        for m in range(3):
            product(ada[:, m, :], [(condT[:, k, :], wadaT[:, k, m * D:(m + 1) * D]) for k in range(KE)]
                    + [(ones32[:], bada[:, m * D:(m + 1) * D])], (NB, D))
        step("DVE", lambda e: e.tensor_scalar(ada[:, 1, :], ada[:, 1, :], 1.0, None, ALU.add))
        step("DVE", lambda e: e.tensor_tensor(mod[:, 0, :], rows[:, 0, :], ada[:, 1, :], ALU.mult))
        step("DVE", lambda e: e.tensor_tensor(mod[:, 1, :], rows[:, 1, :], ada[:, 1, :], ALU.mult))
        step("DVE", lambda e: e.tensor_tensor(mod[:, 1, :], mod[:, 1, :], ada[:, 0, :], ALU.add))
        step("DVE", lambda e: e.tensor_copy(mod[:, 2, :], ada[:, 2, :]))
        step("DVE", lambda e: e.tensor_tensor(mod[:, 3, :], rows[:, 2, :], ada[:, 2, :], ALU.mult))
        step("SP", lambda e: e.dma_start(scr["mod"], mod[:]))

        g2 = col("g2", W["L2_cond_norm2_g"], KD)
        b2row = sb("b2row", [P, D])
        load(b2row[:], W["L2_cond_norm2_b"].partition_broadcast(P))
        tmp = sb("tmp", [P, D])

        def times_b2(out, w, b):
            for c in range(KE):
                step("DVE", lambda e, c=c: e.tensor_tensor(tmp[:], w[:, c, :], b2row[:], ALU.mult))
                step("DVE", lambda e, c=c: e.tensor_reduce(out[:, c:c + 1], tmp[:], AX, ALU.add))
            step("DVE", lambda e: e.tensor_tensor(out[:], out[:], b[:], ALU.add))

        def load_w(name, src, k):
            t = sb(name, [src.shape[0] // k, k, src.shape[1]])
            load(t[:], src.rearrange("(k p) n -> p k n", k=k))
            return t

        wx = load_w("wx", W["L2_cond_Wx"], KE)
        wz = load_w("wz", W["L2_cond_Wz"], KE)
        for k in range(KD):
            transposed(keep["wx"][:, k, :], [wx[:, c, k * P:(k + 1) * P] for c in range(KE)], P, P)
            step("DVE", lambda e, k=k: e.tensor_scalar(keep["wx"][:, k, :], keep["wx"][:, k, :], g2[:, k:k + 1], None, ALU.mult))
        times_b2(keep["bx"], wx, col("bx", W["L2_cond_bx"], KE))
        bz = sb("bzc", [P, KE])
        times_b2(bz, wz, col("bz", W["L2_cond_bz"], KE))
        wf = load_w("wf", W["L2_cond_Wf"], KD)
        for c in range(KE):
            transposed(keep["wf"][:, c, :], [wf[:, k, c * P:(c + 1) * P] for k in range(KD)], P, P)
        wc = sb("wc", [P, KE, E])
        wcT = sb("wcT", [P, KE, E])
        wczT = sb("wczT", [P, KE, D])
        wd = sb("wd", [R + 2 * N, E])
        wdT = sb("wdT", [P, KE, R + 2 * N])
        wdt = sb("wdt", [P, KE, R])
        for s in range(2):
            q = str(s + 1)
            step("SP", lambda e, q=q: e.dma_start(wc[:], W["L2_cond_Wc" + q].rearrange("(k p) n -> p k n", p=P)))
            step("SP", lambda e, q=q: e.dma_start(wd[:], W["L2_cond_Wdbc" + q]))
            step("SP", lambda e, q=q: e.dma_start(wdt[:], W["L2_cond_Wdt" + q].rearrange("(k p) n -> p k n", p=P)))
            for k in range(KE):
                transposed(wcT[:, k, :], [wc[:, c, k * P:(k + 1) * P] for c in range(KE)], P, P)
            transposed(wdT[:], [wd[:, k * P:(k + 1) * P] for k in range(KE)], R + 2 * N, P, lambda r: r.rearrange("p (k r) -> p k r", k=KE))
            transposed(keep["wdt"][0:R, s, :], [wdt[:, c, :] for c in range(KE)], P, R)
            for k in range(KD):
                product(keep["wcz"][:, s, k, :], [(wz[:, c, k * P:(k + 1) * P], wcT[:, c, :]) for c in range(KE)], (P, E), scale=g2[:, k:k + 1])
            for f in range(KE):
                product(wczT[:, f, :], [(wcT[:, c, f * P:(f + 1) * P], wz[:, c, :]) for c in range(KE)], (P, D))
            bc = col("bc" + q, W["L2_cond_bc" + q], KE)
            for f in range(KE):
                product(keep["bcz"][:, s, f:f + 1], [(wcT[:, c, f * P:(f + 1) * P], bz[:, c:c + 1]) for c in range(KE)], (P, 1), plus=bc[:, f:f + 1])
            for k in range(KD):
                product(keep["wd"][:, s, k, :], [(wczT[:, f, k * P:(k + 1) * P], wdT[:, f, :]) for f in range(KE)], (P, R + 2 * N), scale=g2[:, k:k + 1])
            product(keep["bd"][:, s:s + 1], [(wdT[:, f, :], keep["bcz"][:, s, f:f + 1]) for f in range(KE)], (R + 2 * N, 1))
            load(keep["bdt"][:, s, :], W["L2_cond_bdt" + q].rearrange("(k p) -> p k", p=P))
            load(keep["dp"][:, s, :], W["L2_cond_Dp" + q].rearrange("(k p) -> p k", p=P))
            al = sb("al" + q, [P, KE, N])
            load(al[:], W["L2_cond_Alog" + q].rearrange("(k p) n -> p k n", p=P))
            for n4 in range(N4):
                for j in range(4):
                    dst = keep["acol"][n4 * E32:(n4 + 1) * E32, s].rearrange("p (c j) q -> p j c q", j=4)[:, j]
                    src = al[j * E32:(j + 1) * E32].rearrange("p c (q n) -> p n c q", n=N4)[:, n4]
                    step("DVE", lambda e, dst=dst, src=src: e.tensor_copy(dst, src))
        av = keep["acol"][:].rearrange("p s g q -> p (s g q)")
        step("ACT", lambda e: e.activation(av, av, ACT.Exp))
        step("DVE", lambda e: e.tensor_scalar(av, av, -1.0, None, ALU.mult))

        ms, ls = sem("set_step"), sem("set_load")
        block = ctx.enter_context(nc.Block())
        engines = {"PE": block.tensor, "DVE": block.vector, "ACT": block.scalar, "Pool": block.gpsimd, "SP": block.sync}
        total = [0]
        for _, (eng, _) in enumerate(todo):
            total[0] += 16 if eng == "SP" else 1

        for name, on in engines.items():
            @on
            def _(e, name=name):
                if name == "SP":
                    with nc.allow_non_contiguous_dma(reason="columns of bias vectors, once"):
                        for dst, src in loads:
                            e.dma_start(dst, src).then_inc(ls, 16)
                e.wait_ge(ls, 16 * len(loads))
                done, last = 0, None
                if name == "ACT":
                    e.preload_act_table_set(ACT_SET)
                for eng, emit in todo:
                    inc = 16 if eng == "SP" else 1
                    if eng == name:
                        if not (last == name == "PE"):
                            e.wait_ge(ms, done)
                        emit(e).then_inc(ms, inc)
                    done += inc
                    last = eng
                e.wait_ge(ms, done)


def layer_norm(ch, x, out, st, src_after, free_after, tag, eps):
    add = ch.add
    s = [add("DVE", lambda e, t=t: e.bn_stats(st["raw"][:, t, :], x(t)), src_after + free_after, cost=0.5) for t in range(TT)]
    a = [add("DVE", lambda e, t=t: e.bn_aggr(st["mv"][:, t, :], st["raw"][:, t, :]), [s[t]], cost=0.5) for t in range(TT)]
    for step in a:
        step.plain = True
    ln = add("ACT", lambda e: e.activation(st["rs"][:], st["mv"][:, :, 1], ACT.Ln, bias=eps), a)
    r = add("ACT", lambda e: e.activation(st["rs"][:], st["rs"][:], ACT.Exp, scale=-0.5), [ln])
    return [add("DVE", lambda e, t=t: e.tensor_scalar(out[:, t, :], x(t), st["mv"][:, t, 0:1], st["rs"][:, t:t + 1],
                                                      ALU.subtract, ALU.mult), [r, a[t]], cost=0.5) for t in range(TT)]


def turned(ch, ident, src, bank, dst, after, bank_free, dst_free, eng="ACT"):
    t = None
    for c in range(2):
        for r in range(2):
            t = ch.add("PE", lambda e, c=c, r=r: e.transpose(bank[:, c * 256 + r * P:c * 256 + (r + 1) * P], src[:, r, c * P:(c + 1) * P], ident[:]),
                       after + bank_free, cost=0.2)
    flat = dst[:].rearrange("p a b -> p (a b)")
    return t, copy(ch, eng, flat, bank[:, 0:512], [t] + dst_free)


def copy(ch, eng, dst, src, after, cost=1.0):
    if eng == "ACT":
        return ch.add("ACT", lambda e: e.activation(dst, src, ACT.Copy), after, cost=cost)
    return ch.add(eng, lambda e: e.tensor_copy(dst, src), after, cost=cost)


def products(ch, groups, after, cost=0.4):
    last = None
    for out, terms in groups:
        for n, (l, r) in enumerate(terms):
            last = ch.add("PE", lambda e, o=out, l=l, r=r, n=n, m=len(terms): e.matmul(o, l, r, start=n == 0, stop=n == m - 1), after, cost=cost)
    return last


def token_projection(bank, xT, w, bias_row, ones):
    return [(bank[:, t * D:(t + 1) * D], [(xT[:, k, t * P:(t + 1) * P], w[:, k, :]) for k in range(KD)] + [(ones[0:1, 0:P], bias_row)]) for t in range(TT)]


def film_tail(ch, k, B, L, at, ysrc, y_after, gone, x, x_out, x_after):
    add = ch.add
    n2 = layer_norm(ch, ysrc, B["yh"], B["st"], y_after, gone, L, k["eps"][:])
    t = None
    bank = B["bank"][2]
    for c in range(2):
        for r in range(2):
            t = add("PE", lambda e, c=c, r=r: e.transpose(bank[:, c * 256 + r * P:c * 256 + (r + 1) * P], B["yh"][:, r, c * P:(c + 1) * P], k["ident"][:]),
                    n2 + gone, cost=0.2)
    pc = B["pc"]
    hs = [add("DVE", lambda e, c=c: e.tensor_scalar(B["h"][:, c, :], bank[:, c * 256:(c + 1) * 256], pc[:, at + c:at + c + 1],
                                                    pc[:, at + 2 + c:at + 3 + c], ALU.mult, ALU.add), [t] + gone) for c in range(2)]
    es = [add("ACT", lambda e: e.activation(B["s"][:], B["h"][:], ACT.Exp, scale=-1.0), hs + gone)]
    l = add("ACT", lambda e: e.activation(B["s"][:], B["s"][:], ACT.Ln, bias=1.0), es)
    g = add("ACT", lambda e: e.activation(B["s"][:], B["s"][:], ACT.Exp, scale=-1.0), [l])
    m = add("DVE", lambda e: e.tensor_tensor(B["h"][:], B["h"][:], B["s"][:], ALU.mult), [g] + hs)
    o = products(ch, token_projection(B["bank"][3], B["h"], k[L + "wo"], k[L + "bo"][:], k["ones"]), [m] + gone)
    return add("DVE", lambda e: e.tensor_tensor(x_out[:].rearrange("p a b -> p (a b)"), B["bank"][3][:, 0:512],
                                                x[:].rearrange("p a b -> p (a b)"), ALU.add), [o] + x_after)


def linear_attention(ch, k, B, L, dh, mask_at, film_at, x, x_after, gate):
    add, bank, pc = ch.add, B["bank"], B["pc"]
    H = D // dh
    n1 = layer_norm(ch, lambda t: x[:, t, :], B["xh"], B["st"], x_after, gate, L, k["eps"][:])
    _, xT = turned(ch, k["ident"], B["xh"], bank[0], B["xT"], n1, gate, gate)
    q = products(ch, token_projection(bank[1], B["xT"], k[L + "wq"], k[L + "bq"][:], k["ones"]), [xT])
    kk = products(ch, [(bank[2][:, c * 256:(c + 1) * 256], [(k[L + "wk"][:, i, c * P:(c + 1) * P], B["xT"][:, i, :]) for i in range(KD)]
                        + [(k[L + "bk"][0:2, c * P:(c + 1) * P], B["om" + L][0:2, :])]) for c in range(KD)], [xT] + gate)
    v = products(ch, token_projection(bank[3], B["xT"], k[L + "wv"], k[L + "bv"][:], k["ones"]), [xT] + gate)
    q3 = bank[1][:, 0:512].rearrange("p (h d) -> p h d", d=dh)
    qs = B["q"][:].rearrange("p t n -> p (t n)").rearrange("p (h d) -> p h d", d=dh)
    qm, qr = B["qm"][:, 0:TT * H], B["qr"][:, 0:TT * H]
    a = add("DVE", lambda e: e.tensor_reduce(qm, q3, AX, ALU.max), [q] + gate)
    b = add("DVE", lambda e: e.tensor_tensor(qs, q3, rep(qm, 2, dh), ALU.subtract), [a])
    km = add("DVE", lambda e: e.tensor_reduce(B["km"][:], bank[2][:, 0:512].rearrange("p (c t) -> p c t", c=KD), AX, ALU.max, negate=True), [kk])
    qe = add("ACT", lambda e: e.activation(B["q"][:], B["q"][:], ACT.Exp), [b])
    ke = [add("ACT", lambda e, c=c: e.activation(B["ke"][:, c, :], bank[2][:, c * 256:(c + 1) * 256], ACT.Exp, bias=B["km"][:, c:c + 1],
                                                 accum_out=B["ks"][:, c:c + 1]), [km] + gate) for c in range(KD)]
    vm = [add("DVE", lambda e, t=t: e.tensor_scalar(B["v"][:, t, :], bank[3][:, t * D:(t + 1) * D], pc[:, mask_at + t:mask_at + t + 1], None, ALU.mult), [v])
          for t in range(TT)]
    kr = add("DVE", lambda e: e.reciprocal(B["kr"][:], B["ks"][:]), ke)
    qsum = add("DVE", lambda e: e.tensor_reduce(qr, qs, AX, ALU.add), [qe])
    qrec = add("DVE", lambda e: e.reciprocal(qm, qr), [qsum])
    qn = add("Pool", lambda e: e.tensor_tensor(qs, qs, rep(qm, 2, dh), ALU.mult), [qrec])
    kn = ke
    if L == "L0":
        kn = [add("DVE", lambda e, c=c: e.tensor_scalar(B["ke"][:, c, :], B["ke"][:, c, :], B["kr"][:, c:c + 1], None, ALU.mult), ke + [kr], cost=0.4)
              for c in range(KD)]
    lhs, rhs = (B["v"], B["xh"]) if L == "L0" else (B["xh"], B["v"])
    _, kt = turned(ch, k["ident"], B["ke"], bank[0], B["xh"], kn, [xT] + vm, [xT])
    at = products(ch, [(bank[2][:, c * P:(c + 1) * P], [(lhs[:, t, c * P:(c + 1) * P], rhs[:, t, c * P:(c + 1) * P]) for t in range(TT)])
                       for c in range(KD)], vm + [kt] + ke, cost=0.2)
    bd = [add("DVE", lambda e, c=c: e.scalar_tensor_tensor(B["bd"][:, c, :], bank[2][:, c * P:(c + 1) * P],
                                                           1.0 if L == "L0" else B["kr"][:, c:c + 1],
                                                           k["same%d" % dh][:], ALU.mult, ALU.mult), [at, kr]) for c in range(KD)]
    _, qT = turned(ch, k["ident"], B["q"], bank[1], B["xT"], [qn], [b], [v])
    y = products(ch, [(bank[0][:, t * D + c * P:t * D + (c + 1) * P], [(B["xT"][:, c, t * P:(t + 1) * P], B["bd"][:, c, :])])
                      for t in range(TT) for c in range(KD)], [qT, kt] + bd, cost=0.2)
    BB = dict(B, yh=B["q"], h=B["ke"], s=B["xh"])
    return film_tail(ch, k, BB, L, film_at, lambda t: bank[0][:, t * D:(t + 1) * D], [y], [qT] + bd + vm, x, x, [])


def softmax_attention(ch, k, B, x, x_after):
    add, bank, pc, L = ch.add, B["bank"], B["pc"], "L1"
    n1 = layer_norm(ch, lambda t: x[:, t, :], B["xh"], B["st"], x_after, [], L, k["eps"][:])
    _, xT = turned(ch, k["ident"], B["xh"], bank[0], B["xT"], n1, x_after, x_after)
    got = {}
    for m, bb in (("q", (1, 2)), ("k", (0, 3))):
        for half in range(2):
            bk = bank[bb[half]]
            p = products(ch, [(bk[:, c * 256:(c + 1) * 256], [(k[L + "w" + m][:, i, (2 * half + c) * P:(2 * half + c + 1) * P], B["xT"][:, i, :]) for i in range(KD)]
                               + [(k[L + "bq"][0:1, (2 * half + c) * P:(2 * half + c + 1) * P], k["ones"][0:1, 0:T]) if m == "q" else
                                  (k[L + "bk"][0:2, (2 * half + c) * P:(2 * half + c + 1) * P], B["omL1"][0:2, :])]) for c in range(2)], [xT] + x_after)
            got[m, half] = copy(ch, "ACT" if m == "q" else "DVE", B[m + "P"][:, 2 * half:2 * half + 2, :].rearrange("p a b -> p (a b)"), bk[:, 0:512], [p])
    v = products(ch, token_projection(bank[1], B["xT"], k[L + "wv"], k[L + "bv"][:], k["ones"]), [got["q", 0]])
    vm = [add("DVE", lambda e, t=t: e.tensor_scalar(B["v"][:, t, :], bank[1][:, t * D:(t + 1) * D], pc[:, 2 + t:3 + t], None, ALU.mult), [v])
          for t in range(TT)]
    proj = list(got.values()) + vm
    Eb, ETb = (B["q"], B["ke"]), (B["xh"], B["et"])
    sc, tb, yb = (bank[0], bank[1]), bank[2], bank[3]
    y_last, hist = None, {}

    def scores(h):
        i, c = h % 4, h // 4
        o = proj if h < 2 else hist[h - 2, "exp"]
        for t in range(TT):
            s = add("PE", lambda e, t=t: e.matmul(sc[h % 2][:, t * 256:(t + 1) * 256], B["qP"][32 * i:32 * i + DH1 + 1, c, t * P:(t + 1) * P],
                                                  B["kP"][32 * i:32 * i + DH1 + 1, c, :], start=True, stop=True, tile_position=(32 * i, 0)), o, cost=0.5)
        free = hist[h - 2, "exp"] if h >= 2 else []
        m = add("DVE", lambda e: e.tensor_reduce(B["sm"][:, h % 2, :], sc[h % 2][:, 0:512].rearrange("p (t m) -> p t m", t=TT), AX, ALU.max, negate=True),
                [s] + free)
        free = [hist[h - 2, "turn"]] if h >= 2 else []
        hist[h, "exp"] = [add("ACT", lambda e, t=t: e.activation(Eb[h % 2][:, t, :], sc[h % 2][:, t * 256:(t + 1) * 256], ACT.Exp,
                                                                 bias=B["sm"][:, h % 2, t:t + 1], accum_out=B["ssum"][:, t, h:h + 1]), [m] + free + x_after)
                          for t in range(TT)]

    def values(h):
        free = [hist[h - 1, "et"]] if h else [got["q", 1]]
        t = None
        for mt in range(2):
            for nt in range(2):
                t = add("PE", lambda e, mt=mt, nt=nt: e.transpose(tb[:, mt * 256 + nt * P:mt * 256 + (nt + 1) * P], Eb[h % 2][:, nt, mt * P:(mt + 1) * P],
                                                                  k["ident"][:]), hist[h, "exp"] + free, cost=0.2)
        hist[h, "turn"] = t
        free = [hist[h - 2, "y"]] if h >= 2 else [xT] + x_after
        et = hist[h, "et"] = copy(ch, "ACT" if h % 2 else "DVE", ETb[h % 2][:].rearrange("p a b -> p (a b)"), tb[:, 0:512], [t] + free)
        hist[h, "y"] = products(ch, [(yb[:, t * D + h * DH1:t * D + (h + 1) * DH1],
                                      [(ETb[h % 2][:, mt, t * P:(t + 1) * P], B["v"][:, mt, h * DH1:(h + 1) * DH1]) for mt in range(2)])
                                     for t in range(TT)], [et] + proj, cost=0.1)

    scores(0)
    for h in range(H1):
        if h + 1 < H1:
            scores(h + 1)
        values(h)
    rec = add("DVE", lambda e: e.reciprocal(B["srec"][:], B["ssum"][:].rearrange("p t h -> p (t h)")), hist[H1 - 1, "exp"] + hist[H1 - 2, "exp"])
    yn = add("DVE", lambda e: e.tensor_tensor(B["qP"][:, 0:2, :].rearrange("p a b -> p (a b)").rearrange("p (g d) -> p g d", d=DH1),
                                              yb[:, 0:512].rearrange("p (g d) -> p g d", d=DH1), rep(B["srec"][:], 2, DH1), ALU.mult),
             [rec, hist[H1 - 1, "y"]])
    BB = dict(B, yh=B["ke"], h=B["xT"], s=B["xh"])
    return film_tail(ch, k, BB, L, 8, lambda t: B["qP"][:, t, :], [yn], [hist[H1 - 1, "y"], hist[H1 - 1, "et"]], x, x, [])


def chain_buffers(sb, name, shared=None):
    B = shared or {n: sb(f"{name}_{n}", [P, 2, 256]) for n in ("x", "xh", "xT", "q", "ke", "v")}
    if not shared:
        B["bd"] = sb(f"{name}_bd", [P, 2, P])
    B["st"] = {"raw": sb(f"{name}_raw", [P, 2, 6]), "mv": sb(f"{name}_mv", [P, 2, 2]), "rs": sb(f"{name}_rs", [P, 2])}
    B["qm"], B["qr"] = sb(f"{name}_qm", [P, 32]), sb(f"{name}_qr", [P, 32])
    for n in ("km", "ks", "kr"):
        B[n] = sb(f"{name}_{n}", [P, 2])
    B["pc"] = sb(f"{name}_pc", [P, PCOLS])
    return B


def bass_kernel(nc, W, out):
    with ExitStack() as ctx:
        def sb(name, shape, dt=F32):
            return ctx.enter_context(nc.sbuf_tensor(name, shape, dt))

        def sem(name):
            return ctx.enter_context(nc.semaphore(name))

        k = {}
        for L in ("L0", "L1", "L3"):
            for m in "qkvo":
                wide = H1 * PADH if L == "L1" and m in "qk" else D
                k[L + "w" + m] = sb(L + "w" + m, [P, KD, wide])
                k[L + "b" + m] = sb(L + "b" + m, [2 if m == "k" else 1, wide])
        k["wx"], k["wcz"], k["wd"] = sb("wx", [P, KD, E]), sb("wcz", [P, 2, KD, E]), sb("wd", [P, 2, KD, R + 2 * N])
        k["wdt"], k["wf"] = sb("wdt", [R, 2, E]), sb("wf", [P, KE, D])
        k["bx"], k["bcz"], k["bd"] = sb("bx", [P, KE]), sb("bcz", [P, 2, KE]), sb("bd", [R + 2 * N, 2])
        k["bdt"], k["dp"], k["acol"] = sb("bdt", [P, 2, KE]), sb("dp", [P, 2, KE]), sb("acol", [P, 2, E // E32, NQ])
        k["ident"], k["sum4"], k["same16"], k["same32"] = sb("ident", [P, P]), sb("sum4", [P, E32]), sb("same16", [P, P]), sb("same32", [P, P])
        k["ones"], k["eps"] = sb("ones", [1, T]), sb("eps", [P, 1])

        def dram(name, shape):
            return nc.dram_tensor("scr_" + name, shape, F32, kind="Internal").ap()

        scr = {"pcol": dram("pcol", [NB, P, PCOLS]),
               "mask": dram("mask", [NB, 3, T]), "mod": dram("mod", [NB, 4, D]),
               "x2": dram("x2", [NB, P, 2, 256]),
               "res": dram("res", [NB, P, 2, 256]),
               "dd": dram("dd", [NB, 2, KE, P, 2 * T]),
               "bc": dram("bc", [NB, 2, 2 * N, T]),
               "wa": dram("wa", [NB, P, KE, 2, T]),
               "g": dram("g", [NB, P, KE, T])}
        setup_weights(nc, W, k, scr, sem)

        A, C = chain_buffers(sb, "A"), {}
        A["qP"], A["kP"] = sb("A_qP", [P, 4, 256]), sb("A_kP", [P, 4, 256])
        A["et"] = sb("A_et", [P, 2, 256])
        A["sm"], A["ssum"], A["srec"] = sb("A_sm", [P, 2, 2]), sb("A_ssum", [P, 2, H1]), sb("A_srec", [P, 2 * H1])
        A["omL0"], A["omL1"] = sb("omL0", [2, T]), sb("omL1", [2, T])
        for n in ("x", "xh", "xs", "xT", "r"):
            C[n] = sb("C_" + n, [P, 2, 256])
        C["st"] = {"raw": sb("C_raw", [P, 2, 6]), "mv": sb("C_mv", [P, 2, 2]), "rs": sb("C_rs", [P, 2])}
        C["mod"], C["dd"], C["tmp"] = sb("C_mod", [P, 4, D]), sb("C_dd", [P, KE, 2, T]), sb("C_tmp", [P, KE, T])
        C["wa"], C["dbc"] = sb("C_wa", [P, KE, 2, T]), sb("C_dbc", [R + 2 * N, T])
        S = {"slot": sb("S_slot", [P, 2, 4, 2, T]), "bc": sb("S_bc", [P, 2, 2 * NQ, T]), "dA": sb("S_dA", [P, 2, 2, 4, T]),
             "X": sb("S_X", [P, 4, 4, T]), "wa": sb("S_wa", [P, KE, 2, T]), "g": sb("S_g", [P, KE, T])}
        v = C["dd"][:].rearrange("p c a t -> p c (a t)")
        two = lambda ap: ap.rearrange("p (a b) -> p a b", a=2)
        Tt = chain_buffers(sb, "T", {"x": C["x"], "xh": C["xh"], "xT": C["xT"], "q": two(v[:, 0]), "ke": two(v[:, 1]), "v": two(v[:, 2]),
                                     "bd": two(v[:, 3, 0:256]), "gate": v[:, 3, 256:512],
                                     "g": C["wa"][:, 0:2].rearrange("p c a t -> p (c a) t")})
        Tt["omL3"] = sb("omL3", [2, T])
        ps = ctx.enter_context(nc.psum_tensor("ps", [P, 8, 512], F32))
        A["bank"] = [ps[:, b, :] for b in (0, 1, 2, 3)]
        C["bank"] = [ps[:, b, :] for b in (4, 5, 6)]
        Tt["bank"] = [ps[:, b, :] for b in (4, 5, 6, 4)]
        S["bank"] = ps[:, 7, :]
        chains = {"A": Chain("A"), "C": Chain("C"), "S": Chain("S"), "T": Chain("T")}
        chain_a(chains["A"], k, A, W["x"], scr)
        chain_c(chains["C"], k, C, scr, chains)
        chain_s(chains["S"], k, S, scr, chains)
        chain_t(chains["T"], k, Tt, scr, out, chains)
        run(nc, chains, S, A, Tt, sem)


def load(ch, dst, src, after, group, name=None, cost=0.3):
    f = lambda v, b: v(b) if callable(v) else v
    return ch.add("SP", lambda e, b: e.dma_start(f(dst, b), f(src, b)), after, name=name, group=group, cost=cost)


def at_batch(ap, b):
    return ap[b] if isinstance(b, int) else ap[bass.ds(b, 1)].squeeze(0)


def chain_a(ch, k, B, x_in, scr):
    load(ch, B["x"][:], lambda b: at_batch(x_in, b).rearrange("(t p) d -> p t d", p=P), [], "Ain")
    load(ch, B["pc"][:, 0:12], lambda b: at_batch(scr["pcol"], b)[:, 0:12], [], "Ain")
    load(ch, B["omL0"][1:2, :], lambda b: at_batch(scr["mask"], b)[0:1, :], [], "Ain")
    got = load(ch, B["omL1"][1:2, :], lambda b: at_batch(scr["mask"], b)[1:2, :], [], "Ain")
    ch.pos = 4
    x1 = linear_attention(ch, k, B, "L0", D // 16, 0, 4, B["x"], [got], [])
    x2 = softmax_attention(ch, k, B, B["x"], [x1])
    load(ch, lambda b: at_batch(scr["x2"], b), B["x"][:], [x2], "Aout", name="stored")


def chain_c(ch, k, B, scr, chains):
    add, bank, st = ch.add, B["bank"], B["st"]
    banks = [Ago("T", "last")]
    got = load(ch, B["x"][:], lambda b: at_batch(scr["x2"], b), [Ago("A", "stored")], "Cin")
    got = load(ch, B["mod"][:], lambda b: at_batch(scr["mod"], b).partition_broadcast(P), [], "Cin")
    ch.pos = 3
    x, xs, mod = B["x"], B["xs"], B["mod"]
    n1 = layer_norm(ch, lambda t: x[:, t, :], B["xh"], st, [got], [], "C1", k["eps"][:])
    mo = lambda n: rep(mod[:, n, :], 1, TT)
    m1 = add("DVE", lambda e: e.tensor_tensor(xs[:], B["xh"][:], mo(0), ALU.mult), n1)
    m2 = add("DVE", lambda e: e.tensor_tensor(xs[:], xs[:], mo(1), ALU.add), [m1])
    r1 = add("Pool", lambda e: e.tensor_tensor(B["r"][:], xs[:], mo(2), ALU.mult), [m2])
    r2 = add("Pool", lambda e: e.tensor_tensor(B["r"][:], B["r"][:], x[:], ALU.add), [r1], cost=0.2)
    r3 = add("Pool", lambda e: e.tensor_tensor(B["r"][:], B["r"][:], mo(3), ALU.add), [r2], cost=0.2)
    n2 = layer_norm(ch, lambda t: xs[:, t, :], B["xh"], st, [m2], n1, "C2", k["eps"][:])
    _, xT = turned(ch, k["ident"], B["xh"], bank[0], B["xT"], n2, banks, [])
    d_free, u_free, s_out = [xT], [], None
    for s in range(2):
        dbc_bank = bank[s][0:R + 2 * N, 0:T]
        p = products(ch, [(dbc_bank, [(k["wd"][:, s, i, :], B["xT"][:, i, :]) for i in range(KD)])], d_free + banks)
        dbc = add("ACT", lambda e, s=s, o=dbc_bank: e.activation(B["dbc"][:], o, ACT.Identity, bias=k["bd"][:, s:s + 1]), [p] + u_free)
        bcs = load(ch, lambda b, s=s: at_batch(scr["bc"], b)[s], B["dbc"][R:R + 2 * N, :], [dbc], "Cbc", name="bc%d" % s)
        pres, us = [], []
        for h in range(2):
            pre, zb = bank[2], bank[1 - s]
            p = products(ch, [(pre[:, c * T:(c + 1) * T], [(k["wdt"][0:R, s, (2 * h + c) * P:(2 * h + c + 1) * P], B["dbc"][0:R, :])]) for c in range(2)],
                         [dbc] + pres + banks)
            for c in range(2):
                f, o = 2 * h + c, pre[:, c * T:(c + 1) * T]
                pres.append(add("DVE", lambda e, f=f, o=o, s=s: e.tensor_scalar(B["dd"][:, f, 0, :], o, k["bdt"][:, s, f:f + 1], None, ALU.add),
                                [p] + u_free, cost=0.4))
            p = products(ch, [(zb[:, c * T:(c + 1) * T], [(k["wcz"][:, s, i, (2 * h + c) * P:(2 * h + c + 1) * P], B["xT"][:, i, :]) for i in range(KD)])
                              for c in range(2)], [dbc, xT] + us + u_free + banks)
            for c in range(2):
                f, o = 2 * h + c, zb[:, c * T:(c + 1) * T]
                us.append(add("ACT", lambda e, f=f, o=o, s=s: e.activation(B["dd"][:, f, 1, :], o, ACT.Identity, bias=k["bcz"][:, s, f:f + 1]), [p] + u_free, cost=0.4))
        ab = add("ACT", lambda e: e.activation(B["tmp"][:], B["dd"][:, :, 0, :], ACT.Abs), pres + u_free)
        e1 = add("ACT", lambda e: e.activation(B["tmp"][:], B["tmp"][:], ACT.Exp, scale=-1.0), [ab])
        e2 = add("ACT", lambda e: e.activation(B["tmp"][:], B["tmp"][:], ACT.Ln, bias=1.0), [e1])
        w = []
        for c in range(KE):
            if s == 0:
                w.append(add("DVE", lambda e, c=c: e.tensor_scalar(B["wa"][:, c, 0, :], B["dd"][:, c, 1, :], k["dp"][:, 0, c:c + 1], None, ALU.mult), us, cost=0.3))
            else:
                w.append(add("DVE", lambda e, c=c: e.scalar_tensor_tensor(B["wa"][:, c, 0, :], B["dd"][:, c, 1, :], k["dp"][:, 1, c:c + 1],
                                                                          B["wa"][:, c, 0, :], ALU.mult, ALU.add), us + w0, cost=0.3))
        w0 = w
        dl = add("DVE", lambda e: e.scalar_tensor_tensor(B["dd"][:, :, 0, :], B["dd"][:, :, 0, :], 0.0, B["tmp"][:], ALU.max, ALU.add), [e2])
        du = add("DVE", lambda e: e.tensor_tensor(B["dd"][:, :, 1, :], B["dd"][:, :, 1, :], B["dd"][:, :, 0, :], ALU.mult), [dl] + us + w)
        s_out = load(ch, lambda b, s=s: at_batch(scr["dd"], b)[s].rearrange("c p f -> p c f"), B["dd"][:].rearrange("p c a t -> p c (a t)"), [du], "Cdd",
                     name="dd%d" % s)
        d_free, u_free = us, [s_out, du, bcs]
    hs = []
    for h in range(2):
        bk = bank[h]
        p = products(ch, [(bk[:, c * T:(c + 1) * T], [(k["wx"][:, i, (2 * h + c) * P:(2 * h + c + 1) * P], B["xT"][:, i, :]) for i in range(KD)]) for c in range(2)],
                     us + [dbc])
        for c in range(2):
            f, o = 2 * h + c, bk[:, c * T:(c + 1) * T]
            hs.append(add("DVE", lambda e, f=f, o=o: e.tensor_scalar(B["wa"][:, f, 1, :], o, k["bx"][:, f:f + 1], None, ALU.add), [p], cost=0.4))
    e0 = add("ACT", lambda e: e.activation(B["tmp"][:], B["wa"][:, :, 1, :], ACT.Exp, scale=-1.0), hs + [dl])
    e1 = add("ACT", lambda e: e.activation(B["tmp"][:], B["tmp"][:], ACT.Ln, bias=1.0), [e0])
    e2 = add("ACT", lambda e: e.activation(B["tmp"][:], B["tmp"][:], ACT.Exp, scale=-1.0), [e1])
    m = add("DVE", lambda e: e.tensor_tensor(B["wa"][:, :, 1, :], B["wa"][:, :, 1, :], B["tmp"][:], ALU.mult), [e2] + hs, name="last")
    load(ch, lambda b: at_batch(scr["wa"], b), B["wa"][:], [m] + w0, "Cwa", name="wa")
    load(ch, lambda b: at_batch(scr["res"], b), B["r"][:], [r3], "Cres", name="res")


def chain_s(ch, k, B, scr, chains):
    add, n = ch.add, ch.names
    X, dA, bc = B["X"], B["dA"], B["bc"]
    UNITS, SLOTS = 4 * 2 * NQ, 8

    def unit(name, u):
        return n[name + str(u)] if u >= 0 else Ago("S", name + str(u + UNITS))

    def load_slot(m):
        c, s, u = m // 2, m % 2, 4 * m
        src = lambda b: at_batch(scr["dd"], b)[s, c].rearrange("(j e) f -> e j f", e=E32)
        for n4 in range(N4):
            load(ch, B["slot"][n4 * E32:(n4 + 1) * E32, m % 2].rearrange("p j a t -> p j (a t)"), src,
                 [unit("exp", u - 5), unit("bmul", u - 5), Ago("C", "dd%d" % s)], "Sslot%d" % (m % 2), name="slot%d_%d" % (m, n4), cost=0)

    def load_bc(s):
        for n4 in range(N4):
            src = lambda b, n4=n4: at_batch(scr["bc"], b)[s].rearrange("(q n) t -> n q t", n=N4)[n4].partition_broadcast(E32)
            load(ch, bc[n4 * E32:(n4 + 1) * E32, s], src,
                 [unit("cmul", 4 * s + 3 - 8), unit("bmul", 4 * s + 3 - 8), Ago("C", "bc%d" % s)], "Sbc%d" % s, name="bc%d_%d" % (s, n4), cost=0)

    load_slot(0)
    load_bc(0)
    load_slot(1)
    load_bc(1)
    wa = load(ch, B["wa"][:], lambda b: at_batch(scr["wa"], b), [Ago("S", "gate3"), Ago("C", "wa")], "Swa", cost=0)

    def emit_exp(u):
        m, c, s, q = u // 4, u // 8, (u // 4) % 2, u % 4
        lo = 1 - s
        for j in range(4):
            add("ACT", lambda e, j=j: e.activation(dA[:, s, q % 2, j, lo:lo + T - 1], B["slot"][:, m % 2, j, 0, lo:lo + T - 1], ACT.Exp,
                                                   scale=k["acol"][:, s, 4 * c + j, q:q + 1]),
                [n["slot%d_3" % m], unit("scan", u - 2 if q >= 2 else u - 6)], name="exp%d" % u if j == 3 else None, cost=0)

    def emit_bmul(u):
        m, s, q = u // 4, (u // 4) % 2, u % 4
        add("DVE", lambda e: e.tensor_tensor(X[:, u % 4], B["slot"][:, m % 2, :, 1, :], rep(bc[:, s, q, :], 1, 4), ALU.mult),
            [n["slot%d_3" % m], n["bc%d_3" % s], unit("sum", u - 4)], name="bmul%d" % u, cost=0)

    def emit_scan(u):
        s, q = (u // 4) % 2, u % 4
        flat = lambda ap: ap.rearrange("p j t -> p (j t)")[:, ::-1] if s else ap.rearrange("p j t -> p (j t)")
        add("DVE", lambda e: e.tensor_tensor_scan(flat(X[:, u % 4]), flat(dA[:, s, q % 2]), flat(X[:, u % 4]), 0.0, ALU.mult, ALU.add),
            [n["exp%d" % u], n["bmul%d" % u]], name="scan%d" % u, cost=0)

    def emit_cmul(u):
        s, q = (u // 4) % 2, u % 4
        add("Pool", lambda e: e.tensor_tensor(X[:, u % 4], X[:, u % 4], rep(bc[:, s, NQ + q, :], 1, 4), ALU.mult), [n["scan%d" % u]], name="cmul%d" % u, cost=0)

    def emit_sum(u):
        c, first, last = u // 8, u % 8 == 0, u % 8 == 7
        free = [n["gate%d" % (c - 1)] if c else Ago("S", "gate3")] if first else []
        for j in range(4):
            add("PE", lambda e, j=j: e.matmul(B["bank"][32 * j:32 * j + 32, (c % 2) * T:(c % 2 + 1) * T], k["sum4"][:], X[:, u % 4, j, :],
                                              start=first, stop=last, tile_position=(0, 32 * j), skip_group_check=True),
                [n["cmul%d" % u]] + free, name="sum%d" % u if j == 3 else None, cost=0)
        if last:
            g = B["g"][:, c, :]
            a = add("DVE", lambda e: e.tensor_tensor(g, B["bank"][:, (c % 2) * T:(c % 2 + 1) * T], B["wa"][:, c, 0, :], ALU.add),
                    [n["sum%d" % u], wa, Ago("S", "g")], cost=0)
            add("DVE", lambda e: e.tensor_tensor(g, g, B["wa"][:, c, 1, :], ALU.mult), [a], name="gate%d" % c, cost=0)

    for v in range(UNITS + 4):
        ch.pos = v
        if v < UNITS:
            emit_exp(v)
            emit_bmul(v)
        if 1 <= v <= UNITS:
            emit_scan(v - 1)
            if (v - 1) % 4 == 3 and (v - 1) // 4 + 2 < SLOTS:
                load_slot((v - 1) // 4 + 2)
            emit_cmul(v - 1)
        if 2 <= v <= UNITS + 1:
            emit_sum(v - 2)
    load(ch, lambda b: at_batch(scr["g"], b), B["g"][:], [n["gate3"]], "Sg", name="g", cost=1)


def chain_t(ch, k, B, scr, out, chains):
    load(ch, B["g"][:], lambda b: at_batch(scr["g"], b), [Ago("S", "g")], "Tin")
    load(ch, B["x"][:], lambda b: at_batch(scr["res"], b), [Ago("C", "res", 2)], "Tin")
    load(ch, B["gate"][:], lambda b: at_batch(scr["mod"], b)[2].partition_broadcast(P), [], "Tin")
    load(ch, B["omL3"][1:2, :], lambda b: at_batch(scr["mask"], b)[2:3, :], [], "Tin")
    got = load(ch, B["pc"][:, 12:18], lambda b: at_batch(scr["pcol"], b)[:, 12:18], [], "Tin")
    ch.pos = 3
    bk = B["bank"][0]
    o = products(ch, [(bk[:, t * D:(t + 1) * D], [(B["g"][:, c, t * P:(t + 1) * P], k["wf"][:, c, :]) for c in range(KE)]) for t in range(TT)],
                 [got, Ago("C", "last", 0)])
    xf = B["x"]
    a = ch.add("DVE", lambda e: e.tensor_tensor(B["xh"][:], bk[:, 0:512].rearrange("p (t d) -> p t d", t=TT), rep(B["gate"][:], 1, TT), ALU.mult), [o, got])
    b_ = ch.add("DVE", lambda e: e.tensor_tensor(xf[:], xf[:], B["xh"][:], ALU.add), [a])
    last = linear_attention(ch, k, B, "L3", 32, 12, 14, xf, [b_], [])
    ch.names["last"] = last
    load(ch, lambda b: at_batch(out, b).rearrange("(t p) d -> p t d", p=P), xf[:], [last], "Tout")


ENGINES = ("PE", "DVE", "ACT", "Pool", "SP")
SPAN = {"A": (0.0, 1.0), "C": (0.0, 0.55), "S": (0.0, 1.0), "T": (0.56, 1.0)}


def run(nc, chains, S, A, Tt, sem):
    order = []
    for name, ch in chains.items():
        lo, hi = SPAN[name]
        top = max(s.pos for s in ch.steps)
        order += [(lo + (hi - lo) * s.pos / top, name != "S", name, i, s) for i, s in enumerate(ch.steps)]
    order.sort(key=lambda o: o[:4])
    place = {id(o[4]): n for n, o in enumerate(order)}
    keys = {(c, key) for c, ch in chains.items() for key in ch.count}
    sems = {key: sem("s_%s_%s" % key) for key in sorted(keys)}
    ready = sem("s_ready")
    spare = {eng: sem("s_spare_" + eng) for eng in ENGINES}
    lasts = {c: list({s.group or s.eng: s for s in ch.steps}.values()) for c, ch in chains.items()}

    def emit(e, eng, turn):
        known, started = {}, set()
        for _, _, name, _, step in order:
            ch = chains[name]
            if step.eng != eng:
                continue
            batch = turn + OFFSET[name]
            if isinstance(turn, int) and not 0 <= batch < NB:
                continue
            waits = [(a, 0) if isinstance(a, Step) else (chains[a.chain].names[a.name], a.turns) for a in step.after]
            if name != "S" and name not in started:
                started.add(name)
                waits += [(s, 1) for s in lasts[name]]
                waits += {"C": [(s, 1) for s in lasts["T"]], "T": [(s, 0) for s in lasts["C"]]}.get(name, [])
            need = {}
            for s, turns in waits:
                if turns == 0:
                    assert place[id(s)] < place[id(step)], ("order", name, step.eng, s.chain.name, s.eng)
                inc, total = s.inc, s.chain.count[s.group or s.eng]
                off = OFFSET[s.chain.name] - turns
                if isinstance(turn, int) and not 0 <= turn + off < NB:
                    continue
                key = (s.chain.name, s.group or s.eng)
                need[key] = max(need.get(key, -10**9), off * total * inc + (s.n + 1) * inc)
            for key, v in need.items():
                if known.get(key, -10**9) >= v:
                    continue
                known[key] = v
                ch_, grp = key
                total = chains[ch_].count[grp] * (16 if grp not in ENGINES else 1)
                e.wait_ge(sems[key], turn * total + v)
                if eng == "SP" or step.plain:
                    e.sem_inc(spare[eng], 1)
            ins = step.emit(e, batch) if eng == "SP" else step.emit(e)
            ins.then_inc(sems[name, step.group or step.eng], step.inc)

    with nc.Block() as block:
        on = {"PE": block.tensor, "DVE": block.vector, "ACT": block.scalar, "Pool": block.gpsimd, "SP": block.sync}
        for eng in ENGINES:
            @on[eng]
            def _(e, eng=eng):
                if eng == "DVE":
                    for q in range(2):
                        e.memset(S["dA"][:, 0, q, :, 0:1], 0.0).then_inc(ready, 1)
                        e.memset(S["dA"][:, 1, q, :, T - 1:T], 0.0).then_inc(ready, 1)
                    for om in (A["omL0"], A["omL1"], Tt["omL3"]):
                        e.memset(om[0:1, :], 1.0).then_inc(ready, 1)
                e.wait_ge(ready, 7)
                if eng == "ACT":
                    e.preload_act_table_set(ACT_SET)
                first, last = 2, NB - 2
                for turn in range(-2, first):
                    emit(e, eng, turn)
                with e.Fori(first, last) as i:
                    if eng == "ACT":
                        e.preload_act_table_set(ACT_SET)
                    emit(e, eng, i)
                for turn in range(last, NB + 1):
                    emit(e, eng, turn)
                if eng == "SP":
                    e.wait_ge(sems["T", "Tout"], 16 * NB)



def kernel(**inputs):
    import numpy as np
    import concourse.bacc as bacc
    from concourse.bass_utils import run_bass_kernel_spmd

    nc = bacc.Bacc("TRN2", target_bir_lowering=False, num_devices=1)
    arrays, aps = {}, {}
    for name, value in inputs.items():
        if name == "cond_1024":
            continue
        a = np.ascontiguousarray(value)
        arrays["in_" + name] = a
        aps[name] = nc.dram_tensor("in_" + name, a.shape, mybir.dt.from_np(a.dtype), kind="ExternalInput").ap()
    out = nc.dram_tensor("out_x", (NB, T, D), F32, kind="ExternalOutput").ap()
    bass_kernel(nc, aps, out)
    return run_bass_kernel_spmd(nc, [arrays], core_ids=[0]).results[0]["out_x"]
```

```python
from contextlib import ExitStack

import concourse.bass as bass
from concourse import mybir

F32 = mybir.dt.float32
I32 = mybir.dt.int32
BF16 = mybir.dt.bfloat16
ALU = mybir.AluOpType
ACT = mybir.ActivationFunctionType
AX = mybir.AxisListType.X

P = 128
NB, T, D = 32, 256, 256
E, N, R, CE = 512, 16, 64, 512
TT, KD, KE = T // P, D // P, E // P
H1, DH1, PADH = 16, 16, 32
NQ, N4, E32 = N // 4, 4, 32
EPS = 1e-5
NEG0, NEG1 = -1e30, -1e6
PARTS = 3
PCOLS = 18
OFFSET = {"A": 2, "C": 1, "S": 0, "P": 1, "T": -1}
SCAN_COST = 1.0
WINDOW = 0.2
ACT_SET = "natural_log_exp_and_others"


def bias_sections():
    at, sections = 0, {}
    for L in ("L0", "L1", "L3"):
        for m in "qkvo":
            n = H1 * PADH if L == "L1" and m in "qk" else D
            sections[L + m] = slice(at, at + n)
            at += n
    return sections, at


class Step:

    def __init__(self, chain, eng, n, emit, after, group, time):
        self.chain, self.eng, self.n, self.emit, self.after = chain, eng, n, emit, after
        self.group, self.inc, self.time, self.plain = group, 16 if group else 1, time, False


class Ago:

    def __init__(self, chain, name, turns=1):
        self.chain, self.name, self.turns = chain, name, turns


class Chain:

    TIMES = {"DVE": (0.07, 1 / 960), "ACT": (0.12, 1 / 1200), "Pool": (0.1, 1 / 450), "PE": (0.01, 1 / 600), "SP": (0.45, 0)}

    def __init__(self, name):
        self.name, self.steps, self.count, self.names = name, [], {}, {}

    def add(self, eng, emit, after, name=None, group=None, size=512):
        key = group or eng
        n = self.count.get(key, 0)
        self.count[key] = n + 1
        fixed, each = self.TIMES[eng]
        step = Step(self, eng, n, emit, after, group, fixed + each * size)
        self.steps.append(step)
        if name:
            assert name not in self.names, name
            self.names[name] = step
        return step


def rep(ap, dim, n):
    return ap.unsqueeze(dim).broadcast_to(list(ap.shape[:dim]) + [n] + list(ap.shape[dim:]))


def setup_weights(nc, W, keep, scr, sem):
    with ExitStack() as ctx:
        todo = []

        def sb(name, shape, dt=F32):
            return ctx.enter_context(nc.sbuf_tensor("set_" + name, shape, dt))

        ps = ctx.enter_context(nc.psum_tensor("set_ps", [P, 4, 512], F32))
        loads = []

        def load(dst, src):
            loads.append((dst, src))

        def step(eng, emit):
            todo.append((eng, emit))

        mm_bank = [0]

        def product(out, terms, shape, view=None, scale=None, plus=None):
            b = mm_bank[0] = (mm_bank[0] + 1) % 4
            region = ps[0:shape[0], b, 0:shape[1]]
            for n, (lhsT, rhs) in enumerate(terms):
                step("PE", lambda e, l=lhsT, r=rhs, n=n: e.matmul(region, l, r, start=n == 0, stop=n == len(terms) - 1))
            src = region if view is None else view(region)
            if plus is not None:
                step("DVE", lambda e: e.tensor_tensor(out, src, plus, ALU.add))
            elif scale is not None:
                step("DVE", lambda e: e.tensor_scalar(out, src, scale, None, ALU.mult))
            else:
                step("DVE", lambda e: e.tensor_copy(out, src))

        def transposed(out, blocks, rows, cols, view=None):
            b = mm_bank[0] = (mm_bank[0] + 1) % 4
            for n, blk in enumerate(blocks):
                step("PE", lambda e, n=n, blk=blk: e.transpose(ps[0:cols, b, n * rows:(n + 1) * rows], blk, keep["ident"][0:rows, 0:rows]))
            src = ps[0:cols, b, 0:len(blocks) * rows]
            step("DVE", lambda e: e.tensor_copy(out, src if view is None else view(src)))

        ident = keep["ident"]
        step("Pool", lambda e: e.memset(ident[:], 0.0))
        step("Pool", lambda e: e.affine_select(out=ident[:], in_=ident[:], compare_op=ALU.not_equal, fill=1.0, base=0,
                                               pattern=[[-1, P]], channel_multiplier=1))
        s4 = keep["sum4"]
        step("DVE", lambda e: e.tensor_tensor(s4[:], ident[:, 0:32], ident[:, 32:64], ALU.add))
        step("DVE", lambda e: e.tensor_tensor(s4[:], s4[:], ident[:, 64:96], ALU.add))
        step("DVE", lambda e: e.tensor_tensor(s4[:], s4[:], ident[:, 96:128], ALU.add))
        for name, dh in (("same16", 16), ("same32", 32)):
            m = keep[name]
            g = P // dh
            mv = m[:].rearrange("p (g d) -> p g d", g=g)
            step("Pool", lambda e, m=m: e.memset(m[:], 1.0))
            step("Pool", lambda e, mv=mv, g=g, dh=dh: e.affine_select(
                out=mv, in_=mv, compare_op=ALU.is_ge, fill=0.0, base=0, pattern=[[-dh, g], [0, dh]], channel_multiplier=1))
            step("Pool", lambda e, mv=mv, g=g, dh=dh: e.affine_select(
                out=mv, in_=mv, compare_op=ALU.is_ge, fill=0.0, base=dh - 1, pattern=[[dh, g], [0, dh]], channel_multiplier=-1))
        step("DVE", lambda e: e.memset(keep["ones"][:], 1.0))
        sections, nbias = bias_sections()
        allb = sb("allb", [1, nbias])

        def split(parts, src, back):
            for i in range(PARTS):
                step("DVE", lambda e, i=i: e.tensor_copy(parts(i), src))
                if i < PARTS - 1:
                    step("DVE", lambda e, i=i: e.tensor_copy(back, parts(i)))
                    step("DVE", lambda e: e.tensor_tensor(src, src, back, ALU.subtract))

        step("DVE", lambda e: e.memset(keep["eps"][:], EPS))
        ones32 = sb("ones32", [1, 32])
        step("DVE", lambda e: e.memset(ones32[:], 1.0))

        def col(name, src, k):
            t = sb(name, [P, k])
            load(t[:], src.rearrange("(k p) -> p k", p=P))
            return t

        def row(name, src):
            t = sb(name, [1, src.shape[0]])
            load(t[:], src.rearrange("(a n) -> a n", a=1))
            return t

        names = {
            "L0": ("norm_scale", "norm_bias", "Wq", "bq", "Wk", "bk", "Wv", "bv", "film_out_W", "film_out_b"),
            "L1": ("norm_w", "norm_b", "q_w", "q_b", "k_w", "k_b", "v_w", "v_b", "out_w", "out_b"),
            "L3": ("ln_w", "ln_b", "Wq", "bq", "Wk", "bk", "Wv", "bv", "W_out", "b_out"),
        }
        for L, ns in names.items():
            a = [W[f"{L}_cond_{n}"] for n in ns]
            g, b = col(L + "g", a[0], KD), col(L + "b", a[1], KD)
            load(keep[L + "wo"][:], a[8].rearrange("(k p) n -> p k n", p=P))
            load(allb[:, sections[L + "o"]], a[9].rearrange("(a n) -> a n", a=1))
            for m, (w, bias) in {"q": a[2:4], "k": a[4:6], "v": a[6:8]}.items():
                raw = sb(L + m + "raw", [P, KD, D])
                load(raw[:], w.rearrange("(k p) n -> p k n", p=P))
                wt, bt = keep[L + "w" + m], allb[:, sections[L + m]]
                padded = L == "L1" and m != "v"
                brow = row(L + m + "b", bias) if padded else bt
                if not padded:
                    load(bt, bias.rearrange("(a n) -> a n", a=1))
                if padded:
                    step("DVE", lambda e, wt=wt: e.memset(wt[:], 0.0))
                    step("DVE", lambda e, bt=bt: e.memset(bt[0:1, :], 0.0))
                for k in range(KD):
                    dst, src = wt[:, k, :], raw[:, k, :]
                    if padded:
                        dst = dst.rearrange("p (h d) -> p h d", d=PADH)[:, :, 0:DH1]
                        src = src.rearrange("p (h d) -> p h d", d=DH1)
                    step("DVE", lambda e, dst=dst, src=src, g=g, k=k: e.tensor_scalar(dst, src, g[:, k:k + 1], None, ALU.mult))
                dst, view, plus = bt[0:1, :], None, brow[:]
                if padded:
                    dst = dst.rearrange("p (h d) -> p h d", d=PADH)[:, :, 0:DH1]
                    view = lambda r: r.rearrange("p (h d) -> p h d", d=DH1)
                    plus = view(plus)
                product(dst, [(b[:, k:k + 1], raw[:, k, :]) for k in range(KD)], (1, D), view=view, plus=plus)
                if padded and m == "q":
                    spare = bt[0:1, :].rearrange("p (h d) -> p h d", d=PADH)[:, :, DH1:DH1 + 1]
                    step("DVE", lambda e, spare=spare: e.memset(spare, 1.0))
        step("DVE", lambda e: e.memset(keep["bias"][:], 1.0))
        where = keep["bias"][:, sections["L1k"]]
        step("DVE", lambda e: e.memset(where, 0.0))
        step("DVE", lambda e: e.memset(where.rearrange("p (h d) -> p h d", d=PADH)[:, :, DH1:DH1 + 1], 1.0))
        step("SP", lambda e: e.dma_start(scr["bias"].rearrange("(a n) -> a n", a=1), allb[:]))
        rowsb, back = sb("rowsb", [nbias // P, P]), sb("back", [nbias // P, P])
        bparts = sb("bparts", [nbias // P, PARTS, P], BF16)
        step("SP", lambda e: e.dma_start(rowsb[:], scr["bias"].rearrange("(a n) -> a n", n=P)))
        split(lambda i: bparts[:, i, :], rowsb[:], back[:])
        step("SP", lambda e: e.dma_start(scr["bparts"].rearrange("i (a n) -> a i n", n=P), bparts[:]))
        step("SP", lambda e: e.dma_start(keep["bias"][0:PARTS, :], scr["bparts"]))

        cond = sb("cond", [NB, CE])
        sig = sb("sig", [NB, CE])
        condT = sb("condT", [P, KE, NB])
        load(cond[:], W["cond_2048"])
        step("ACT", lambda e: e.activation(sig[:], cond[:], ACT.Exp, scale=-1.0))
        step("ACT", lambda e: e.activation(sig[:], sig[:], ACT.Ln, bias=1.0))
        step("ACT", lambda e: e.activation(sig[:], sig[:], ACT.Exp, scale=-1.0))
        step("DVE", lambda e: e.tensor_tensor(cond[:], cond[:], sig[:], ALU.mult))
        transposed(condT[:], [cond[:, k * P:(k + 1) * P] for k in range(KE)], NB, P, lambda r: r.rearrange("p (k b) -> p k b", k=KE))

        pc = sb("pcol", [P, NB, PCOLS])
        film = {"L0": ("film_emb_W", "film_emb_b", "film_norm_scale", "film_norm_bias", 4),
                "L1": ("emb_w", "emb_b", "sb_norm_w", "sb_norm_b", 8), "L3": ("W_emb", "b_emb", "ln2_w", "ln2_b", 14)}
        fw = sb("fw", [P, KE, 2 * D])
        so = sb("so", [P, 4, NB])
        serial = []
        for L, (w, b, s, t, at) in film.items():
            bc, sc, tc = col(L + "fb", W[f"{L}_cond_{b}"], 4), col(L + "fs", W[f"{L}_cond_{s}"], KD), col(L + "ft", W[f"{L}_cond_{t}"], KD)
            step("SP", lambda e, w=w, L=L: e.dma_start(fw[:], W[f"{L}_cond_{w}"].rearrange("(k p) n -> p k n", p=P)))
            for m in range(4):
                product(so[:, m, :], [(fw[:, k, m * P:(m + 1) * P], condT[:, k, :]) for k in range(KE)], (P, NB))
                step("DVE", lambda e, m=m, bc=bc: e.tensor_scalar(so[:, m, :], so[:, m, :], bc[:, m:m + 1], 1.0 if m < 2 else 0.0, ALU.add, ALU.add))
            for k in range(KD):
                a_, b_ = pc[:, :, at + k], pc[:, :, at + 2 + k]
                step("DVE", lambda e, a_=a_, k=k, sc=sc: e.tensor_scalar(a_, so[:, k, :], sc[:, k:k + 1], None, ALU.mult))
                step("DVE", lambda e, b_=b_, k=k, tc=tc: e.scalar_tensor_tensor(b_, so[:, k, :], tc[:, k:k + 1], so[:, 2 + k, :], ALU.mult, ALU.add))

        mi = sb("mi", [NB, T], I32)
        mf = sb("mf", [NB, 3, T])
        mr = sb("mr", [NB, 3, T])
        load(mi[:], W["mask_BxS_ik0"])
        load(mf[:, 1, :], W["mask_BxS_ff1"])
        load(mf[:, 2, :], W["mask_BxSx1_fk1"].rearrange("b t a -> b (t a)"))
        step("DVE", lambda e: e.tensor_copy(mf[:, 0, :], mi[:]))
        step("DVE", lambda e: e.tensor_scalar(mr[:, 0, :], mf[:, 0, :], 1.0, NEG0, ALU.is_equal, ALU.mult))
        step("DVE", lambda e: e.tensor_scalar(mf[:, 0, :], mf[:, 0, :], 1.0, None, ALU.not_equal))
        step("DVE", lambda e: e.tensor_scalar(mr[:, 1:3, :], mf[:, 1:3, :], -1.0, 1.0, ALU.mult, ALU.add))
        step("DVE", lambda e: e.tensor_scalar(mr[:, 1:3, :], mr[:, 1:3, :], NEG1, None, ALU.mult))
        mback, mparts = sb("mback", [NB, 3, T]), sb("mparts", [NB, 3, PARTS, T], BF16)
        split(lambda i: mparts[:, :, i, :], mr[:], mback[:])
        step("SP", lambda e: e.dma_start(scr["mask"], mparts[:]))
        for m, at in ((0, 0), (1, 2), (2, 12)):
            transposed(pc[:, :, at:at + 2].rearrange("p b t -> p t b"), [mf[:, m, tt * P:(tt + 1) * P] for tt in range(TT)], NB, P,
                       lambda r: r.rearrange("p (t b) -> p t b", t=TT))

        step("SP", lambda e: e.dma_start(scr["pcol"].rearrange("b p n -> p b n"), pc[:]))

        wada = sb("wada", [P, 6, CE])
        wadaT = sb("wadaT", [P, KE, 3 * D])
        load(wada[:], W["L2_cond_Wada"].rearrange("(m p) k -> p m k", p=P))
        bada = row("bada", W["L2_cond_bada"])
        for k in range(KE):
            for h in range(2):
                transposed(wadaT[:, k, h * 384:(h + 1) * 384], [wada[:, 3 * h + m, k * P:(k + 1) * P] for m in range(3)], P, P)
        ada = sb("ada", [NB, 3, D])
        mod = sb("mod", [NB, 4, D])
        rows = sb("rows", [NB, 3, D])
        for n, src in enumerate(("norm1_g", "norm1_b", "bf")):
            load(rows[:, n, :], W["L2_cond_" + src].partition_broadcast(NB))
        for m in range(3):
            product(ada[:, m, :], [(condT[:, k, :], wadaT[:, k, m * D:(m + 1) * D]) for k in range(KE)]
                    + [(ones32[:], bada[:, m * D:(m + 1) * D])], (NB, D))
        step("DVE", lambda e: e.tensor_scalar(ada[:, 1, :], ada[:, 1, :], 1.0, None, ALU.add))
        step("DVE", lambda e: e.tensor_tensor(mod[:, 0, :], rows[:, 0, :], ada[:, 1, :], ALU.mult))
        step("DVE", lambda e: e.tensor_tensor(mod[:, 1, :], rows[:, 1, :], ada[:, 1, :], ALU.mult))
        step("DVE", lambda e: e.tensor_tensor(mod[:, 1, :], mod[:, 1, :], ada[:, 0, :], ALU.add))
        step("DVE", lambda e: e.tensor_copy(mod[:, 2, :], ada[:, 2, :]))
        step("DVE", lambda e: e.tensor_tensor(mod[:, 3, :], rows[:, 2, :], ada[:, 2, :], ALU.mult))
        step("SP", lambda e: e.dma_start(scr["mod"], mod[:]))

        g2 = col("g2", W["L2_cond_norm2_g"], KD)
        b2row = sb("b2row", [P, D])
        load(b2row[:], W["L2_cond_norm2_b"].partition_broadcast(P))
        tmp = sb("tmp", [P, D])

        def times_b2(out, w, b):
            for c in range(KE):
                step("DVE", lambda e, c=c: e.tensor_tensor(tmp[:], w[:, c, :], b2row[:], ALU.mult))
                step("DVE", lambda e, c=c: e.tensor_reduce(out[:, c:c + 1], tmp[:], AX, ALU.add))
            step("DVE", lambda e: e.tensor_tensor(out[:], out[:], b[:], ALU.add))

        def load_w(name, src, k):
            t = sb(name, [src.shape[0] // k, k, src.shape[1]])
            load(t[:], src.rearrange("(k p) n -> p k n", k=k))
            return t

        wx = load_w("wx", W["L2_cond_Wx"], KE)
        wz = load_w("wz", W["L2_cond_Wz"], KE)
        for k in range(KD):
            transposed(keep["wx"][:, k, :], [wx[:, c, k * P:(k + 1) * P] for c in range(KE)], P, P)
            step("DVE", lambda e, k=k: e.tensor_scalar(keep["wx"][:, k, :], keep["wx"][:, k, :], g2[:, k:k + 1], None, ALU.mult))
        times_b2(keep["bx"], wx, col("bx", W["L2_cond_bx"], KE))
        bz = sb("bzc", [P, KE])
        times_b2(bz, wz, col("bz", W["L2_cond_bz"], KE))
        wf = load_w("wf", W["L2_cond_Wf"], KD)
        for c in range(KE):
            transposed(keep["wf"][:, c, :], [wf[:, k, c * P:(c + 1) * P] for k in range(KD)], P, P)
        wc = sb("wc", [P, KE, E])
        wcT = sb("wcT", [P, KE, E])
        wczT = sb("wczT", [P, KE, D])
        wd = sb("wd", [R + 2 * N, E])
        wdT = sb("wdT", [P, KE, R + 2 * N])
        wdt = sb("wdt", [P, KE, R])
        for s in range(2):
            q = str(s + 1)
            step("SP", lambda e, q=q: e.dma_start(wc[:], W["L2_cond_Wc" + q].rearrange("(k p) n -> p k n", p=P)))
            step("SP", lambda e, q=q: e.dma_start(wd[:], W["L2_cond_Wdbc" + q]))
            step("SP", lambda e, q=q: e.dma_start(wdt[:], W["L2_cond_Wdt" + q].rearrange("(k p) n -> p k n", p=P)))
            for k in range(KE):
                transposed(wcT[:, k, :], [wc[:, c, k * P:(k + 1) * P] for c in range(KE)], P, P)
            transposed(wdT[:], [wd[:, k * P:(k + 1) * P] for k in range(KE)], R + 2 * N, P, lambda r: r.rearrange("p (k r) -> p k r", k=KE))
            transposed(keep["wdt"][0:R, s, :], [wdt[:, c, :] for c in range(KE)], P, R)
            for k in range(KD):
                product(keep["wcz"][:, s, k, :], [(wz[:, c, k * P:(k + 1) * P], wcT[:, c, :]) for c in range(KE)], (P, E), scale=g2[:, k:k + 1])
            for f in range(KE):
                product(wczT[:, f, :], [(wcT[:, c, f * P:(f + 1) * P], wz[:, c, :]) for c in range(KE)], (P, D))
            bc = col("bc" + q, W["L2_cond_bc" + q], KE)
            for f in range(KE):
                product(keep["bcz"][:, s, f:f + 1], [(wcT[:, c, f * P:(f + 1) * P], bz[:, c:c + 1]) for c in range(KE)], (P, 1), plus=bc[:, f:f + 1])
            for k in range(KD):
                product(keep["wd"][:, s, k, :], [(wczT[:, f, k * P:(k + 1) * P], wdT[:, f, :]) for f in range(KE)], (P, R + 2 * N), scale=g2[:, k:k + 1])
            product(keep["bd"][:, s:s + 1], [(wdT[:, f, :], keep["bcz"][:, s, f:f + 1]) for f in range(KE)], (R + 2 * N, 1))
            load(keep["bdt"][:, s, :], W["L2_cond_bdt" + q].rearrange("(k p) -> p k", p=P))
            load(keep["dp"][:, s, :], W["L2_cond_Dp" + q].rearrange("(k p) -> p k", p=P))
            al = sb("al" + q, [P, KE, N])
            load(al[:], W["L2_cond_Alog" + q].rearrange("(k p) n -> p k n", p=P))
            for n4 in range(N4):
                for j in range(4):
                    dst = keep["acol"][n4 * E32:(n4 + 1) * E32, s].rearrange("p (c j) q -> p j c q", j=4)[:, j]
                    src = al[j * E32:(j + 1) * E32].rearrange("p c (q n) -> p n c q", n=N4)[:, n4]
                    step("DVE", lambda e, dst=dst, src=src: e.tensor_copy(dst, src))
        av = keep["acol"][:].rearrange("p s g q -> p (s g q)")
        step("ACT", lambda e: e.activation(av, av, ACT.Exp))
        step("DVE", lambda e: e.tensor_scalar(av, av, -1.0, None, ALU.mult))

        ms, ls = sem("set_step"), sem("set_load")
        block = ctx.enter_context(nc.Block())
        engines = {"PE": block.tensor, "DVE": block.vector, "ACT": block.scalar, "Pool": block.gpsimd, "SP": block.sync}
        total = [0]
        for _, (eng, _) in enumerate(todo):
            total[0] += 16 if eng == "SP" else 1

        for name, on in engines.items():
            @on
            def _(e, name=name):
                if name == "SP":
                    with nc.allow_non_contiguous_dma(reason="columns of bias vectors, once"):
                        for dst, src in loads:
                            e.dma_start(dst, src).then_inc(ls, 16)
                e.wait_ge(ls, 16 * len(loads))
                done, last = 0, None
                if name == "ACT":
                    e.preload_act_table_set(ACT_SET)
                for eng, emit in todo:
                    inc = 16 if eng == "SP" else 1
                    if eng == name:
                        if not (last == name == "PE"):
                            e.wait_ge(ms, done)
                        emit(e).then_inc(ms, inc)
                    done += inc
                    last = eng
                e.wait_ge(ms, done)


def layer_norm(ch, x, out, st, src_after, free_after, tag, eps):
    add = ch.add
    s = [add("DVE", lambda e, t=t: e.bn_stats(st["raw"][:, t, :], x(t)), src_after + free_after, size=D) for t in range(TT)]
    a = [add("DVE", lambda e, t=t: e.bn_aggr(st["mv"][:, t, :], st["raw"][:, t, :]), [s[t]], size=2) for t in range(TT)]
    for step in a:
        step.plain = True
    ln = add("ACT", lambda e: e.activation(st["rs"][:], st["mv"][:, :, 1], ACT.Ln, bias=eps), a, size=2)
    r = add("ACT", lambda e: e.activation(st["rs"][:], st["rs"][:], ACT.Exp, scale=-0.5), [ln], size=2)
    return [add("DVE", lambda e, t=t: e.tensor_scalar(out[:, t, :], x(t), st["mv"][:, t, 0:1], st["rs"][:, t:t + 1],
                                                      ALU.subtract, ALU.mult), [r, a[t]], size=D) for t in range(TT)]


def turned(ch, ident, src, bank, dst, after, bank_free, dst_free, eng="ACT"):
    t = None
    for c in range(2):
        for r in range(2):
            t = ch.add("PE", lambda e, c=c, r=r: e.transpose(bank[:, c * 256 + r * P:c * 256 + (r + 1) * P], src[:, r, c * P:(c + 1) * P], ident[:]),
                       after + bank_free, size=64)
    flat = dst[:].rearrange("p a b -> p (a b)")
    return t, copy(ch, eng, flat, bank[:, 0:512], [t] + dst_free)


def copy(ch, eng, dst, src, after):
    if eng == "ACT":
        return ch.add("ACT", lambda e: e.activation(dst, src, ACT.Copy), after)
    return ch.add(eng, lambda e: e.tensor_copy(dst, src), after)


def products(ch, groups, after, size=256):
    last = None
    for out, terms in groups:
        for n, (l, r) in enumerate(terms):
            last = ch.add("PE", lambda e, o=out, l=l, r=r, n=n, m=len(terms): e.matmul(o, l, r, start=n == 0, stop=n == m - 1), after,
                          size=size / 4 if l.dtype == BF16 else size)
    return last


def token_projection(bank, xT, w, bias, ones):
    return [(bank[:, t * D:(t + 1) * D], [(xT[:, k, t * P:(t + 1) * P], w[:, k, :]) for k in range(KD)] + [(ones[0:PARTS, 0:P], bias)]) for t in range(TT)]


def film_tail(ch, k, B, L, at, ysrc, y_after, gone, x, x_out, x_after):
    add = ch.add
    n2 = layer_norm(ch, ysrc, B["yh"], B["st"], y_after, gone, L, k["eps"][:])
    t = None
    bank = B["bank"][2]
    for c in range(2):
        for r in range(2):
            t = add("PE", lambda e, c=c, r=r: e.transpose(bank[:, c * 256 + r * P:c * 256 + (r + 1) * P], B["yh"][:, r, c * P:(c + 1) * P], k["ident"][:]),
                    n2 + gone, size=64)
    pc = B["pc"]
    hs = [add("DVE", lambda e, c=c: e.tensor_scalar(B["h"][:, c, :], bank[:, c * 256:(c + 1) * 256], pc[:, at + c:at + c + 1],
                                                    pc[:, at + 2 + c:at + 3 + c], ALU.mult, ALU.add), [t] + gone) for c in range(2)]
    es = [add("ACT", lambda e: e.activation(B["s"][:], B["h"][:], ACT.Exp, scale=-1.0), hs + gone)]
    l = add("ACT", lambda e: e.activation(B["s"][:], B["s"][:], ACT.Ln, bias=1.0), es)
    g = add("ACT", lambda e: e.activation(B["s"][:], B["s"][:], ACT.Exp, scale=-1.0), [l])
    m = add("Pool", lambda e: e.tensor_tensor(B["h"][:], B["h"][:], B["s"][:], ALU.mult), [g] + hs)
    o = products(ch, token_projection(B["bank"][3], B["h"], k[L + "wo"], k["bias"][0:PARTS, k["at"][L + "o"]], k["ones"]), [m] + gone)
    return add("DVE", lambda e: e.tensor_tensor(x_out[:].rearrange("p a b -> p (a b)"), B["bank"][3][:, 0:512],
                                                x[:].rearrange("p a b -> p (a b)"), ALU.add), [o] + x_after)


def linear_attention(ch, k, B, L, dh, mask_at, film_at, x, x_after, gate):
    add, bank, pc = ch.add, B["bank"], B["pc"]
    H = D // dh
    n1 = layer_norm(ch, lambda t: x[:, t, :], B["xh"], B["st"], x_after, gate, L, k["eps"][:])
    _, xT = turned(ch, k["ident"], B["xh"], bank[0], B["xT"], n1, gate, gate)
    q = products(ch, token_projection(bank[1], B["xT"], k[L + "wq"], k["bias"][0:PARTS, k["at"][L + "q"]], k["ones"]), [xT])
    kk = products(ch, [(bank[2][:, c * 256:(c + 1) * 256], [(k[L + "wk"][:, i, c * P:(c + 1) * P], B["xT"][:, i, :]) for i in range(KD)]
                        + [(k["bias"][:, k["at"][L + "k"]][:, c * P:(c + 1) * P], B["om" + L][:])]) for c in range(KD)], [xT] + gate)
    v = products(ch, token_projection(bank[3], B["xT"], k[L + "wv"], k["bias"][0:PARTS, k["at"][L + "v"]], k["ones"]), [xT] + gate)
    q3 = bank[1][:, 0:512].rearrange("p (h d) -> p h d", d=dh)
    qs = B["q"][:].rearrange("p t n -> p (t n)").rearrange("p (h d) -> p h d", d=dh)
    qm, qr = B["qm"][:, 0:TT * H], B["qr"][:, 0:TT * H]
    a = add("DVE", lambda e: e.tensor_reduce(qm, q3, AX, ALU.max), [q] + gate)
    b = add("DVE", lambda e: e.tensor_tensor(qs, q3, rep(qm, 2, dh), ALU.subtract), [a])
    km = add("DVE", lambda e: e.tensor_reduce(B["km"][:], bank[2][:, 0:512].rearrange("p (c t) -> p c t", c=KD), AX, ALU.max, negate=True), [kk])
    qe = add("ACT", lambda e: e.activation(B["q"][:], B["q"][:], ACT.Exp), [b])
    ke = [add("ACT", lambda e, c=c: e.activation(B["ke"][:, c, :], bank[2][:, c * 256:(c + 1) * 256], ACT.Exp, bias=B["km"][:, c:c + 1],
                                                 accum_out=B["ks"][:, c:c + 1]), [km] + gate) for c in range(KD)]
    vm = [add("ACT", lambda e, t=t: e.activation(B["v"][:, t, :], bank[3][:, t * D:(t + 1) * D], ACT.Copy, scale=pc[:, mask_at + t:mask_at + t + 1]), [v] + gate, size=340)
          for t in range(TT)]
    kr = add("DVE", lambda e: e.reciprocal(B["kr"][:], B["ks"][:]), ke)
    qsum = add("DVE", lambda e: e.tensor_reduce(qr, qs, AX, ALU.add), [qe])
    qrec = add("DVE", lambda e: e.reciprocal(qm, qr), [qsum])
    qn = add("Pool", lambda e: e.tensor_tensor(qs, qs, rep(qm, 2, dh), ALU.mult), [qrec])
    kn = ke
    if L == "L0":
        kn = [add("DVE", lambda e, c=c: e.tensor_scalar(B["ke"][:, c, :], B["ke"][:, c, :], B["kr"][:, c:c + 1], None, ALU.mult), ke + [kr], size=D)
              for c in range(KD)]
    lhs, rhs = (B["v"], B["xh"]) if L == "L0" else (B["xh"], B["v"])
    _, kt = turned(ch, k["ident"], B["ke"], bank[0], B["xh"], kn, [xT] + vm, [xT])
    at = products(ch, [(bank[2][:, c * P:(c + 1) * P], [(lhs[:, t, c * P:(c + 1) * P], rhs[:, t, c * P:(c + 1) * P]) for t in range(TT)])
                       for c in range(KD)], vm + [kt] + ke, size=P)
    bd = [add("DVE", lambda e, c=c: e.scalar_tensor_tensor(B["bd"][:, c, :], bank[2][:, c * P:(c + 1) * P],
                                                           1.0 if L == "L0" else B["kr"][:, c:c + 1],
                                                           k["same%d" % dh][:], ALU.mult, ALU.mult), [at, kr]) for c in range(KD)]
    _, qT = turned(ch, k["ident"], B["q"], bank[1], B["xT"], [qn], [b], [v])
    y = products(ch, [(bank[0][:, t * D + c * P:t * D + (c + 1) * P], [(B["xT"][:, c, t * P:(t + 1) * P], B["bd"][:, c, :])])
                      for t in range(TT) for c in range(KD)], [qT, kt] + bd, size=P)
    BB = dict(B, yh=B["q"], h=B["ke"], s=B["xh"])
    return film_tail(ch, k, BB, L, film_at, lambda t: bank[0][:, t * D:(t + 1) * D], [y], [qT] + bd + vm, x, x, [])


def softmax_attention(ch, k, B, x, x_after):
    add, bank, pc, L = ch.add, B["bank"], B["pc"], "L1"
    n1 = layer_norm(ch, lambda t: x[:, t, :], B["xh"], B["st"], x_after, [], L, k["eps"][:])
    _, xT = turned(ch, k["ident"], B["xh"], bank[0], B["xT"], n1, x_after, x_after)
    got = {}
    for m, bb in (("q", (1, 2)), ("k", (0, 3))):
        for half in range(2):
            bk = bank[bb[half]]
            p = products(ch, [(bk[:, c * 256:(c + 1) * 256], [(k[L + "w" + m][:, i, (2 * half + c) * P:(2 * half + c + 1) * P], B["xT"][:, i, :]) for i in range(KD)]
                               + [(k["bias"][0:PARTS, k["at"]["L1q"]][:, (2 * half + c) * P:(2 * half + c + 1) * P], k["ones"][0:PARTS, 0:T]) if m == "q" else
                                  (k["bias"][:, k["at"]["L1k"]][:, (2 * half + c) * P:(2 * half + c + 1) * P], B["omL1"][:])]) for c in range(2)], [xT] + x_after)
            got[m, half] = copy(ch, "ACT" if m == "q" else "DVE", B[m + "P"][:, 2 * half:2 * half + 2, :].rearrange("p a b -> p (a b)"), bk[:, 0:512], [p])
    v = products(ch, token_projection(bank[1], B["xT"], k[L + "wv"], k["bias"][0:PARTS, k["at"][L + "v"]], k["ones"]), [got["q", 0]])
    vm = [add("ACT", lambda e, t=t: e.activation(B["v"][:, t, :], bank[1][:, t * D:(t + 1) * D], ACT.Copy, scale=pc[:, 2 + t:3 + t]), [v], size=340)
          for t in range(TT)]
    proj = list(got.values()) + vm
    Eb, ETb = (B["q"], B["ke"]), (B["xh"], B["et"])
    sc, tb, yb = (bank[0], bank[1]), bank[2], bank[3]
    y_last, hist = None, {}

    def scores(h):
        i, c = h % 4, h // 4
        o = proj if h < 2 else hist[h - 2, "exp"]
        for t in range(TT):
            s = add("PE", lambda e, t=t: e.matmul(sc[h % 2][:, t * 256:(t + 1) * 256], B["qP"][32 * i:32 * i + DH1 + 1, c, t * P:(t + 1) * P],
                                                  B["kP"][32 * i:32 * i + DH1 + 1, c, :], start=True, stop=True, tile_position=(32 * i, 0)), o, size=T)
        free = hist[h - 2, "exp"] if h >= 2 else []
        m = add("DVE", lambda e: e.tensor_reduce(B["sm"][:, h % 2, :], sc[h % 2][:, 0:512].rearrange("p (t m) -> p t m", t=TT), AX, ALU.max, negate=True),
                [s] + free)
        free = [hist[h - 2, "turn"]] if h >= 2 else []
        hist[h, "exp"] = [add("ACT", lambda e, t=t: e.activation(Eb[h % 2][:, t, :], sc[h % 2][:, t * 256:(t + 1) * 256], ACT.Exp,
                                                                 bias=B["sm"][:, h % 2, t:t + 1], accum_out=B["ssum"][:, t, h:h + 1]), [m] + free + x_after)
                          for t in range(TT)]

    def turn_scores(h):
        free = [hist[h - 1, "et"]] if h else [got["q", 1]]
        t = None
        for mt in range(2):
            for nt in range(2):
                t = add("PE", lambda e, mt=mt, nt=nt: e.transpose(tb[:, mt * 256 + nt * P:mt * 256 + (nt + 1) * P], Eb[h % 2][:, nt, mt * P:(mt + 1) * P],
                                                                  k["ident"][:]), hist[h, "exp"] + free, size=64)
        hist[h, "turn"] = t
        free = [hist[h - 2, "y"]] if h >= 2 else [xT] + x_after
        hist[h, "et"] = copy(ch, "ACT", ETb[h % 2][:].rearrange("p a b -> p (a b)"), tb[:, 0:512], [t] + free)

    def values(h):
        hist[h, "y"] = products(ch, [(yb[:, t * D + h * DH1:t * D + (h + 1) * DH1],
                                      [(ETb[h % 2][:, mt, t * P:(t + 1) * P], B["v"][:, mt, h * DH1:(h + 1) * DH1]) for mt in range(2)])
                                     for t in range(TT)], [hist[h, "et"]] + proj, size=60)

    for h in range(H1 + 2):
        if h < H1:
            scores(h)
        if 1 <= h <= H1:
            turn_scores(h - 1)
        if h >= 2:
            values(h - 2)
    rec = add("DVE", lambda e: e.reciprocal(B["srec"][:], B["ssum"][:].rearrange("p t h -> p (t h)")), hist[H1 - 1, "exp"] + hist[H1 - 2, "exp"])
    yn = add("DVE", lambda e: e.tensor_tensor(B["qP"][:, 0:2, :].rearrange("p a b -> p (a b)").rearrange("p (g d) -> p g d", d=DH1),
                                              yb[:, 0:512].rearrange("p (g d) -> p g d", d=DH1), rep(B["srec"][:], 2, DH1), ALU.mult),
             [rec, hist[H1 - 1, "y"]])
    BB = dict(B, yh=B["ke"], h=B["xT"], s=B["xh"])
    return film_tail(ch, k, BB, L, 8, lambda t: B["qP"][:, t, :], [yn], [hist[H1 - 1, "y"], hist[H1 - 1, "et"]], x, x, [])


def chain_buffers(sb, name, shared=None):
    B = shared or {n: sb(f"{name}_{n}", [P, 2, 256]) for n in ("x", "xh", "xT", "q", "ke", "v")}
    if not shared:
        B["bd"] = sb(f"{name}_bd", [P, 2, P])
    B["st"] = {"raw": sb(f"{name}_raw", [P, 2, 6]), "mv": sb(f"{name}_mv", [P, 2, 2]), "rs": sb(f"{name}_rs", [P, 2])}
    B["qm"], B["qr"] = sb(f"{name}_qm", [P, 32]), sb(f"{name}_qr", [P, 32])
    for n in ("km", "ks", "kr"):
        B[n] = sb(f"{name}_{n}", [P, 2])
    B["pc"] = sb(f"{name}_pc", [P, PCOLS])
    return B


def bass_kernel(nc, W, out):
    with ExitStack() as ctx:
        def sb(name, shape, dt=F32):
            return ctx.enter_context(nc.sbuf_tensor(name, shape, dt))

        def sem(name):
            return ctx.enter_context(nc.semaphore(name))

        k = {}
        for L in ("L0", "L1", "L3"):
            for m in "qkvo":
                wide = H1 * PADH if L == "L1" and m in "qk" else D
                k[L + "w" + m] = sb(L + "w" + m, [P, KD, wide])
        k["wx"], k["wcz"], k["wd"] = sb("wx", [P, KD, E]), sb("wcz", [P, 2, KD, E]), sb("wd", [P, 2, KD, R + 2 * N])
        k["wdt"], k["wf"] = sb("wdt", [R, 2, E]), sb("wf", [P, KE, D])
        k["bx"], k["bcz"], k["bd"] = sb("bx", [P, KE]), sb("bcz", [P, 2, KE]), sb("bd", [R + 2 * N, 2])
        k["bdt"], k["dp"], k["acol"] = sb("bdt", [P, 2, KE]), sb("dp", [P, 2, KE]), sb("acol", [P, 2, E // E32, NQ])
        k["ident"], k["sum4"], k["same16"], k["same32"] = sb("ident", [P, P]), sb("sum4", [P, E32]), sb("same16", [P, P]), sb("same32", [P, P])
        k["ones"], k["eps"] = sb("ones", [PARTS, T], BF16), sb("eps", [P, 1])
        k["at"], nbias = bias_sections()
        k["bias"] = sb("bias", [2 * PARTS, nbias], BF16)

        def dram(name, shape, dt=F32):
            return nc.dram_tensor("scr_" + name, shape, dt, kind="Internal").ap()

        scr = {"pcol": dram("pcol", [NB, P, PCOLS]),
               "mask": dram("mask", [NB, 3, PARTS, T], BF16), "bias": dram("bias", [nbias]), "bparts": dram("bparts", [PARTS, nbias], BF16),
               "mod": dram("mod", [NB, 4, D]),
               "x2": dram("x2", [NB, P, 2, 256]),
               "res": dram("res", [NB, P, 2, 256]),
               "dd": dram("dd", [NB, 2, KE, P, 2 * T]),
               "bc": dram("bc", [NB, 2, 2 * N, T]),
               "wa": dram("wa", [NB, P, KE, 2, T]),
               "g": dram("g", [NB, P, KE, T])}
        setup_weights(nc, W, k, scr, sem)

        A, C = chain_buffers(sb, "A"), {}
        A["qP"], A["kP"] = sb("A_qP", [P, 4, 256]), sb("A_kP", [P, 4, 256])
        A["et"] = sb("A_et", [P, 2, 256])
        A["sm"], A["ssum"], A["srec"] = sb("A_sm", [P, 2, 2]), sb("A_ssum", [P, 2, H1]), sb("A_srec", [P, 2 * H1])
        A["omL0"], A["omL1"] = sb("omL0", [2 * PARTS, T], BF16), sb("omL1", [2 * PARTS, T], BF16)
        for n in ("x", "xh", "xs", "xT", "r"):
            C[n] = sb("C_" + n, [P, 2, 256])
        C["st"] = {"raw": sb("C_raw", [P, 2, 6]), "mv": sb("C_mv", [P, 2, 2]), "rs": sb("C_rs", [P, 2])}
        C["mod"], C["dd"], C["tmp"] = sb("C_mod", [P, 4, D]), sb("C_dd", [P, KE, 2, T]), sb("C_tmp", [P, KE, T])
        C["wa"], C["dbc"] = sb("C_wa", [P, KE, 2, T]), sb("C_dbc", [R + 2 * N, T])
        S = {"slot": sb("S_slot", [P, 2, 4, 2, T]), "bc": sb("S_bc", [P, 2, 2 * NQ, T]), "dA": sb("S_dA", [P, 2, 2, 4, T]),
             "X": sb("S_X", [P, 4, 4, T]), "wa": sb("S_wa", [P, KE, 2, T]), "g": sb("S_g", [P, KE, T])}
        v = C["dd"][:].rearrange("p c a t -> p c (a t)")
        two = lambda ap: ap.rearrange("p (a b) -> p a b", a=2)
        Tt = chain_buffers(sb, "T", {"x": C["x"], "xh": C["xh"], "xT": C["xT"], "q": two(v[:, 0]), "ke": two(v[:, 1]), "v": two(v[:, 2]),
                                     "bd": two(v[:, 3, 0:256]), "gate": v[:, 3, 256:512],
                                     "g": C["wa"][:, 0:2].rearrange("p c a t -> p (c a) t")})
        Tt["omL3"] = sb("omL3", [2 * PARTS, T], BF16)
        ps = ctx.enter_context(nc.psum_tensor("ps", [P, 8, 512], F32))
        A["bank"] = [ps[:, b, :] for b in (0, 1, 2, 3)]
        C["bank"] = [ps[:, b, :] for b in (4, 5, 6)]
        Tt["bank"] = [ps[:, b, :] for b in (4, 5, 6, 4)]
        S["bank"] = ps[:, 7, :]
        chains = {"A": Chain("A"), "C": Chain("C"), "S": Chain("S"), "P": Chain("P"), "T": Chain("T")}
        chain_a(chains["A"], k, A, W["x"], scr)
        chain_c(chains["C"], k, C, scr)
        chain_s(chains["S"], k, S, scr)
        chain_p(chains["P"], S, scr)
        chain_t(chains["T"], k, Tt, scr, out)
        run(nc, chains, S, A, Tt, sem)


def load(ch, dst, src, after, group, name=None):
    f = lambda v, b: v(b) if callable(v) else v
    return ch.add("SP", lambda e, b: e.dma_start(f(dst, b), f(src, b)), after, name=name, group=group)


def at_batch(ap, b):
    return ap[b] if isinstance(b, int) else ap[bass.ds(b, 1)].squeeze(0)


def chain_a(ch, k, B, x_in, scr):
    load(ch, B["x"][:], lambda b: at_batch(x_in, b).rearrange("(t p) d -> p t d", p=P), [], "Ain")
    load(ch, B["pc"][:, 0:12], lambda b: at_batch(scr["pcol"], b)[:, 0:12], [], "Ain")
    load(ch, B["omL0"][PARTS:2 * PARTS, :], lambda b: at_batch(scr["mask"], b)[0], [], "Ain")
    got = load(ch, B["omL1"][PARTS:2 * PARTS, :], lambda b: at_batch(scr["mask"], b)[1], [], "Ain")
    x1 = linear_attention(ch, k, B, "L0", D // 16, 0, 4, B["x"], [got], [])
    x2 = softmax_attention(ch, k, B, B["x"], [x1])
    load(ch, lambda b: at_batch(scr["x2"], b), B["x"][:], [x2], "Aout", name="stored")


def chain_c(ch, k, B, scr):
    add, bank, st = ch.add, B["bank"], B["st"]
    banks = [Ago("T", "last")]
    got = load(ch, B["x"][:], lambda b: at_batch(scr["x2"], b), [Ago("A", "stored")], "Cin")
    got = load(ch, B["mod"][:], lambda b: at_batch(scr["mod"], b).partition_broadcast(P), [], "Cin")
    x, xs, mod = B["x"], B["xs"], B["mod"]
    n1 = layer_norm(ch, lambda t: x[:, t, :], B["xh"], st, [got], [], "C1", k["eps"][:])
    mo = lambda n: rep(mod[:, n, :], 1, TT)
    m1 = add("Pool", lambda e: e.tensor_tensor(xs[:], B["xh"][:], mo(0), ALU.mult), n1)
    m2 = add("Pool", lambda e: e.tensor_tensor(xs[:], xs[:], mo(1), ALU.add), [m1])
    r1 = add("Pool", lambda e: e.tensor_tensor(B["r"][:], xs[:], mo(2), ALU.mult), [m2])
    r2 = add("Pool", lambda e: e.tensor_tensor(B["r"][:], B["r"][:], x[:], ALU.add), [r1], size=512)
    r3 = add("Pool", lambda e: e.tensor_tensor(B["r"][:], B["r"][:], mo(3), ALU.add), [r2], size=512)
    n2 = layer_norm(ch, lambda t: xs[:, t, :], B["xh"], st, [m2], n1, "C2", k["eps"][:])
    _, xT = turned(ch, k["ident"], B["xh"], bank[0], B["xT"], n2, banks, [])
    d_free, u_free, s_out = [xT], [], None
    for s in range(2):
        dbc_bank = bank[s][0:R + 2 * N, 0:T]
        p = products(ch, [(dbc_bank, [(k["wd"][:, s, i, :], B["xT"][:, i, :]) for i in range(KD)])], d_free + banks)
        dbc = add("ACT", lambda e, s=s, o=dbc_bank: e.activation(B["dbc"][:], o, ACT.Identity, bias=k["bd"][:, s:s + 1]), [p] + u_free)
        bcs = load(ch, lambda b, s=s: at_batch(scr["bc"], b)[s], B["dbc"][R:R + 2 * N, :], [dbc], "bc%d" % s, name="bc%d" % s)
        pres, us = [], []
        for h in range(2):
            pre, zb = bank[2], bank[1 - s]
            p = products(ch, [(pre[:, c * T:(c + 1) * T], [(k["wdt"][0:R, s, (2 * h + c) * P:(2 * h + c + 1) * P], B["dbc"][0:R, :])]) for c in range(2)],
                         [dbc] + pres + banks)
            for c in range(2):
                f, o = 2 * h + c, pre[:, c * T:(c + 1) * T]
                pres.append(add("ACT", lambda e, f=f, o=o, s=s: e.activation(B["dd"][:, f, 0, :], o, ACT.Identity, bias=k["bdt"][:, s, f:f + 1]),
                                [p] + u_free, size=340))
            p = products(ch, [(zb[:, c * T:(c + 1) * T], [(k["wcz"][:, s, i, (2 * h + c) * P:(2 * h + c + 1) * P], B["xT"][:, i, :]) for i in range(KD)])
                              for c in range(2)], [dbc, xT] + us + u_free + banks)
            for c in range(2):
                f, o = 2 * h + c, zb[:, c * T:(c + 1) * T]
                us.append(add("ACT", lambda e, f=f, o=o, s=s: e.activation(B["dd"][:, f, 1, :], o, ACT.Identity, bias=k["bcz"][:, s, f:f + 1]), [p] + u_free, size=340))
        ab = add("ACT", lambda e: e.activation(B["tmp"][:], B["dd"][:, :, 0, :], ACT.Abs), pres + u_free)
        e1 = add("ACT", lambda e: e.activation(B["tmp"][:], B["tmp"][:], ACT.Exp, scale=-1.0), [ab])
        e2 = add("ACT", lambda e: e.activation(B["tmp"][:], B["tmp"][:], ACT.Ln, bias=1.0), [e1])
        w = []
        for c in range(KE):
            if s == 0:
                w.append(add("DVE", lambda e, c=c: e.tensor_scalar(B["wa"][:, c, 0, :], B["dd"][:, c, 1, :], k["dp"][:, 0, c:c + 1], None, ALU.mult), us, size=T))
            else:
                w.append(add("DVE", lambda e, c=c: e.scalar_tensor_tensor(B["wa"][:, c, 0, :], B["dd"][:, c, 1, :], k["dp"][:, 1, c:c + 1],
                                                                          B["wa"][:, c, 0, :], ALU.mult, ALU.add), us + w0, size=T))
        w0 = w
        dl = add("DVE", lambda e: e.scalar_tensor_tensor(B["dd"][:, :, 0, :], B["dd"][:, :, 0, :], 0.0, B["tmp"][:], ALU.max, ALU.add), [e2])
        du = add("Pool", lambda e: e.tensor_tensor(B["dd"][:, :, 1, :], B["dd"][:, :, 1, :], B["dd"][:, :, 0, :], ALU.mult), [dl] + us + w)
        s_out = load(ch, lambda b, s=s: at_batch(scr["dd"], b)[s].rearrange("c p f -> p c f"), B["dd"][:].rearrange("p c a t -> p c (a t)"), [du], "dd%d" % s,
                     name="dd%d" % s)
        d_free, u_free = us, [s_out, du, bcs]
    hs = []
    for h in range(2):
        bk = bank[h]
        p = products(ch, [(bk[:, c * T:(c + 1) * T], [(k["wx"][:, i, (2 * h + c) * P:(2 * h + c + 1) * P], B["xT"][:, i, :]) for i in range(KD)]) for c in range(2)],
                     us + [dbc])
        for c in range(2):
            f, o = 2 * h + c, bk[:, c * T:(c + 1) * T]
            hs.append(add("DVE", lambda e, f=f, o=o: e.tensor_scalar(B["wa"][:, f, 1, :], o, k["bx"][:, f:f + 1], None, ALU.add), [p], size=T))
    e0 = add("ACT", lambda e: e.activation(B["tmp"][:], B["wa"][:, :, 1, :], ACT.Exp, scale=-1.0), hs + [dl])
    e1 = add("ACT", lambda e: e.activation(B["tmp"][:], B["tmp"][:], ACT.Ln, bias=1.0), [e0])
    e2 = add("ACT", lambda e: e.activation(B["tmp"][:], B["tmp"][:], ACT.Exp, scale=-1.0), [e1])
    m = add("Pool", lambda e: e.tensor_tensor(B["wa"][:, :, 1, :], B["wa"][:, :, 1, :], B["tmp"][:], ALU.mult), [e2] + hs, name="last")
    load(ch, lambda b: at_batch(scr["wa"], b), B["wa"][:], [m] + w0, "Cwa", name="wa")
    load(ch, lambda b: at_batch(scr["res"], b), B["r"][:], [r3], "Cres", name="res")


def load_slot(ch, B, scr, m, after):
    c, s = m // 2, m % 2
    src = lambda b: at_batch(scr["dd"], b)[s, c].rearrange("(j e) f -> e j f", e=E32)
    for n4 in range(N4):
        load(ch, B["slot"][n4 * E32:(n4 + 1) * E32, s].rearrange("p j a t -> p j (a t)"), src, after, "slots%d" % s,
             name="slot%d" % m if n4 == N4 - 1 else None)


def chain_p(ch, B, scr):
    for s in range(2):
        u = 27 + 4 * s
        last = [Ago("S", "exp%d" % u, 0), Ago("S", "bmul%d" % u, 0)]
        load_slot(ch, B, scr, s, last + [Ago("C", "dd%d" % s, 0)])
        for n4 in range(N4):
            src = lambda b, n4=n4, s=s: at_batch(scr["bc"], b)[s].rearrange("(q n) t -> n q t", n=N4)[n4].partition_broadcast(E32)
            load(ch, B["bc"][n4 * E32:(n4 + 1) * E32, s], src, last + [Ago("S", "cmul%d" % u, 0), Ago("C", "bc%d" % s, 0)],
                 "bc%d" % s, name="bc%d" % s if n4 == N4 - 1 else None)
    load(ch, B["wa"][:], lambda b: at_batch(scr["wa"], b), [Ago("S", "gate3", 0), Ago("C", "wa", 0)], "wa", name="wa")


def chain_s(ch, k, B, scr):
    add, n = ch.add, ch.names
    X, dA, bc = B["X"], B["dA"], B["bc"]
    UNITS, SLOTS = 4 * 2 * NQ, 8

    def unit(name, u):
        return n[name + str(u)] if u >= 0 else Ago("S", name + str(u + UNITS))

    def slot(m):
        return n["slot%d" % m] if m >= 2 else Ago("P", "slot%d" % m)

    def emit_exp(u):
        m, c, s, q = u // 4, u // 8, (u // 4) % 2, u % 4
        lo = 1 - s
        for j in range(4):
            add("ACT", lambda e, j=j: e.activation(dA[:, s, q % 2, j, lo:lo + T - 1], B["slot"][:, m % 2, j, 0, lo:lo + T - 1], ACT.Exp,
                                                   scale=k["acol"][:, s, 4 * c + j, q:q + 1]),
                [slot(m), unit("scan", u - 2 if q >= 2 else u - 6)], name="exp%d" % u if j == 3 else None, size=340)

    def emit_bmul(u):
        m, s, q = u // 4, (u // 4) % 2, u % 4
        add("DVE", lambda e: e.tensor_tensor(X[:, u % 4], B["slot"][:, m % 2, :, 1, :], rep(bc[:, s, q, :], 1, 4), ALU.mult),
            [slot(m), Ago("P", "bc%d" % s), unit("sum", u - 4)], name="bmul%d" % u, size=1024)

    def emit_scan(u):
        s, q = (u // 4) % 2, u % 4
        flat = lambda ap: ap.rearrange("p j t -> p (j t)")[:, ::-1] if s else ap.rearrange("p j t -> p (j t)")
        add("DVE", lambda e: e.tensor_tensor_scan(flat(X[:, u % 4]), flat(dA[:, s, q % 2]), flat(X[:, u % 4]), 0.0, ALU.mult, ALU.add),
            [n["exp%d" % u], n["bmul%d" % u]], name="scan%d" % u, size=SCAN_COST * 1024)

    def emit_cmul(u):
        s, q = (u // 4) % 2, u % 4
        add("Pool", lambda e: e.tensor_tensor(X[:, u % 4], X[:, u % 4], rep(bc[:, s, NQ + q, :], 1, 4), ALU.mult), [n["scan%d" % u]], name="cmul%d" % u, size=1024)

    def emit_sum(u):
        c, first, last = u // 8, u % 8 == 0, u % 8 == 7
        free = [n["gate%d" % (c - 1)] if c else Ago("S", "gate3")] if first else []
        for j in range(4):
            add("PE", lambda e, j=j: e.matmul(B["bank"][32 * j:32 * j + 32, (c % 2) * T:(c % 2 + 1) * T], k["sum4"][:], X[:, u % 4, j, :],
                                              start=first, stop=last, tile_position=(0, 32 * j), skip_group_check=True),
                [n["cmul%d" % u]] + free, name="sum%d" % u if j == 3 else None, size=70)
        if last:
            g = B["g"][:, c, :]
            a = add("DVE", lambda e: e.tensor_tensor(g, B["bank"][:, (c % 2) * T:(c % 2 + 1) * T], B["wa"][:, c, 0, :], ALU.add),
                    [n["sum%d" % u], Ago("P", "wa"), Ago("S", "g")], size=T)
            add("DVE", lambda e: e.tensor_tensor(g, g, B["wa"][:, c, 1, :], ALU.mult), [a], name="gate%d" % c, size=T)

    for v in range(UNITS + 2):
        if v < UNITS:
            emit_exp(v)
            emit_bmul(v)
        if 1 <= v <= UNITS:
            emit_scan(v - 1)
            if (v - 1) % 4 == 3 and (v - 1) // 4 + 2 < SLOTS:
                load_slot(ch, B, scr, (v - 1) // 4 + 2, [n["exp%d" % (v - 1)], n["bmul%d" % (v - 1)]])
            emit_cmul(v - 1)
        if 2 <= v <= UNITS + 1:
            emit_sum(v - 2)
    load(ch, lambda b: at_batch(scr["g"], b), B["g"][:], [n["gate3"]], "Sg", name="g")


def chain_t(ch, k, B, scr, out):
    load(ch, B["g"][:], lambda b: at_batch(scr["g"], b), [Ago("S", "g")], "Tin")
    load(ch, B["x"][:], lambda b: at_batch(scr["res"], b), [Ago("C", "res", 2)], "Tin")
    load(ch, B["gate"][:], lambda b: at_batch(scr["mod"], b)[2].partition_broadcast(P), [], "Tin")
    load(ch, B["omL3"][PARTS:2 * PARTS, :], lambda b: at_batch(scr["mask"], b)[2], [], "Tin")
    got = load(ch, B["pc"][:, 12:18], lambda b: at_batch(scr["pcol"], b)[:, 12:18], [], "Tin")
    bk = B["bank"][0]
    o = products(ch, [(bk[:, t * D:(t + 1) * D], [(B["g"][:, c, t * P:(t + 1) * P], k["wf"][:, c, :]) for c in range(KE)]) for t in range(TT)],
                 [got, Ago("C", "last", 0)])
    xf = B["x"]
    a = ch.add("DVE", lambda e: e.tensor_tensor(B["xh"][:], bk[:, 0:512].rearrange("p (t d) -> p t d", t=TT), rep(B["gate"][:], 1, TT), ALU.mult), [o, got])
    b_ = ch.add("DVE", lambda e: e.tensor_tensor(xf[:], xf[:], B["xh"][:], ALU.add), [a])
    last = linear_attention(ch, k, B, "L3", 32, 12, 14, xf, [b_], [])
    ch.names["last"] = last
    load(ch, lambda b: at_batch(out, b).rearrange("(t p) d -> p t d", p=P), xf[:], [last], "Tout")


ENGINES = ("PE", "DVE", "ACT", "Pool", "SP")
GATED = ("A", "C", "T")


def step_waits(chains):
    lasts = {c: list({s.group or s.eng: s for s in ch.steps}.values()) for c, ch in chains.items()}
    waits = {}
    for name, ch in chains.items():
        started = set()
        for step in ch.steps:
            w = [(a, 0) if isinstance(a, Step) else (chains[a.chain].names[a.name], a.turns) for a in step.after]
            if name in GATED and step.eng not in started:
                started.add(step.eng)
                w += [(s, 1) for s in lasts[name]]
                w += {"C": [(s, 1) for s in lasts["T"]], "T": [(s, 0) for s in lasts["C"]]}.get(name, [])
            waits[step] = w
    return waits


def alternate(chains, waits, rounds=4):
    tail, behind, after = {}, {}, {}
    for ch in chains.values():
        nxt = {}
        for step in reversed(ch.steps):
            behind[step] = nxt.get(step.eng)
            nxt[step.eng] = step
    for step, w in waits.items():
        for s, turns in w:
            if turns == 0:
                after.setdefault(s, []).append(step)

    def lag(step):
        return step.time + (2.2 if step.group else 0.25)

    def way(step):
        if step not in tail:
            later = after.get(step, []) + ([behind[step]] if behind[step] else [])
            tail[step] = lag(step) + max((way(x) for x in later), default=0.0)
        return tail[step]

    for ch in chains.values():
        for step in reversed(ch.steps):
            way(step)
    free, before, order = {}, {}, []
    for _ in range(rounds):
        done, order = {}, []
        queues = {(c, eng): [s for s in ch.steps if s.eng == eng] for c, ch in chains.items() for eng in ENGINES}
        at = {q: 0 for q in queues}
        while len(order) < sum(len(q) for q in queues.values()):
            heads = []
            for q, steps in queues.items():
                if at[q] == len(steps):
                    continue
                step = steps[at[q]]
                if any(turns == 0 and s not in done for s, turns in waits[step]):
                    continue
                start = max([free.get(step.eng, 0.0)] + [(done if turns == 0 else before).get(s, 0.0) for s, turns in waits[step]])
                heads.append((start, step, q))
            eng = min(heads, key=lambda h: h[0])[1].eng
            mine = [h for h in heads if h[1].eng == eng]
            first = min(h[0] for h in mine)
            start, step, q = max((h for h in mine if h[0] <= first + WINDOW), key=lambda h: tail[h[1]])
            at[q] += 1
            free[eng] = start + step.time
            done[step] = start + lag(step)
            order.append(step)
        before = done
    return order


def run(nc, chains, S, A, Tt, sem):
    waits = step_waits(chains)
    order = alternate(chains, waits)
    place = {s: n for n, s in enumerate(order)}
    keys = {(c, key) for c, ch in chains.items() for key in ch.count}
    sems = {key: sem("s_%s_%s" % key) for key in sorted(keys)}
    ready = sem("s_ready")
    spare = {eng: sem("s_spare_" + eng) for eng in ENGINES}

    def emit(e, eng, turn):
        known = {}
        for step in order:
            name = step.chain.name
            if step.eng != eng:
                continue
            batch = turn + OFFSET[name]
            if isinstance(turn, int) and not 0 <= batch < NB:
                continue
            need = {}
            for s, turns in waits[step]:
                if turns == 0:
                    assert place[s] < place[step], ("order", name, step.eng, s.chain.name, s.eng)
                inc, total = s.inc, s.chain.count[s.group or s.eng]
                off = OFFSET[s.chain.name] - turns
                if isinstance(turn, int) and not 0 <= turn + off < NB:
                    continue
                key = (s.chain.name, s.group or s.eng)
                need[key] = max(need.get(key, -10**9), off * total * inc + (s.n + 1) * inc)
            for key, v in need.items():
                if known.get(key, -10**9) >= v:
                    continue
                known[key] = v
                ch_, grp = key
                total = chains[ch_].count[grp] * (16 if grp not in ENGINES else 1)
                e.wait_ge(sems[key], turn * total + v)
                if eng == "SP" or step.plain:
                    e.sem_inc(spare[eng], 1)
            ins = step.emit(e, batch) if eng == "SP" else step.emit(e)
            ins.then_inc(sems[name, step.group or step.eng], step.inc)

    with nc.Block() as block:
        on = {"PE": block.tensor, "DVE": block.vector, "ACT": block.scalar, "Pool": block.gpsimd, "SP": block.sync}
        for eng in ENGINES:
            @on[eng]
            def _(e, eng=eng):
                if eng == "DVE":
                    for q in range(2):
                        e.memset(S["dA"][:, 0, q, :, 0:1], 0.0).then_inc(ready, 1)
                        e.memset(S["dA"][:, 1, q, :, T - 1:T], 0.0).then_inc(ready, 1)
                    for om in (A["omL0"], A["omL1"], Tt["omL3"]):
                        e.memset(om[0:PARTS, :], 1.0).then_inc(ready, 1)
                e.wait_ge(ready, 7)
                if eng == "ACT":
                    e.preload_act_table_set(ACT_SET)
                first, last = 2, NB - 2
                for turn in range(-2, first):
                    emit(e, eng, turn)
                with e.Fori(first, last) as i:
                    if eng == "ACT":
                        e.preload_act_table_set(ACT_SET)
                    emit(e, eng, i)
                for turn in range(last, NB + 1):
                    emit(e, eng, turn)
                if eng == "SP":
                    e.wait_ge(sems["T", "Tout"], 16 * NB)



def kernel(**inputs):
    import numpy as np
    import concourse.bacc as bacc
    from concourse.bass_utils import run_bass_kernel_spmd

    nc = bacc.Bacc("TRN2", target_bir_lowering=False, num_devices=1)
    arrays, aps = {}, {}
    for name, value in inputs.items():
        if name == "cond_1024":
            continue
        a = np.ascontiguousarray(value)
        arrays["in_" + name] = a
        aps[name] = nc.dram_tensor("in_" + name, a.shape, mybir.dt.from_np(a.dtype), kind="ExternalInput").ap()
    out = nc.dram_tensor("out_x", (NB, T, D), F32, kind="ExternalOutput").ap()
    bass_kernel(nc, aps, out)
    return run_bass_kernel_spmd(nc, [arrays], core_ids=[0]).results[0]["out_x"]
```

```python
from contextlib import ExitStack

import concourse.bass as bass
from concourse import mybir

F32 = mybir.dt.float32
I32 = mybir.dt.int32
BF16 = mybir.dt.bfloat16
ALU = mybir.AluOpType
ACT = mybir.ActivationFunctionType
AX = mybir.AxisListType.X

P = 128
NB, T, D = 32, 256, 256
E, N, R, CE = 512, 16, 64, 512
TT, KD, KE = T // P, D // P, E // P
H1, DH1, PADH = 16, 16, 32
NQ, N4, E32 = N // 4, 4, 32
EPS = 1e-5
NEG0, NEG1 = -1e30, -1e6
PARTS = 3
QH = 4
PCOLS = 18
OFFSET = {"A": 2, "C": 1, "S": 0, "P": 1, "T": -1, "PA": 3, "PT": -1}
WINDOW = 0.0
PE_TICK = 3.413
STREAMS = ("start", "attention", "conditions", "scans")
ACT_SET = "natural_log_exp_and_others"


def bias_sections():
    at, sections = 0, {}
    for L in ("L0", "L1", "L3"):
        for m in "qkvo":
            n = H1 * PADH if L == "L1" and m in "qk" else D
            sections[L + m] = slice(at, at + n)
            at += n
    return sections, at


class Step:

    def __init__(self, chain, eng, n, emit, after, group, time):
        self.chain, self.eng, self.n, self.emit, self.after = chain, eng, n, emit, after
        self.group, self.inc, self.time, self.plain = group, 16 if group else 1, time, False


class Ago:

    def __init__(self, chain, name, turns=1):
        self.chain, self.name, self.turns = chain, name, turns


class Chain:

    TIMES = {"DVE": (0.07, 1 / 960), "ACT": (0.12, 1 / 1200), "Pool": (0.1, 1 / 450), "PE": (0.01, 1 / 600), "SP": (0.45, 0)}

    def __init__(self, name):
        self.name, self.steps, self.count, self.names = name, [], {}, {}

    def add(self, eng, emit, after, name=None, group=None, size=512):
        key = group or eng
        n = self.count.get(key, 0)
        self.count[key] = n + 1
        fixed, each = self.TIMES[eng]
        step = Step(self, eng, n, emit, after, group, fixed + each * size)
        self.steps.append(step)
        if name:
            assert name not in self.names, name
            self.names[name] = step
        return step


def rep(ap, dim, n):
    return ap.unsqueeze(dim).broadcast_to(list(ap.shape[:dim]) + [n] + list(ap.shape[dim:]))


def setup_weights(nc, W, keep, scr, sem):
    with ExitStack() as ctx:
        todo, stream = [], ["start"]

        def sb(name, shape, dt=F32):
            return ctx.enter_context(nc.sbuf_tensor("set_" + name, shape, dt))

        ps = ctx.enter_context(nc.psum_tensor("set_ps", [P, 2 * len(STREAMS), 512], F32))
        loads = []

        def load(dst, src):
            loads.append((dst, src))

        def step(eng, emit):
            todo.append((stream[0], eng, emit))

        mm_bank = {name: 0 for name in STREAMS}

        def next_bank():
            n = mm_bank[stream[0]] = 1 - mm_bank[stream[0]]
            return 2 * STREAMS.index(stream[0]) + n

        def product(out, terms, shape, view=None, scale=None, plus=None):
            b = next_bank()
            region = ps[0:shape[0], b, 0:shape[1]]
            for n, (lhsT, rhs) in enumerate(terms):
                step("PE", lambda e, l=lhsT, r=rhs, n=n: e.matmul(region, l, r, start=n == 0, stop=n == len(terms) - 1))
            src = region if view is None else view(region)
            if plus is not None:
                step("DVE", lambda e: e.tensor_tensor(out, src, plus, ALU.add))
            elif scale is not None:
                step("DVE", lambda e: e.tensor_scalar(out, src, scale, None, ALU.mult))
            else:
                step("DVE", lambda e: e.tensor_copy(out, src))

        def transposed(out, blocks, rows, cols, view=None):
            b = next_bank()
            for n, blk in enumerate(blocks):
                step("PE", lambda e, n=n, blk=blk: e.transpose(ps[0:cols, b, n * rows:(n + 1) * rows], blk, keep["ident"][0:rows, 0:rows]))
            src = ps[0:cols, b, 0:len(blocks) * rows]
            step("DVE", lambda e: e.tensor_copy(out, src if view is None else view(src)))

        ident = keep["ident"]
        step("Pool", lambda e: e.memset(ident[:], 0.0))
        step("Pool", lambda e: e.affine_select(out=ident[:], in_=ident[:], compare_op=ALU.not_equal, fill=1.0, base=0,
                                               pattern=[[-1, P]], channel_multiplier=1))
        s4 = keep["sum4"]
        step("DVE", lambda e: e.tensor_tensor(s4[:], ident[:, 0:32], ident[:, 32:64], ALU.add))
        step("DVE", lambda e: e.tensor_tensor(s4[:], s4[:], ident[:, 64:96], ALU.add))
        step("DVE", lambda e: e.tensor_tensor(s4[:], s4[:], ident[:, 96:128], ALU.add))
        for name, dh in (("same16", 16), ("same32", 32)):
            m = keep[name]
            g = P // dh
            mv = m[:].rearrange("p (g d) -> p g d", g=g)
            step("Pool", lambda e, m=m: e.memset(m[:], 1.0))
            step("Pool", lambda e, mv=mv, g=g, dh=dh: e.affine_select(
                out=mv, in_=mv, compare_op=ALU.is_ge, fill=0.0, base=0, pattern=[[-dh, g], [0, dh]], channel_multiplier=1))
            step("Pool", lambda e, mv=mv, g=g, dh=dh: e.affine_select(
                out=mv, in_=mv, compare_op=ALU.is_ge, fill=0.0, base=dh - 1, pattern=[[dh, g], [0, dh]], channel_multiplier=-1))
        step("DVE", lambda e: e.memset(keep["ones"][:], 1.0))
        sections, nbias = bias_sections()
        allb = sb("allb", [1, nbias])

        def split(parts, src, back):
            for i in range(PARTS):
                step("DVE", lambda e, i=i: e.tensor_copy(parts(i), src))
                if i < PARTS - 1:
                    step("DVE", lambda e, i=i: e.tensor_copy(back, parts(i)))
                    step("DVE", lambda e: e.tensor_tensor(src, src, back, ALU.subtract))

        step("DVE", lambda e: e.memset(keep["eps"][:], EPS))
        ones32 = sb("ones32", [1, 32])
        step("DVE", lambda e: e.memset(ones32[:], 1.0))

        def col(name, src, k):
            t = sb(name, [P, k])
            load(t[:], src.rearrange("(k p) -> p k", p=P))
            return t

        def row(name, src):
            t = sb(name, [1, src.shape[0]])
            load(t[:], src.rearrange("(a n) -> a n", a=1))
            return t

        stream[0] = "attention"
        names = {
            "L0": ("norm_scale", "norm_bias", "Wq", "bq", "Wk", "bk", "Wv", "bv", "film_out_W", "film_out_b"),
            "L1": ("norm_w", "norm_b", "q_w", "q_b", "k_w", "k_b", "v_w", "v_b", "out_w", "out_b"),
            "L3": ("ln_w", "ln_b", "Wq", "bq", "Wk", "bk", "Wv", "bv", "W_out", "b_out"),
        }
        for L, ns in names.items():
            a = [W[f"{L}_cond_{n}"] for n in ns]
            g, b = col(L + "g", a[0], KD), col(L + "b", a[1], KD)
            load(keep[L + "wo"][:], a[8].rearrange("(k p) n -> p k n", p=P))
            load(allb[:, sections[L + "o"]], a[9].rearrange("(a n) -> a n", a=1))
            for m, (w, bias) in {"q": a[2:4], "k": a[4:6], "v": a[6:8]}.items():
                raw = sb(L + m + "raw", [P, KD, D])
                load(raw[:], w.rearrange("(k p) n -> p k n", p=P))
                wt, bt = keep[L + "w" + m], allb[:, sections[L + m]]
                padded = L == "L1" and m != "v"
                brow = row(L + m + "b", bias) if padded else bt
                if not padded:
                    load(bt, bias.rearrange("(a n) -> a n", a=1))
                if padded:
                    step("DVE", lambda e, wt=wt: e.memset(wt[:], 0.0))
                    step("DVE", lambda e, bt=bt: e.memset(bt[0:1, :], 0.0))
                for k in range(KD):
                    dst, src = wt[:, k, :], raw[:, k, :]
                    if padded:
                        dst = dst.rearrange("p (h d) -> p h d", d=PADH)[:, :, 0:DH1]
                        src = src.rearrange("p (h d) -> p h d", d=DH1)
                    step("DVE", lambda e, dst=dst, src=src, g=g, k=k: e.tensor_scalar(dst, src, g[:, k:k + 1], None, ALU.mult))
                dst, view, plus = bt[0:1, :], None, brow[:]
                if padded:
                    dst = dst.rearrange("p (h d) -> p h d", d=PADH)[:, :, 0:DH1]
                    view = lambda r: r.rearrange("p (h d) -> p h d", d=DH1)
                    plus = view(plus)
                product(dst, [(b[:, k:k + 1], raw[:, k, :]) for k in range(KD)], (1, D), view=view, plus=plus)
                if padded and m == "q":
                    spare = bt[0:1, :].rearrange("p (h d) -> p h d", d=PADH)[:, :, DH1:DH1 + 1]
                    step("DVE", lambda e, spare=spare: e.memset(spare, 1.0))
        step("DVE", lambda e: e.memset(keep["bias"][:], 1.0))
        where = keep["bias"][:, sections["L1k"]]
        step("DVE", lambda e: e.memset(where, 0.0))
        step("DVE", lambda e: e.memset(where.rearrange("p (h d) -> p h d", d=PADH)[:, :, DH1:DH1 + 1], 1.0))
        step("SP", lambda e: e.dma_start(scr["bias"].rearrange("(a n) -> a n", a=1), allb[:]))
        rowsb, back = sb("rowsb", [nbias // P, P]), sb("back", [nbias // P, P])
        bparts = sb("bparts", [nbias // P, PARTS, P], BF16)
        step("SP", lambda e: e.dma_start(rowsb[:], scr["bias"].rearrange("(a n) -> a n", n=P)))
        split(lambda i: bparts[:, i, :], rowsb[:], back[:])
        step("SP", lambda e: e.dma_start(scr["bparts"].rearrange("i (a n) -> a i n", n=P), bparts[:]))
        step("SP", lambda e: e.dma_start(keep["bias"][0:PARTS, :], scr["bparts"]))

        stream[0] = "conditions"
        cond = sb("cond", [NB, CE])
        sig = sb("sig", [NB, CE])
        condT = sb("condT", [P, KE, NB])
        load(cond[:], W["cond_2048"])
        step("ACT", lambda e: e.activation(sig[:], cond[:], ACT.Exp, scale=-1.0))
        step("ACT", lambda e: e.activation(sig[:], sig[:], ACT.Ln, bias=1.0))
        step("ACT", lambda e: e.activation(sig[:], sig[:], ACT.Exp, scale=-1.0))
        step("DVE", lambda e: e.tensor_tensor(cond[:], cond[:], sig[:], ALU.mult))
        transposed(condT[:], [cond[:, k * P:(k + 1) * P] for k in range(KE)], NB, P, lambda r: r.rearrange("p (k b) -> p k b", k=KE))

        pc = sb("pcol", [P, NB, PCOLS])
        film = {"L0": ("film_emb_W", "film_emb_b", "film_norm_scale", "film_norm_bias", 4),
                "L1": ("emb_w", "emb_b", "sb_norm_w", "sb_norm_b", 8), "L3": ("W_emb", "b_emb", "ln2_w", "ln2_b", 14)}
        fw = sb("fw", [P, KE, 2 * D])
        so = sb("so", [P, 4, NB])
        for L, (w, b, s, t, at) in film.items():
            bc, sc, tc = col(L + "fb", W[f"{L}_cond_{b}"], 4), col(L + "fs", W[f"{L}_cond_{s}"], KD), col(L + "ft", W[f"{L}_cond_{t}"], KD)
            step("SP", lambda e, w=w, L=L: e.dma_start(fw[:], W[f"{L}_cond_{w}"].rearrange("(k p) n -> p k n", p=P)))
            for m in range(4):
                product(so[:, m, :], [(fw[:, k, m * P:(m + 1) * P], condT[:, k, :]) for k in range(KE)], (P, NB))
                step("DVE", lambda e, m=m, bc=bc: e.tensor_scalar(so[:, m, :], so[:, m, :], bc[:, m:m + 1], 1.0 if m < 2 else 0.0, ALU.add, ALU.add))
            for k in range(KD):
                a_, b_ = pc[:, :, at + k], pc[:, :, at + 2 + k]
                step("DVE", lambda e, a_=a_, k=k, sc=sc: e.tensor_scalar(a_, so[:, k, :], sc[:, k:k + 1], None, ALU.mult))
                step("DVE", lambda e, b_=b_, k=k, tc=tc: e.scalar_tensor_tensor(b_, so[:, k, :], tc[:, k:k + 1], so[:, 2 + k, :], ALU.mult, ALU.add))

        mi = sb("mi", [NB, T], I32)
        mf = sb("mf", [NB, 3, T])
        mr = sb("mr", [NB, 3, T])
        load(mi[:], W["mask_BxS_ik0"])
        load(mf[:, 1, :], W["mask_BxS_ff1"])
        load(mf[:, 2, :], W["mask_BxSx1_fk1"].rearrange("b t a -> b (t a)"))
        step("DVE", lambda e: e.tensor_copy(mf[:, 0, :], mi[:]))
        step("DVE", lambda e: e.tensor_scalar(mr[:, 0, :], mf[:, 0, :], 1.0, NEG0, ALU.is_equal, ALU.mult))
        step("DVE", lambda e: e.tensor_scalar(mf[:, 0, :], mf[:, 0, :], 1.0, None, ALU.not_equal))
        step("DVE", lambda e: e.tensor_scalar(mr[:, 1:3, :], mf[:, 1:3, :], -1.0, 1.0, ALU.mult, ALU.add))
        step("DVE", lambda e: e.tensor_scalar(mr[:, 1:3, :], mr[:, 1:3, :], NEG1, None, ALU.mult))
        mback, mparts = sb("mback", [NB, 3, T]), sb("mparts", [NB, 3, PARTS, T], BF16)
        split(lambda i: mparts[:, :, i, :], mr[:], mback[:])
        step("SP", lambda e: e.dma_start(scr["mask"], mparts[:]))
        for m, at in ((0, 0), (1, 2), (2, 12)):
            transposed(pc[:, :, at:at + 2].rearrange("p b t -> p t b"), [mf[:, m, tt * P:(tt + 1) * P] for tt in range(TT)], NB, P,
                       lambda r: r.rearrange("p (t b) -> p t b", t=TT))

        step("SP", lambda e: e.dma_start(scr["pcol"].rearrange("b p n -> p b n"), pc[:]))

        wada = sb("wada", [P, 6, CE])
        wadaT = sb("wadaT", [P, KE, 3 * D])
        load(wada[:], W["L2_cond_Wada"].rearrange("(m p) k -> p m k", p=P))
        bada = row("bada", W["L2_cond_bada"])
        for k in range(KE):
            for h in range(2):
                transposed(wadaT[:, k, h * 384:(h + 1) * 384], [wada[:, 3 * h + m, k * P:(k + 1) * P] for m in range(3)], P, P)
        ada = sb("ada", [NB, 3, D])
        mod = sb("mod", [NB, 4, D])
        rows = sb("rows", [NB, 3, D])
        for n, src in enumerate(("norm1_g", "norm1_b", "bf")):
            load(rows[:, n, :], W["L2_cond_" + src].partition_broadcast(NB))
        for m in range(3):
            product(ada[:, m, :], [(condT[:, k, :], wadaT[:, k, m * D:(m + 1) * D]) for k in range(KE)]
                    + [(ones32[:], bada[:, m * D:(m + 1) * D])], (NB, D))
        step("DVE", lambda e: e.tensor_scalar(ada[:, 1, :], ada[:, 1, :], 1.0, None, ALU.add))
        step("DVE", lambda e: e.tensor_tensor(mod[:, 0, :], rows[:, 0, :], ada[:, 1, :], ALU.mult))
        step("DVE", lambda e: e.tensor_tensor(mod[:, 1, :], rows[:, 1, :], ada[:, 1, :], ALU.mult))
        step("DVE", lambda e: e.tensor_tensor(mod[:, 1, :], mod[:, 1, :], ada[:, 0, :], ALU.add))
        step("DVE", lambda e: e.tensor_copy(mod[:, 2, :], ada[:, 2, :]))
        step("DVE", lambda e: e.tensor_tensor(mod[:, 3, :], rows[:, 2, :], ada[:, 2, :], ALU.mult))
        step("SP", lambda e: e.dma_start(scr["mod"], mod[:]))

        stream[0] = "scans"
        g2 = col("g2", W["L2_cond_norm2_g"], KD)
        b2row = sb("b2row", [P, D])
        load(b2row[:], W["L2_cond_norm2_b"].partition_broadcast(P))

        def times_b2(out, w, b, tmp):
            for c in range(KE):
                step("DVE", lambda e, c=c: e.tensor_tensor(tmp[:], w[:, c, :], b2row[:], ALU.mult))
                step("DVE", lambda e, c=c: e.tensor_reduce(out[:, c:c + 1], tmp[:], AX, ALU.add))
            step("DVE", lambda e: e.tensor_tensor(out[:], out[:], b[:], ALU.add))

        def load_w(name, src, k):
            t = sb(name, [src.shape[0] // k, k, src.shape[1]])
            load(t[:], src.rearrange("(k p) n -> p k n", k=k))
            return t

        wx = load_w("wx", W["L2_cond_Wx"], KE)
        wz = load_w("wz", W["L2_cond_Wz"], KE)
        stream[0] = "attention"
        for k in range(KD):
            transposed(keep["wx"][:, k, :], [wx[:, c, k * P:(k + 1) * P] for c in range(KE)], P, P)
            step("DVE", lambda e, k=k: e.tensor_scalar(keep["wx"][:, k, :], keep["wx"][:, k, :], g2[:, k:k + 1], None, ALU.mult))
        times_b2(keep["bx"], wx, col("bx", W["L2_cond_bx"], KE), sb("tmpx", [P, D]))
        bz = sb("bzc", [P, KE])
        wf = load_w("wf", W["L2_cond_Wf"], KD)
        for c in range(KE):
            transposed(keep["wf"][:, c, :], [wf[:, k, c * P:(c + 1) * P] for k in range(KD)], P, P)
        stream[0] = "scans"
        times_b2(bz, wz, col("bz", W["L2_cond_bz"], KE), sb("tmpz", [P, D]))
        wc = sb("wc", [P, KE, E])
        wcT = sb("wcT", [P, KE, E])
        wczT = sb("wczT", [P, KE, D])
        wd = sb("wd", [R + 2 * N, E])
        wdT = sb("wdT", [P, KE, R + 2 * N])
        wdt = sb("wdt", [P, KE, R])
        for s in range(2):
            q = str(s + 1)
            step("SP", lambda e, q=q: e.dma_start(wc[:], W["L2_cond_Wc" + q].rearrange("(k p) n -> p k n", p=P)))
            step("SP", lambda e, q=q: e.dma_start(wd[:], W["L2_cond_Wdbc" + q]))
            step("SP", lambda e, q=q: e.dma_start(wdt[:], W["L2_cond_Wdt" + q].rearrange("(k p) n -> p k n", p=P)))
            for k in range(KE):
                transposed(wcT[:, k, :], [wc[:, c, k * P:(k + 1) * P] for c in range(KE)], P, P)
            transposed(wdT[:], [wd[:, k * P:(k + 1) * P] for k in range(KE)], R + 2 * N, P, lambda r: r.rearrange("p (k r) -> p k r", k=KE))
            transposed(keep["wdt"][0:R, s, :], [wdt[:, c, :] for c in range(KE)], P, R)
            for k in range(KD):
                product(keep["wcz"][:, s, k, :], [(wz[:, c, k * P:(k + 1) * P], wcT[:, c, :]) for c in range(KE)], (P, E), scale=g2[:, k:k + 1])
            for f in range(KE):
                product(wczT[:, f, :], [(wcT[:, c, f * P:(f + 1) * P], wz[:, c, :]) for c in range(KE)], (P, D))
            bc = col("bc" + q, W["L2_cond_bc" + q], KE)
            for f in range(KE):
                product(keep["bcz"][:, s, f:f + 1], [(wcT[:, c, f * P:(f + 1) * P], bz[:, c:c + 1]) for c in range(KE)], (P, 1), plus=bc[:, f:f + 1])
            for k in range(KD):
                product(keep["wd"][:, s, k, :], [(wczT[:, f, k * P:(k + 1) * P], wdT[:, f, :]) for f in range(KE)], (P, R + 2 * N), scale=g2[:, k:k + 1])
            product(keep["bd"][:, s:s + 1], [(wdT[:, f, :], keep["bcz"][:, s, f:f + 1]) for f in range(KE)], (R + 2 * N, 1))
            load(keep["bdt"][:, s, :], W["L2_cond_bdt" + q].rearrange("(k p) -> p k", p=P))
            load(keep["dp"][:, s, :], W["L2_cond_Dp" + q].rearrange("(k p) -> p k", p=P))
            al = sb("al" + q, [P, KE, N])
            load(al[:], W["L2_cond_Alog" + q].rearrange("(k p) n -> p k n", p=P))
            for n4 in range(N4):
                for j in range(4):
                    dst = keep["acol"][n4 * E32:(n4 + 1) * E32, s].rearrange("p (c j) q -> p j c q", j=4)[:, j]
                    src = al[j * E32:(j + 1) * E32].rearrange("p c (q n) -> p n c q", n=N4)[:, n4]
                    step("DVE", lambda e, dst=dst, src=src: e.tensor_copy(dst, src))
        av = keep["acol"][:].rearrange("p s g q -> p (s g q)")
        step("ACT", lambda e: e.activation(av, av, ACT.Exp))
        step("DVE", lambda e: e.tensor_scalar(av, av, -1.0, None, ALU.mult))

        length = {name: sum(1 for t in todo if t[0] == name) for name in STREAMS}
        seen, order = {name: 0 for name in STREAMS}, []
        for n, (name, eng, emit) in enumerate(todo):
            seen[name] += 1
            order.append((0 if name == "start" else seen[name] / length[name], n))
        ms, ls = {name: sem("set_" + name) for name in STREAMS}, sem("set_load")
        block = ctx.enter_context(nc.Block())
        engines = {"PE": block.tensor, "DVE": block.vector, "ACT": block.scalar, "Pool": block.gpsimd, "SP": block.sync}

        for engine, on in engines.items():
            @on
            def _(e, engine=engine):
                if engine == "SP":
                    with nc.allow_non_contiguous_dma(reason="columns of bias vectors, once"):
                        for dst, src in loads:
                            e.dma_start(dst, src).then_inc(ls, 16)
                e.wait_ge(ls, 16 * len(loads))
                if engine == "ACT":
                    e.preload_act_table_set(ACT_SET)
                begun, done, last = set(), {name: 0 for name in STREAMS}, {name: None for name in STREAMS}
                for _, n in sorted(order):
                    name, eng, emit = todo[n]
                    if eng == engine:
                        if name not in ("start", *begun):
                            e.wait_ge(ms["start"], done["start"])
                            begun.add(name)
                        if done[name] and not (last[name] == eng == "PE"):
                            e.wait_ge(ms[name], done[name])
                        emit(e).then_inc(ms[name], 16 if eng == "SP" else 1)
                    done[name] += 16 if eng == "SP" else 1
                    last[name] = eng
                for name in STREAMS:
                    e.wait_ge(ms[name], done[name])


def layer_norm(ch, x, out, st, src_after, free_after, tag, eps):
    add = ch.add
    s = [add("DVE", lambda e, t=t: e.bn_stats(st["raw"][:, t, :], x(t)), src_after + free_after, size=D) for t in range(TT)]
    a = [add("DVE", lambda e, t=t: e.bn_aggr(st["mv"][:, t, :], st["raw"][:, t, :]), [s[t]], size=2) for t in range(TT)]
    for step in a:
        step.plain = True
    ln = add("ACT", lambda e: e.activation(st["rs"][:], st["mv"][:, :, 1], ACT.Ln, bias=eps), a, size=2)
    r = add("ACT", lambda e: e.activation(st["rs"][:], st["rs"][:], ACT.Exp, scale=-0.5), [ln], size=2)
    return [add("DVE", lambda e, t=t: e.tensor_scalar(out[:, t, :], x(t), st["mv"][:, t, 0:1], st["rs"][:, t:t + 1],
                                                      ALU.subtract, ALU.mult), [r, a[t]], size=D) for t in range(TT)]


def turned(ch, ident, src, bank, dst, after, bank_free, dst_free, eng="ACT"):
    t = None
    for c in range(2):
        for r in range(2):
            t = ch.add("PE", lambda e, c=c, r=r: e.transpose(bank[:, c * 256 + r * P:c * 256 + (r + 1) * P], src[:, r, c * P:(c + 1) * P], ident[:]),
                       after + bank_free, size=64)
    flat = dst[:].rearrange("p a b -> p (a b)")
    return t, copy(ch, eng, flat, bank[:, 0:512], [t] + dst_free)


def copy(ch, eng, dst, src, after):
    if eng == "ACT":
        return ch.add("ACT", lambda e: e.activation(dst, src, ACT.Copy), after)
    return ch.add(eng, lambda e: e.tensor_copy(dst, src), after)


def products(ch, groups, after, size=256):
    last = None
    for out, terms in groups:
        for n, (l, r) in enumerate(terms):
            last = ch.add("PE", lambda e, o=out, l=l, r=r, n=n, m=len(terms): e.matmul(o, l, r, start=n == 0, stop=n == m - 1), after,
                          size=size / 4 if l.dtype == BF16 else size)
    return last


def token_projection(bank, xT, w, bias, ones):
    return [(bank[:, t * D:(t + 1) * D], [(xT[:, k, t * P:(t + 1) * P], w[:, k, :]) for k in range(KD)] + [(ones[0:PARTS, 0:P], bias)]) for t in range(TT)]


def film_tail(ch, k, B, L, at, ysrc, y_after, gone, x, x_out, x_after):
    add = ch.add
    n2 = layer_norm(ch, ysrc, B["yh"], B["st"], y_after, gone, L, k["eps"][:])
    t = None
    bank = B["bank"][2]
    for c in range(2):
        for r in range(2):
            t = add("PE", lambda e, c=c, r=r: e.transpose(bank[:, c * 256 + r * P:c * 256 + (r + 1) * P], B["yh"][:, r, c * P:(c + 1) * P], k["ident"][:]),
                    n2 + gone, size=64)
    pc = B["pc"]
    hs = [add("DVE", lambda e, c=c: e.tensor_scalar(B["h"][:, c, :], bank[:, c * 256:(c + 1) * 256], pc[:, at + c:at + c + 1],
                                                    pc[:, at + 2 + c:at + 3 + c], ALU.mult, ALU.add), [t] + gone) for c in range(2)]
    es = [add("ACT", lambda e: e.activation(B["s"][:], B["h"][:], ACT.Exp, scale=-1.0), hs + gone)]
    l = add("ACT", lambda e: e.activation(B["s"][:], B["s"][:], ACT.Ln, bias=1.0), es)
    g = add("ACT", lambda e: e.activation(B["s"][:], B["s"][:], ACT.Exp, scale=-1.0), [l])
    m = add("Pool", lambda e: e.tensor_tensor(B["h"][:], B["h"][:], B["s"][:], ALU.mult), [g] + hs)
    o = products(ch, token_projection(B["bank"][3], B["h"], k[L + "wo"], k["bias"][0:PARTS, k["at"][L + "o"]], k["ones"]), [m] + gone)
    return add("DVE", lambda e: e.tensor_tensor(x_out[:].rearrange("p a b -> p (a b)"), B["bank"][3][:, 0:512],
                                                x[:].rearrange("p a b -> p (a b)"), ALU.add), [o] + x_after)


def linear_attention(ch, k, B, L, dh, mask_at, film_at, x, x_after, gate, x_out, x_free):
    add, bank, pc = ch.add, B["bank"], B["pc"]
    H = D // dh
    n1 = layer_norm(ch, lambda t: x[:, t, :], B["xh"], B["st"], x_after, gate, L, k["eps"][:])
    _, xT = turned(ch, k["ident"], B["xh"], bank[0], B["xT"], n1, gate, gate)
    q = products(ch, token_projection(bank[1], B["xT"], k[L + "wq"], k["bias"][0:PARTS, k["at"][L + "q"]], k["ones"]), [xT])
    kk = products(ch, [(bank[2][:, c * 256:(c + 1) * 256], [(k[L + "wk"][:, i, c * P:(c + 1) * P], B["xT"][:, i, :]) for i in range(KD)]
                        + [(k["bias"][:, k["at"][L + "k"]][:, c * P:(c + 1) * P], B["om" + L][:])]) for c in range(KD)], [xT] + gate)
    v = products(ch, token_projection(bank[3], B["xT"], k[L + "wv"], k["bias"][0:PARTS, k["at"][L + "v"]], k["ones"]), [xT] + gate)
    q3 = bank[1][:, 0:512].rearrange("p (h d) -> p h d", d=dh)
    qs = B["q"][:].rearrange("p t n -> p (t n)").rearrange("p (h d) -> p h d", d=dh)
    qm, qr = B["qm"][:, 0:TT * H], B["qr"][:, 0:TT * H]
    a = add("DVE", lambda e: e.tensor_reduce(qm, q3, AX, ALU.max), [q] + gate)
    b = add("DVE", lambda e: e.tensor_tensor(qs, q3, rep(qm, 2, dh), ALU.subtract), [a])
    km = add("DVE", lambda e: e.tensor_reduce(B["km"][:], bank[2][:, 0:512].rearrange("p (c t) -> p c t", c=KD), AX, ALU.max, negate=True), [kk])
    qe = add("ACT", lambda e: e.activation(B["q"][:], B["q"][:], ACT.Exp), [b])
    ke = [add("ACT", lambda e, c=c: e.activation(B["ke"][:, c, :], bank[2][:, c * 256:(c + 1) * 256], ACT.Exp, bias=B["km"][:, c:c + 1],
                                                 accum_out=B["ks"][:, c:c + 1]), [km] + gate) for c in range(KD)]
    vm = [add("ACT", lambda e, t=t: e.activation(B["v"][:, t, :], bank[3][:, t * D:(t + 1) * D], ACT.Copy, scale=pc[:, mask_at + t:mask_at + t + 1]), [v] + gate, size=340)
          for t in range(TT)]
    kr = add("DVE", lambda e: e.reciprocal(B["kr"][:], B["ks"][:]), ke)
    qsum = add("DVE", lambda e: e.tensor_reduce(qr, qs, AX, ALU.add), [qe])
    qrec = add("DVE", lambda e: e.reciprocal(qm, qr), [qsum])
    qn = add("Pool", lambda e: e.tensor_tensor(qs, qs, rep(qm, 2, dh), ALU.mult), [qrec])
    kn = ke
    if L == "L0":
        kn = [add("DVE", lambda e, c=c: e.tensor_scalar(B["ke"][:, c, :], B["ke"][:, c, :], B["kr"][:, c:c + 1], None, ALU.mult), ke + [kr], size=D)
              for c in range(KD)]
    lhs, rhs = (B["v"], B["xh"]) if L == "L0" else (B["xh"], B["v"])
    _, kt = turned(ch, k["ident"], B["ke"], bank[0], B["xh"], kn, [xT] + vm, [xT])
    at = products(ch, [(bank[2][:, c * P:(c + 1) * P], [(lhs[:, t, c * P:(c + 1) * P], rhs[:, t, c * P:(c + 1) * P]) for t in range(TT)])
                       for c in range(KD)], vm + [kt] + ke, size=P)
    bd = [add("DVE", lambda e, c=c: e.scalar_tensor_tensor(B["bd"][:, c, :], bank[2][:, c * P:(c + 1) * P],
                                                           1.0 if L == "L0" else B["kr"][:, c:c + 1],
                                                           k["same%d" % dh][:], ALU.mult, ALU.mult), [at, kr]) for c in range(KD)]
    _, qT = turned(ch, k["ident"], B["q"], bank[1], B["xT"], [qn], [b], [v])
    y = products(ch, [(bank[0][:, t * D + c * P:t * D + (c + 1) * P], [(B["xT"][:, c, t * P:(t + 1) * P], B["bd"][:, c, :])])
                      for t in range(TT) for c in range(KD)], [qT, kt] + bd, size=P)
    BB = dict(B, yh=B["q"], h=B["ke"], s=B["xh"])
    return film_tail(ch, k, BB, L, film_at, lambda t: bank[0][:, t * D:(t + 1) * D], [y], [qT] + bd + vm, x, x_out, x_free)


def softmax_attention(ch, k, B, x, x_after, got_inputs):
    add, bank, pc, L = ch.add, B["bank"], B["pc"], "L1"
    n1 = layer_norm(ch, lambda t: x[:, t, :], B["xh"], B["st"], x_after, [], L, k["eps"][:])
    _, xT = turned(ch, k["ident"], B["xh"], bank[0], B["xT"], n1, x_after, x_after)
    got = {}
    for m, bb in (("q", (1, 2)), ("k", (0, 3))):
        for half in range(2):
            bk = bank[bb[half]]
            p = products(ch, [(bk[:, c * 256:(c + 1) * 256], [(k[L + "w" + m][:, i, (2 * half + c) * P:(2 * half + c + 1) * P], B["xT"][:, i, :]) for i in range(KD)]
                               + [(k["bias"][0:PARTS, k["at"]["L1q"]][:, (2 * half + c) * P:(2 * half + c + 1) * P], k["ones"][0:PARTS, 0:T]) if m == "q" else
                                  (k["bias"][:, k["at"]["L1k"]][:, (2 * half + c) * P:(2 * half + c + 1) * P], B["omL1"][:])]) for c in range(2)], [xT] + x_after + got_inputs)
            got[m, half] = copy(ch, "ACT" if m == "q" else "DVE", B[m + "P"][:, 2 * half:2 * half + 2, :].rearrange("p a b -> p (a b)"), bk[:, 0:512], [p])
    v = products(ch, token_projection(bank[1], B["xT"], k[L + "wv"], k["bias"][0:PARTS, k["at"][L + "v"]], k["ones"]), [got["q", 0]])
    vm = [add("ACT", lambda e, t=t: e.activation(B["v"][:, t, :], bank[1][:, t * D:(t + 1) * D], ACT.Copy, scale=pc[:, 2 + t:3 + t]), [v] + got_inputs, size=340)
          for t in range(TT)]
    proj = list(got.values()) + vm
    Eb, ETb = (B["q"], B["ke"]), (B["xh"], B["et"])
    sc, tb, yb = (bank[0], bank[1]), bank[2], bank[3]
    y_last, hist = None, {}

    def one_head(h):
        i, c = h % 4, h // 4
        free = [hist[h - QH, "scores"]] if h >= QH else []
        hist[h, "one"] = add("Pool", lambda e: e.tensor_scalar(B["qh"][:, h % QH, :], B["qP"][:, c, :], k["same32"][:, PADH * i:PADH * i + 1], None, ALU.mult),
                             [got["q", c // 2]] + free, size=128)
        hist[h, "one"].plain = True

    def scores(h):
        c = h // 4
        o = (proj if h < 2 else hist[h - 2, "exp"]) + [hist[h, "one"]]
        for t in range(TT):
            s = add("PE", lambda e, t=t: e.matmul(sc[h % 2][:, t * 256:(t + 1) * 256], B["qh"][:, h % QH, t * P:(t + 1) * P],
                                                  B["kP"][:, c, :], start=True, stop=True), o, size=T)
        hist[h, "scores"] = s
        free = hist[h - 2, "exp"] if h >= 2 else []
        m = add("DVE", lambda e: e.tensor_reduce(B["sm"][:, h % 2, :], sc[h % 2][:, 0:512].rearrange("p (t m) -> p t m", t=TT), AX, ALU.max, negate=True),
                [s] + free)
        free = [hist[h - 2, "turn"]] if h >= 2 else []
        hist[h, "exp"] = [add("ACT", lambda e, t=t: e.activation(Eb[h % 2][:, t, :], sc[h % 2][:, t * 256:(t + 1) * 256], ACT.Exp,
                                                                 bias=B["sm"][:, h % 2, t:t + 1], accum_out=B["ssum"][:, t, h:h + 1]), [m] + free + x_after)
                          for t in range(TT)]

    def turn_scores(h):
        free = [hist[h - 1, "et"]] if h else [got["q", 1]]
        t = None
        for mt in range(2):
            for nt in range(2):
                t = add("PE", lambda e, mt=mt, nt=nt: e.transpose(tb[:, mt * 256 + nt * P:mt * 256 + (nt + 1) * P], Eb[h % 2][:, nt, mt * P:(mt + 1) * P],
                                                                  k["ident"][:]), hist[h, "exp"] + free, size=64)
        hist[h, "turn"] = t
        free = [hist[h - 2, "y"]] if h >= 2 else [xT] + x_after
        hist[h, "et"] = copy(ch, "ACT", ETb[h % 2][:].rearrange("p a b -> p (a b)"), tb[:, 0:512], [t] + free)

    def values(h):
        hist[h, "y"] = products(ch, [(yb[:, t * D + h * DH1:t * D + (h + 1) * DH1],
                                      [(ETb[h % 2][:, mt, t * P:(t + 1) * P], B["v"][:, mt, h * DH1:(h + 1) * DH1]) for mt in range(2)])
                                     for t in range(TT)], [hist[h, "et"]] + proj, size=60)

    for h in range(QH - 1):
        one_head(h)
    for h in range(H1 + 2):
        if h + QH - 1 < H1:
            one_head(h + QH - 1)
        if h < H1:
            scores(h)
        if 1 <= h <= H1:
            turn_scores(h - 1)
        if h >= 2:
            values(h - 2)
    rec = add("DVE", lambda e: e.reciprocal(B["srec"][:], B["ssum"][:].rearrange("p t h -> p (t h)")), hist[H1 - 1, "exp"] + hist[H1 - 2, "exp"])
    yn = add("DVE", lambda e: e.tensor_tensor(B["qP"][:, 0:2, :].rearrange("p a b -> p (a b)").rearrange("p (g d) -> p g d", d=DH1),
                                              yb[:, 0:512].rearrange("p (g d) -> p g d", d=DH1), rep(B["srec"][:], 2, DH1), ALU.mult),
             [rec, hist[H1 - 1, "y"]])
    BB = dict(B, yh=B["ke"], h=B["xT"], s=B["xh"])
    return film_tail(ch, k, BB, L, 8, lambda t: B["qP"][:, t, :], [yn], [hist[H1 - 1, "y"], hist[H1 - 1, "et"]], x, x, [])


def chain_buffers(sb, name, shared=None):
    B = shared or {n: sb(f"{name}_{n}", [P, 2, 256]) for n in ("x", "xh", "xT", "q", "ke", "v")}
    if not shared:
        B["bd"] = sb(f"{name}_bd", [P, 2, P])
    B["st"] = {"raw": sb(f"{name}_raw", [P, 2, 6]), "mv": sb(f"{name}_mv", [P, 2, 2]), "rs": sb(f"{name}_rs", [P, 2])}
    B["qm"], B["qr"] = sb(f"{name}_qm", [P, 32]), sb(f"{name}_qr", [P, 32])
    for n in ("km", "ks", "kr"):
        B[n] = sb(f"{name}_{n}", [P, 2])
    B["pc"] = sb(f"{name}_pc", [P, PCOLS])
    return B


def bass_kernel(nc, W, out):
    with ExitStack() as ctx:
        def sb(name, shape, dt=F32):
            return ctx.enter_context(nc.sbuf_tensor(name, shape, dt))

        def sem(name):
            return ctx.enter_context(nc.semaphore(name))

        k = {}
        for L in ("L0", "L1", "L3"):
            for m in "qkvo":
                wide = H1 * PADH if L == "L1" and m in "qk" else D
                k[L + "w" + m] = sb(L + "w" + m, [P, KD, wide])
        k["wx"], k["wcz"], k["wd"] = sb("wx", [P, KD, E]), sb("wcz", [P, 2, KD, E]), sb("wd", [P, 2, KD, R + 2 * N])
        k["wdt"], k["wf"] = sb("wdt", [R, 2, E]), sb("wf", [P, KE, D])
        k["bx"], k["bcz"], k["bd"] = sb("bx", [P, KE]), sb("bcz", [P, 2, KE]), sb("bd", [R + 2 * N, 2])
        k["bdt"], k["dp"], k["acol"] = sb("bdt", [P, 2, KE]), sb("dp", [P, 2, KE]), sb("acol", [P, 2, E // E32, NQ])
        k["ident"], k["sum4"], k["same16"], k["same32"] = sb("ident", [P, P]), sb("sum4", [P, E32]), sb("same16", [P, P]), sb("same32", [P, P])
        k["ones"], k["eps"] = sb("ones", [PARTS, T], BF16), sb("eps", [P, 1])
        k["at"], nbias = bias_sections()
        k["bias"] = sb("bias", [2 * PARTS, nbias], BF16)

        def dram(name, shape, dt=F32):
            return nc.dram_tensor("scr_" + name, shape, dt, kind="Internal").ap()

        scr = {"pcol": dram("pcol", [NB, P, PCOLS]),
               "mask": dram("mask", [NB, 3, PARTS, T], BF16), "bias": dram("bias", [nbias]), "bparts": dram("bparts", [PARTS, nbias], BF16),
               "mod": dram("mod", [NB, 4, D]),
               "res": dram("res", [NB, P, 2, 256]),
               "dd": dram("dd", [NB, 2, KE, P, 2 * T]),
               "bc": dram("bc", [NB, 2, 2 * N, T]),
               "wa": dram("wa", [NB, P, KE, 2, T]),
               "g": dram("g", [NB, P, KE, T])}
        setup_weights(nc, W, k, scr, sem)

        A, C = chain_buffers(sb, "A"), {}
        A["qP"], A["kP"] = sb("A_qP", [P, 4, 256]), sb("A_kP", [P, 4, 256])
        A["xin"], A["pc0"] = sb("A_xin", [P, 2, 256]), sb("A_pc0", [P, 8])
        A["qh"] = sb("A_qh", [P, QH, 256])
        A["et"] = sb("A_et", [P, 2, 256])
        A["sm"], A["ssum"], A["srec"] = sb("A_sm", [P, 2, 2]), sb("A_ssum", [P, 2, H1]), sb("A_srec", [P, 2 * H1])
        A["omL0"], A["omL1"] = sb("omL0", [2 * PARTS, T], BF16), sb("omL1", [2 * PARTS, T], BF16)
        for n in ("xh", "xs", "xT", "r"):
            C[n] = sb("C_" + n, [P, 2, 256])
        C["xA"] = A["x"]
        C["st"] = {"raw": sb("C_raw", [P, 2, 6]), "mv": sb("C_mv", [P, 2, 2]), "rs": sb("C_rs", [P, 2])}
        C["mod"], C["dd"], C["tmp"] = sb("C_mod", [P, 4, D]), sb("C_dd", [P, KE, 2, T]), sb("C_tmp", [P, KE, T])
        C["wa"], C["dbc"] = sb("C_wa", [P, KE, 2, T]), sb("C_dbc", [R + 2 * N, T])
        S = {"slot": sb("S_slot", [P, 2, 4, 2, T]), "bc": sb("S_bc", [P, 2, 2 * NQ, T]), "dA": sb("S_dA", [P, 2, 2, 4, T]),
             "X": sb("S_X", [P, 4, 4, T]), "wa": sb("S_wa", [P, KE, 2, T]), "g": sb("S_g", [P, KE, T])}
        v = C["dd"][:].rearrange("p c a t -> p c (a t)")
        two = lambda ap: ap.rearrange("p (a b) -> p a b", a=2)
        Tt = chain_buffers(sb, "T", {"x": sb("T_x", [P, 2, 256]), "xh": C["xh"], "xT": C["xT"], "q": two(v[:, 0]), "ke": two(v[:, 1]), "v": two(v[:, 2]),
                                     "bd": two(v[:, 3, 0:256]), "gate": sb("T_gate", [P, D]),
                                     "g": sb("T_g", [P, KE, T])})
        Tt["omL3"] = sb("omL3", [2 * PARTS, T], BF16)
        ps = ctx.enter_context(nc.psum_tensor("ps", [P, 8, 512], F32))
        A["bank"] = [ps[:, b, :] for b in (0, 1, 2, 3)]
        C["bank"] = [ps[:, b, :] for b in (4, 5, 6)]
        Tt["bank"] = [ps[:, b, :] for b in (4, 5, 6, 4)]
        S["bank"] = ps[:, 7, :]
        chains = {"A": Chain("A"), "C": Chain("C"), "S": Chain("S"), "P": Chain("P"), "T": Chain("T"), "PA": Chain("PA"), "PT": Chain("PT")}
        chain_a(chains["A"], k, A, scr)
        chain_pa(chains["PA"], A, W["x"], scr)
        chain_pt(chains["PT"], Tt, scr)
        chain_c(chains["C"], k, C, scr)
        chain_s(chains["S"], k, S, scr)
        chain_p(chains["P"], S, scr)
        chain_t(chains["T"], k, Tt, scr, out)
        run(nc, chains, S, A, Tt, sem)


def load(ch, dst, src, after, group, name=None):
    f = lambda v, b: v(b) if callable(v) else v
    return ch.add("SP", lambda e, b: e.dma_start(f(dst, b), f(src, b)), after, name=name, group=group)


def at_batch(ap, b):
    return ap[b] if isinstance(b, int) else ap[bass.ds(b, 1)].squeeze(0)


def chain_a(ch, k, B, scr):
    load(ch, B["pc"][:, 0:12], lambda b: at_batch(scr["pcol"], b)[:, 0:12], [], "Ain")
    got = load(ch, B["omL1"][PARTS:2 * PARTS, :], lambda b: at_batch(scr["mask"], b)[1], [], "Ain")
    x1 = linear_attention(ch, k, dict(B, pc=B["pc0"]), "L0", D // 16, 0, 4, B["xin"], [Ago("PA", "in")], [], B["x"], [Ago("C", "x read", 0), Ago("C", "x normed", 0)])
    ch.names["L0 done"] = x1
    x2 = softmax_attention(ch, k, B, B["x"], [x1], [got])
    ch.names["x2"] = x2


def chain_pa(ch, B, x_in, scr):
    free = [Ago("A", "L0 done", 0)]
    load(ch, B["xin"][:], lambda b: at_batch(x_in, b).rearrange("(t p) d -> p t d", p=P), free, "in")
    load(ch, B["pc0"][:, 0:8], lambda b: at_batch(scr["pcol"], b)[:, 0:8], free, "in")
    load(ch, B["omL0"][PARTS:2 * PARTS, :], lambda b: at_batch(scr["mask"], b)[0], free, "in", name="in")


def chain_c(ch, k, B, scr):
    add, bank, st = ch.add, B["bank"], B["st"]
    banks = [Ago("T", "last")]
    got = load(ch, B["mod"][:], lambda b: at_batch(scr["mod"], b).partition_broadcast(P), [], "Cin")
    x, xs, mod = B["xA"], B["xs"], B["mod"]
    n1 = layer_norm(ch, lambda t: x[:, t, :], B["xh"], st, [Ago("A", "x2")], [], "C1", k["eps"][:])
    ch.names["x normed"] = n1[-1]
    mo = lambda n: rep(mod[:, n, :], 1, TT)
    m1 = add("Pool", lambda e: e.tensor_tensor(xs[:], B["xh"][:], mo(0), ALU.mult), n1 + [got])
    m2 = add("Pool", lambda e: e.tensor_tensor(xs[:], xs[:], mo(1), ALU.add), [m1])
    r1 = add("Pool", lambda e: e.tensor_tensor(B["r"][:], xs[:], mo(2), ALU.mult), [m2])
    r2 = add("Pool", lambda e: e.tensor_tensor(B["r"][:], B["r"][:], x[:], ALU.add), [r1, Ago("A", "x2")], name="x read", size=512)
    r3 = add("Pool", lambda e: e.tensor_tensor(B["r"][:], B["r"][:], mo(3), ALU.add), [r2], size=512)
    n2 = layer_norm(ch, lambda t: xs[:, t, :], B["xh"], st, [m2], n1, "C2", k["eps"][:])
    _, xT = turned(ch, k["ident"], B["xh"], bank[0], B["xT"], n2, banks, [])
    d_free, u_free, s_out = [xT], [], None
    for s in range(2):
        dbc_bank = bank[s][0:R + 2 * N, 0:T]
        p = products(ch, [(dbc_bank, [(k["wd"][:, s, i, :], B["xT"][:, i, :]) for i in range(KD)])], d_free + banks)
        dbc = add("ACT", lambda e, s=s, o=dbc_bank: e.activation(B["dbc"][:], o, ACT.Identity, bias=k["bd"][:, s:s + 1]), [p] + u_free)
        bcs = load(ch, lambda b, s=s: at_batch(scr["bc"], b)[s], B["dbc"][R:R + 2 * N, :], [dbc], "bc%d" % s, name="bc%d" % s)
        pres, us = [], []
        for h in range(2):
            pre, zb = bank[2], bank[1 - s]
            p = products(ch, [(pre[:, c * T:(c + 1) * T], [(k["wdt"][0:R, s, (2 * h + c) * P:(2 * h + c + 1) * P], B["dbc"][0:R, :])]) for c in range(2)],
                         [dbc] + pres + banks)
            for c in range(2):
                f, o = 2 * h + c, pre[:, c * T:(c + 1) * T]
                pres.append(add("ACT", lambda e, f=f, o=o, s=s: e.activation(B["dd"][:, f, 0, :], o, ACT.Identity, bias=k["bdt"][:, s, f:f + 1]),
                                [p] + u_free, size=340))
            p = products(ch, [(zb[:, c * T:(c + 1) * T], [(k["wcz"][:, s, i, (2 * h + c) * P:(2 * h + c + 1) * P], B["xT"][:, i, :]) for i in range(KD)])
                              for c in range(2)], [dbc, xT] + us + u_free + banks)
            for c in range(2):
                f, o = 2 * h + c, zb[:, c * T:(c + 1) * T]
                us.append(add("ACT", lambda e, f=f, o=o, s=s: e.activation(B["dd"][:, f, 1, :], o, ACT.Identity, bias=k["bcz"][:, s, f:f + 1]), [p] + u_free, size=340))
        ab = add("ACT", lambda e: e.activation(B["tmp"][:], B["dd"][:, :, 0, :], ACT.Abs), pres + u_free)
        e1 = add("ACT", lambda e: e.activation(B["tmp"][:], B["tmp"][:], ACT.Exp, scale=-1.0), [ab])
        e2 = add("ACT", lambda e: e.activation(B["tmp"][:], B["tmp"][:], ACT.Ln, bias=1.0), [e1])
        w = []
        for c in range(KE):
            if s == 0:
                w.append(add("DVE", lambda e, c=c: e.tensor_scalar(B["wa"][:, c, 0, :], B["dd"][:, c, 1, :], k["dp"][:, 0, c:c + 1], None, ALU.mult), us, size=T))
            else:
                w.append(add("DVE", lambda e, c=c: e.scalar_tensor_tensor(B["wa"][:, c, 0, :], B["dd"][:, c, 1, :], k["dp"][:, 1, c:c + 1],
                                                                          B["wa"][:, c, 0, :], ALU.mult, ALU.add), us + w0, size=T))
        w0 = w
        dl = add("DVE", lambda e: e.scalar_tensor_tensor(B["dd"][:, :, 0, :], B["dd"][:, :, 0, :], 0.0, B["tmp"][:], ALU.max, ALU.add), [e2])
        du = add("Pool", lambda e: e.tensor_tensor(B["dd"][:, :, 1, :], B["dd"][:, :, 1, :], B["dd"][:, :, 0, :], ALU.mult), [dl] + us + w)
        s_out = load(ch, lambda b, s=s: at_batch(scr["dd"], b)[s].rearrange("c p f -> p c f"), B["dd"][:].rearrange("p c a t -> p c (a t)"), [du], "dd%d" % s,
                     name="dd%d" % s)
        d_free, u_free = us, [s_out, du, bcs]
    hs = []
    for h in range(2):
        bk = bank[h]
        p = products(ch, [(bk[:, c * T:(c + 1) * T], [(k["wx"][:, i, (2 * h + c) * P:(2 * h + c + 1) * P], B["xT"][:, i, :]) for i in range(KD)]) for c in range(2)],
                     us + [dbc])
        for c in range(2):
            f, o = 2 * h + c, bk[:, c * T:(c + 1) * T]
            hs.append(add("DVE", lambda e, f=f, o=o: e.tensor_scalar(B["wa"][:, f, 1, :], o, k["bx"][:, f:f + 1], None, ALU.add), [p], size=T))
    e0 = add("ACT", lambda e: e.activation(B["tmp"][:], B["wa"][:, :, 1, :], ACT.Exp, scale=-1.0), hs + [dl])
    e1 = add("ACT", lambda e: e.activation(B["tmp"][:], B["tmp"][:], ACT.Ln, bias=1.0), [e0])
    e2 = add("ACT", lambda e: e.activation(B["tmp"][:], B["tmp"][:], ACT.Exp, scale=-1.0), [e1])
    m = add("Pool", lambda e: e.tensor_tensor(B["wa"][:, :, 1, :], B["wa"][:, :, 1, :], B["tmp"][:], ALU.mult), [e2] + hs, name="last")
    load(ch, lambda b: at_batch(scr["wa"], b), B["wa"][:], [m] + w0, "Cwa", name="wa")
    load(ch, lambda b: at_batch(scr["res"], b), B["r"][:], [r3], "Cres", name="res")


def load_slot(ch, B, scr, m, after):
    c, s = m // 2, m % 2
    src = lambda b: at_batch(scr["dd"], b)[s, c].rearrange("(j e) f -> e j f", e=E32)
    for n4 in range(N4):
        load(ch, B["slot"][n4 * E32:(n4 + 1) * E32, s].rearrange("p j a t -> p j (a t)"), src, after, "slots%d" % s,
             name="slot%d" % m if n4 == N4 - 1 else None)


def chain_p(ch, B, scr):
    for s in range(2):
        u = 27 + 4 * s
        last = [Ago("S", "exp%d" % u, 0), Ago("S", "bmul%d" % u, 0)]
        load_slot(ch, B, scr, s, last + [Ago("C", "dd%d" % s, 0)])
        for n4 in range(N4):
            src = lambda b, n4=n4, s=s: at_batch(scr["bc"], b)[s].rearrange("(q n) t -> n q t", n=N4)[n4].partition_broadcast(E32)
            load(ch, B["bc"][n4 * E32:(n4 + 1) * E32, s], src, last + [Ago("S", "cmul%d" % u, 0), Ago("C", "bc%d" % s, 0)],
                 "bc%d" % s, name="bc%d" % s if n4 == N4 - 1 else None)
    load(ch, B["wa"][:], lambda b: at_batch(scr["wa"], b), [Ago("S", "gate3", 0), Ago("C", "wa", 0)], "wa", name="wa")


def chain_s(ch, k, B, scr):
    add, n = ch.add, ch.names
    X, dA, bc = B["X"], B["dA"], B["bc"]
    UNITS, SLOTS = 4 * 2 * NQ, 8

    def unit(name, u):
        return n[name + str(u)] if u >= 0 else Ago("S", name + str(u + UNITS))

    def slot(m):
        return n["slot%d" % m] if m >= 2 else Ago("P", "slot%d" % m)

    def emit_exp(u):
        m, c, s, q = u // 4, u // 8, (u // 4) % 2, u % 4
        lo = 1 - s
        for j in range(4):
            add("ACT", lambda e, j=j: e.activation(dA[:, s, q % 2, j, lo:lo + T - 1], B["slot"][:, m % 2, j, 0, lo:lo + T - 1], ACT.Exp,
                                                   scale=k["acol"][:, s, 4 * c + j, q:q + 1]),
                [slot(m), unit("scan", u - 2 if q >= 2 else u - 6)], name="exp%d" % u if j == 3 else None, size=340)

    def emit_bmul(u):
        m, s, q = u // 4, (u // 4) % 2, u % 4
        add("DVE", lambda e: e.tensor_tensor(X[:, u % 4], B["slot"][:, m % 2, :, 1, :], rep(bc[:, s, q, :], 1, 4), ALU.mult),
            [slot(m), Ago("P", "bc%d" % s), unit("sum", u - 4)], name="bmul%d" % u, size=1024)

    def emit_scan(u):
        s, q = (u // 4) % 2, u % 4
        flat = lambda ap: ap.rearrange("p j t -> p (j t)")[:, ::-1] if s else ap.rearrange("p j t -> p (j t)")
        add("DVE", lambda e: e.tensor_tensor_scan(flat(X[:, u % 4]), flat(dA[:, s, q % 2]), flat(X[:, u % 4]), 0.0, ALU.mult, ALU.add),
            [n["exp%d" % u], n["bmul%d" % u]], name="scan%d" % u, size=1024)

    def emit_cmul(u):
        s, q = (u // 4) % 2, u % 4
        add("Pool", lambda e: e.tensor_tensor(X[:, u % 4], X[:, u % 4], rep(bc[:, s, NQ + q, :], 1, 4), ALU.mult), [n["scan%d" % u]], name="cmul%d" % u, size=1024)

    def emit_sum(u):
        c, first, last = u // 8, u % 8 == 0, u % 8 == 7
        free = [n["gate%d" % (c - 1)] if c else Ago("S", "gate3")] if first else []
        for j in range(4):
            add("PE", lambda e, j=j: e.matmul(B["bank"][32 * j:32 * j + 32, (c % 2) * T:(c % 2 + 1) * T], k["sum4"][:], X[:, u % 4, j, :],
                                              start=first, stop=last, tile_position=(0, 32 * j), skip_group_check=True),
                [n["cmul%d" % u]] + free, name="sum%d" % u if j == 3 else None, size=70)
        if last:
            g = B["g"][:, c, :]
            a = add("DVE", lambda e: e.tensor_tensor(g, B["bank"][:, (c % 2) * T:(c % 2 + 1) * T], B["wa"][:, c, 0, :], ALU.add),
                    [n["sum%d" % u], Ago("P", "wa"), Ago("S", "g")], size=T)
            add("DVE", lambda e: e.tensor_tensor(g, g, B["wa"][:, c, 1, :], ALU.mult), [a], name="gate%d" % c, size=T)

    for v in range(UNITS + 2):
        if v < UNITS:
            emit_exp(v)
            emit_bmul(v)
        if 1 <= v <= UNITS:
            emit_scan(v - 1)
            if (v - 1) % 4 == 3 and (v - 1) // 4 + 2 < SLOTS:
                load_slot(ch, B, scr, (v - 1) // 4 + 2, [n["exp%d" % (v - 1)], n["bmul%d" % (v - 1)]])
            emit_cmul(v - 1)
        if 2 <= v <= UNITS + 1:
            emit_sum(v - 2)
    load(ch, lambda b: at_batch(scr["g"], b), B["g"][:], [n["gate3"]], "Sg", name="g")


def chain_pt(ch, B, scr):
    free = [Ago("T", "last"), Ago("T", "stored")]
    load(ch, B["x"][:], lambda b: at_batch(scr["res"], b), [Ago("C", "res", 2)] + free, "in")
    load(ch, B["gate"][:], lambda b: at_batch(scr["mod"], b)[2].partition_broadcast(P), free, "in")
    load(ch, B["omL3"][PARTS:2 * PARTS, :], lambda b: at_batch(scr["mask"], b)[2], free, "in")
    load(ch, B["pc"][:, 12:18], lambda b: at_batch(scr["pcol"], b)[:, 12:18], free, "in")
    load(ch, B["g"][:], lambda b: at_batch(scr["g"], b), [Ago("S", "g")] + free, "in", name="in")


def chain_t(ch, k, B, scr, out):
    got = Ago("PT", "in", 0)
    bk = B["bank"][0]
    o = products(ch, [(bk[:, t * D:(t + 1) * D], [(B["g"][:, c, t * P:(t + 1) * P], k["wf"][:, c, :]) for c in range(KE)]) for t in range(TT)],
                 [got, Ago("C", "last", 0)])
    xf = B["x"]
    a = ch.add("DVE", lambda e: e.tensor_tensor(B["xh"][:], bk[:, 0:512].rearrange("p (t d) -> p t d", t=TT), rep(B["gate"][:], 1, TT), ALU.mult), [o, got])
    b_ = ch.add("DVE", lambda e: e.tensor_tensor(xf[:], xf[:], B["xh"][:], ALU.add), [a])
    last = linear_attention(ch, k, B, "L3", 32, 12, 14, xf, [b_], [], xf, [])
    ch.names["last"] = last
    load(ch, lambda b: at_batch(out, b).rearrange("(t p) d -> p t d", p=P), xf[:], [last], "Tout", name="stored")


ENGINES = ("PE", "DVE", "ACT", "Pool", "SP")
GATED = ("A", "C", "T")


def step_waits(chains):
    lasts = {c: list({s.group or s.eng: s for s in ch.steps}.values()) for c, ch in chains.items()}
    waits = {}
    for name, ch in chains.items():
        started = set()
        for step in ch.steps:
            w = [(a, 0) if isinstance(a, Step) else (chains[a.chain].names[a.name], a.turns) for a in step.after]
            if name in GATED and step.eng not in started:
                started.add(step.eng)
                w += [(s, 1) for s in lasts[name]]
                w += {"C": [(s, 1) for s in lasts["T"]], "T": [(s, 0) for s in lasts["C"]]}.get(name, [])
            waits[step] = w
    return waits


def alternate(chains, waits, rounds=4):
    tail, behind, after = {}, {}, {}
    for ch in chains.values():
        nxt = {}
        for step in reversed(ch.steps):
            behind[step] = nxt.get(step.eng)
            nxt[step.eng] = step
    for step, w in waits.items():
        for s, turns in w:
            if turns == 0:
                after.setdefault(s, []).append(step)

    def lag(step):
        return step.time + (2.2 if step.group else 0.25)

    def way(step):
        if step not in tail:
            later = after.get(step, []) + ([behind[step]] if behind[step] else [])
            tail[step] = lag(step) + max((way(x) for x in later), default=0.0)
        return tail[step]

    for ch in chains.values():
        for step in reversed(ch.steps):
            way(step)
    free, before, order, work = {}, {}, [], {}
    for _ in range(rounds):
        done, order = {}, []
        queues = {(c, eng): [s for s in ch.steps if s.eng == eng] for c, ch in chains.items() for eng in ENGINES}
        at = {q: 0 for q in queues}
        while len(order) < sum(len(q) for q in queues.values()):
            heads = []
            for q, steps in queues.items():
                if at[q] == len(steps):
                    continue
                step = steps[at[q]]
                if any(turns == 0 and s not in done for s, turns in waits[step]):
                    continue
                start = max([free.get(step.eng, 0.0)] + [(done if turns == 0 else before).get(s, 0.0) for s, turns in waits[step]])
                heads.append((start, step, q))
            eng = min(heads, key=lambda h: h[0])[1].eng
            mine = [h for h in heads if h[1].eng == eng]
            first = min(h[0] for h in mine)
            start, step, q = max((h for h in mine if h[0] <= first + WINDOW), key=lambda h: tail[h[1]])
            at[q] += 1
            slow = 0.0
            if eng == "PE":
                tick = int(start / PE_TICK)
                slow = step.time if work.get(tick - 1, 0.0) < 0.375 * PE_TICK else 0.0
                work[tick] = work.get(tick, 0.0) + step.time
            free[eng] = start + step.time + slow
            done[step] = start + lag(step) + slow
            order.append(step)
        before = done
    return order


def run(nc, chains, S, A, Tt, sem):
    waits = step_waits(chains)
    order = alternate(chains, waits)
    place = {s: n for n, s in enumerate(order)}
    keys = {(c, key) for c, ch in chains.items() for key in ch.count}
    sems = {key: sem("s_%s_%s" % key) for key in sorted(keys)}
    ready = sem("s_ready")
    spare = {eng: sem("s_spare_" + eng) for eng in ENGINES}

    def emit(e, eng, turn):
        known = {}
        for step in order:
            name = step.chain.name
            if step.eng != eng:
                continue
            batch = turn + OFFSET[name]
            if isinstance(turn, int) and not 0 <= batch < NB:
                continue
            need = {}
            for s, turns in waits[step]:
                if turns == 0:
                    assert place[s] < place[step], ("order", name, step.eng, s.chain.name, s.eng)
                inc, total = s.inc, s.chain.count[s.group or s.eng]
                off = OFFSET[s.chain.name] - turns
                if isinstance(turn, int) and not 0 <= turn + off < NB:
                    continue
                key = (s.chain.name, s.group or s.eng)
                need[key] = max(need.get(key, -10**9), off * total * inc + (s.n + 1) * inc)
            for key, v in need.items():
                if known.get(key, -10**9) >= v:
                    continue
                known[key] = v
                ch_, grp = key
                total = chains[ch_].count[grp] * (16 if grp not in ENGINES else 1)
                e.wait_ge(sems[key], turn * total + v)
                if eng == "SP" or step.plain:
                    e.sem_inc(spare[eng], 1)
            ins = step.emit(e, batch) if eng == "SP" else step.emit(e)
            ins.then_inc(sems[name, step.group or step.eng], step.inc)

    with nc.Block() as block:
        on = {"PE": block.tensor, "DVE": block.vector, "ACT": block.scalar, "Pool": block.gpsimd, "SP": block.sync}
        for eng in ENGINES:
            @on[eng]
            def _(e, eng=eng):
                if eng == "DVE":
                    for q in range(2):
                        e.memset(S["dA"][:, 0, q, :, 0:1], 0.0).then_inc(ready, 1)
                        e.memset(S["dA"][:, 1, q, :, T - 1:T], 0.0).then_inc(ready, 1)
                    for om in (A["omL0"], A["omL1"], Tt["omL3"]):
                        e.memset(om[0:PARTS, :], 1.0).then_inc(ready, 1)
                e.wait_ge(ready, 7)
                if eng == "ACT":
                    e.preload_act_table_set(ACT_SET)
                first, last = 2, NB - 3
                for turn in range(-3, first):
                    emit(e, eng, turn)
                with e.Fori(first, last) as i:
                    if eng == "ACT":
                        e.preload_act_table_set(ACT_SET)
                    emit(e, eng, i)
                for turn in range(last, NB + 1):
                    emit(e, eng, turn)
                if eng == "SP":
                    e.wait_ge(sems["T", "Tout"], 16 * NB)



def kernel(**inputs):
    import numpy as np
    import concourse.bacc as bacc
    from concourse.bass_utils import run_bass_kernel_spmd

    nc = bacc.Bacc("TRN2", target_bir_lowering=False, num_devices=1)
    arrays, aps = {}, {}
    for name, value in inputs.items():
        if name == "cond_1024":
            continue
        a = np.ascontiguousarray(value)
        arrays["in_" + name] = a
        aps[name] = nc.dram_tensor("in_" + name, a.shape, mybir.dt.from_np(a.dtype), kind="ExternalInput").ap()
    out = nc.dram_tensor("out_x", (NB, T, D), F32, kind="ExternalOutput").ap()
    bass_kernel(nc, aps, out)
    return run_bass_kernel_spmd(nc, [arrays], core_ids=[0]).results[0]["out_x"]
```
